# Optimizing a Trainium2 kernel written in Bass

```python
import numpy as np
import jax
import jax.numpy as jnp

def _softmax(x, axis=-1):
    return jax.nn.softmax(x, axis=axis)

def _gelu(x):
    return jax.nn.gelu(x, approximate=True)

def _silu(x):
    return jax.nn.silu(x)

def _sigmoid(x):
    return jax.nn.sigmoid(x)

def _layernorm(x, axis=-1, eps=1e-05):
    m = jnp.mean(x, axis=axis, keepdims=True)
    v = jnp.var(x, axis=axis, keepdims=True)
    return (x - m) / jnp.sqrt(v + eps)

def _scatter_add(tgt, idx, src, axis=0):
    return tgt.at[idx].add(src)

def _segment_sum(src, seg, n):
    return jax.ops.segment_sum(src, seg, n)
kernel_name = 'mk_gnn_resnorm_d1_gnn_r64_faad79'

def setup_inputs(seed: int=0):
    np.random.seed(seed)
    _w = jnp.asarray

    def _rec_inputs():
        import jax
        import jax.numpy as jnp
        _gk = jax.random.key(seed)
        x = -0.0003713 + 1 * jax.random.normal(jax.random.fold_in(_gk, 1), (100000, 256), jnp.float32)
        _s = jax.random.randint(jax.random.fold_in(_gk, 2), (12500,), 0, 100000, jnp.int32)
        _d = jax.random.randint(jax.random.fold_in(_gk, 3), (12500,), 0, 100000, jnp.int32)
        _loop = jnp.arange(100000, dtype=jnp.int32)
        src = jnp.concatenate([_s, _d, _loop])
        dst = jnp.concatenate([_d, _s, _loop])
        _o = jnp.argsort(dst, stable=True)
        src = src[_o]
        dst = dst[_o]
        return (x, src, dst)
    x, src, dst = _rec_inputs()

    def _L0_gnn_setup():
        import jax, jax.numpy as jnp
        import numpy as np
        N = 50000
        E = 12500
        D_IN = 256
        HID = 256
        EPS = 1e-12

        def _glorot(key, shape):
            fan_in, fan_out = (shape[1], shape[0])
            lim = jnp.sqrt(6.0 / (fan_in + fan_out))
            return jax.random.uniform(key, shape, jnp.float32, -lim, lim)

        def _sage_conv(x, src, dst, Wl, bl, Wr, num_nodes):
            agg = jax.ops.segment_sum(x[src], dst, num_segments=num_nodes)
            cnt = jax.ops.segment_sum(jnp.ones((src.shape[0],), x.dtype), dst, num_segments=num_nodes)
            mean = agg / jnp.maximum(cnt, 1.0)[:, None]
            out = mean @ Wl.T + bl + x @ Wr.T
            norm = jnp.linalg.norm(out, axis=-1, keepdims=True)
            return out / jnp.maximum(norm, EPS)
        key = jax.random.key(seed)
        ks = jax.random.split(key, 8)
        x = jax.random.normal(ks[0], (N, D_IN), jnp.float32)
        edge_index = jax.random.randint(ks[1], (2, E), 0, N, jnp.int64)
        W1l = _glorot(ks[2], (HID, D_IN))
        b1l = jnp.zeros((HID,), jnp.float32)
        W1r = _glorot(ks[3], (HID, D_IN))
        W2l = _glorot(ks[4], (HID, HID))
        b2l = jnp.zeros((HID,), jnp.float32)
        W2r = _glorot(ks[5], (HID, HID))
        return {'x': x, 'edge_index': edge_index, 'W1l': W1l, 'b1l': b1l, 'W1r': W1r, 'W2l': W2l, 'b2l': b2l, 'W2r': W2r}
    _L0_gnn_all = _L0_gnn_setup()
    _L0_gnn_in = {k: v for k, v in _L0_gnn_all.items() if k in ('W1l', 'b1l', 'W1r', 'W2l', 'b2l', 'W2r')}
    del _L0_gnn_all
    return {'x': x, 'src': src, 'dst': dst, 'L0_gnn_W1l': _L0_gnn_in['W1l'], 'L0_gnn_b1l': _L0_gnn_in['b1l'], 'L0_gnn_W1r': _L0_gnn_in['W1r'], 'L0_gnn_W2l': _L0_gnn_in['W2l'], 'L0_gnn_b2l': _L0_gnn_in['b2l'], 'L0_gnn_W2r': _L0_gnn_in['W2r']}

def reference(x, src, dst, L0_gnn_W1l, L0_gnn_b1l, L0_gnn_W1r, L0_gnn_W2l, L0_gnn_b2l, L0_gnn_W2r):
    import jax
    import jax.numpy as jnp

    def _L0_gnn_ref(x, edge_index, W1l, b1l, W1r, W2l, b2l, W2r):
        import jax, jax.numpy as jnp
        import numpy as np
        N = 50000
        E = 12500
        D_IN = 256
        HID = 256
        EPS = 1e-12

        def _glorot(key, shape):
            fan_in, fan_out = (shape[1], shape[0])
            lim = jnp.sqrt(6.0 / (fan_in + fan_out))
            return jax.random.uniform(key, shape, jnp.float32, -lim, lim)

        def _sage_conv(x, src, dst, Wl, bl, Wr, num_nodes):
            agg = jax.ops.segment_sum(x[src], dst, num_segments=num_nodes)
            cnt = jax.ops.segment_sum(jnp.ones((src.shape[0],), x.dtype), dst, num_segments=num_nodes)
            mean = agg / jnp.maximum(cnt, 1.0)[:, None]
            out = mean @ Wl.T + bl + x @ Wr.T
            norm = jnp.linalg.norm(out, axis=-1, keepdims=True)
            return out / jnp.maximum(norm, EPS)
        src, dst = (edge_index[0], edge_index[1])
        n = x.shape[0]
        h = _sage_conv(x, src, dst, W1l, b1l, W1r, n)
        h = jax.nn.relu(h)
        h = _sage_conv(h, src, dst, W2l, b2l, W2r, n)
        return h
    edge_index = jnp.stack([src, dst])
    x = _layernorm(x + _L0_gnn_ref(x, edge_index, L0_gnn_W1l, L0_gnn_b1l, L0_gnn_W1r, L0_gnn_W2l, L0_gnn_b2l, L0_gnn_W2r), axis=-1)
    return x

_drawn_inputs = setup_inputs


def setup_inputs(seed=0):
    import zlib

    import numpy as np

    out = dict(_drawn_inputs(seed))
    spreads = {'L0_gnn_b1l': (0.0, 0.1), 'L0_gnn_b2l': (0.0, 0.1)}
    factors = {}
    for name, (base, spread) in spreads.items():
        noise = np.random.default_rng([zlib.crc32(name.encode()), seed]).standard_normal(out[name].shape)
        drawn = base * np.exp(spread * noise) if base else spread * noise
        out[name] = jnp.asarray(drawn.astype(out[name].dtype))
    for name, factor in factors.items():
        out[name] = (out[name] * factor).astype(out[name].dtype)
    return out
```

```python
import numpy as np
import concourse.bass as bass
from concourse import mybir
from contextlib import ExitStack

F32 = mybir.dt.float32
BF16 = mybir.dt.bfloat16
I32 = mybir.dt.int32
ALU = mybir.AluOpType
ACT = mybir.ActivationFunctionType
AX = mybir.AxisListType

P = 128
N = 100000
E = 125000
D = 256
H = D // P
EPR = -(-E // P)
LAST = E - EPR * (P - 1)
CB = 8
MAXB = -(-EPR // CB)
REC = 6
SRC, DST, SAME, BASE, END, ENDF = range(REC)
KEPT = 5
BIG = 1 << 22

ROWS = 512
JT = ROWS // P
SLOTS = 3
TRI = N // ROWS // SLOTS
NSUP = TRI * SLOTS
PAIRS = 2 * SLOTS
TAIL = N - NSUP * ROWS
TP = TAIL // 2
LASTU = NSUP * 2
HID0 = N
HROWS = N + P * (1 + CB * MAXB)
FEWB = 32
RP = 80
LN_EPS = 1e-5
NORM_EPS = 1e-12
BESIDE = [(), (7, 6), (5, 4), (3, 2), (1, 0), ()]


def build_gnn(nc, x, src, dst, w1l, b1, w1r, w2l, b2, w2r, out):
    ctx = ExitStack()

    def sb(name, shape, dt=F32):
        return ctx.enter_context(nc.sbuf_tensor(name, shape, dt))

    def pb(name, shape):
        return ctx.enter_context(nc.psum_tensor(name, shape, F32))

    def sem(name):
        return ctx.enter_context(nc.semaphore(name))

    def sems(name, n):
        return [sem(f"{name}{i}") for i in range(n)]

    with ctx:
        recs = nc.dram_tensor("edge_records", [P * EPR, REC], F32).ap()
        redirect = nc.dram_tensor("redirect", [N, 1], I32).ap()
        h_all = nc.dram_tensor("h_all", [HROWS, D], F32).ap()
        self_x = nc.dram_tensor("self_x", [P * (1 + CB * MAXB), D], F32).ap()
        bias_parts = nc.dram_tensor("bias_parts", [3, 2 * D], BF16).ap()

        mark = sem("mark")
        ident = sb("ident", [P, P])
        ones3 = sb("ones3", [3, P], BF16)
        ln_eps = sb("ln_eps", [P, 1])
        bias3 = sb("bias3", [3, 2, 2, D], BF16)
        W = {n: sb(n, [P, H, D]) for n in ("w1l_sb", "w1r_sb", "w1s_sb", "w2l_sb", "w2r_sb", "w2s_sb")}
        nb_i = sb("nb_i", [1, 3], I32)
        order = sb("order", [P, (MAXB + 2) * CB])
        edge0 = sb("edge0", [P, 1])
        slot0 = sb("slot0", [P, CB], I32)
        f_dst = sb("f_dst", [P, 1])
        f_base = sb("f_base", [P, 1])
        f_get = sb("f_get", [P, 1], I32)
        f_put = sb("f_put", [P, 1], I32)
        carry = sb("carry", [P, P])
        kept = sb("kept", [P, MAXB + 2, KEPT, CB])
        hrow = sb("hrow", [P, MAXB + 2, CB], I32)
        e_idx = sb("e_idx", [P, CB], I32)
        got = sb("got", [P, CB, REC])
        valid = sb("valid", [P, CB])
        cur = sb("cur", [P, KEPT, CB])
        src_i = sb("src_i", [P, CB], I32)
        dst_i = sb("dst_i", [P, CB], I32)
        put_i = sb("put_i", [P, CB], I32)
        slot_i = sb("slot_i", [P, CB], I32)
        e_f = sb("e_f", [P, CB])
        end_f = sb("end_f", [P, CB])

        with ExitStack() as first:
            prepare_edges(nc, first, locals())
        with ExitStack() as second:
            columns = column_buffers(nc, second, locals())
            col_sems = column_sems(sem, sems)
            with ExitStack() as sweep:
                dense_and_first(nc, sweep, locals(), columns)
            clear_semaphores(nc, col_sems)
            second_layer(nc, second, locals(), columns)
    return nc


def prepare_edges(nc, first, v):
    src, dst, x = v["src"], v["dst"], v["x"]
    recs, redirect, bias_parts = v["recs"], v["redirect"], v["bias_parts"]
    ident, ones3, bias3, W = v["ident"], v["ones3"], v["bias3"], v["W"]

    def sb(name, shape, dt=F32):
        return first.enter_context(nc.sbuf_tensor(name, shape, dt))

    sem = v["sem"]
    di = sb("dst_ints", [P, EPR + 3], I32)
    si = sb("src_ints", [P, EPR + 1], I32)
    df = sb("dst_f", [P, EPR + 3])
    sf = sb("src_f", [P, EPR + 1])
    last = sb("last", [P, EPR + 1])
    lself = sb("lself", [P, EPR + 1])
    tmp = sb("tmp", [P, EPR + 1])
    listed = sb("listed", [P, EPR])
    over = sb("over", [P, EPR])
    record = sb("record", [P, EPR, REC])
    key = sb("key", [P, EPR])
    pos1 = sb("pos1", [P, EPR])
    best = sb("best", [P, CB])
    cnt = sb("cnt", [P, 1])
    cmax = sb("cmax", [P, 1])
    nbi = sb("nbi", [1, 1], I32)
    f_has = sb("f_has", [P, 1])
    f_tmp = sb("f_tmp", [P, 1])
    l_has = sb("l_has", [P, 1])
    l_dst = sb("l_dst", [P, 1])
    diag = sb("diag", [P, P])
    onesf = sb("onesf", [P, P])
    ramp = sb("ramp", [RP, N // RP], I32)
    bias = sb("bias", [1, 2 * D])
    bpart = sb("bpart", [1, 3, 2 * D], BF16)
    spread = first.enter_context(nc.psum_tensor("spread", [P, P], F32))
    f_num = sb("f_num", [P, 1], I32)
    zeros = sb("zeros", [P, CB * D])

    blank = sem("blank")
    edges_in = sem("edges_in")
    weights_in = sem("weights_in")
    ramp_out = sem("ramp_out")
    consts = sem("consts")
    dve_step = sem("dve_step")
    counted = sem("counted")
    max_known = sem("max_known")
    diag_ready = sem("diag_ready")
    spread_ready = sem("spread_ready")
    record_ready = sem("record_ready")
    record_out = sem("record_out")
    bias_ready = sem("bias_ready")
    bias_out = sem("bias_out")
    bias_in = sem("bias_in")
    f_ready = sem("f_ready")
    f_put_out = sem("f_put_out")
    nb_known = sem("nb_known")
    filled = sem("filled")

    with nc.Block() as block:
        @block.sync
        def _(sp):
            sp.wait_ge(blank, 2)
            for tile, lead, width in ((di, 1, EPR + 3), (si, 0, EPR + 1)):
                t = dst if tile is di else src
                if lead:
                    sp.dma_start(tile[0:1, 1:width], bass.AP(t.tensor, 0, [[EPR, 1], [1, width - 1]])).then_inc(edges_in, 16)
                else:
                    sp.dma_start(tile[0:1, :], bass.AP(t.tensor, 0, [[EPR, 1], [1, width]])).then_inc(edges_in, 16)
                sp.dma_start(tile[1:P - 1, :], bass.AP(t.tensor, EPR - lead, [[EPR, P - 2], [1, width]])).then_inc(edges_in, 16)
                sp.dma_start(tile[P - 1:P, 0:LAST + lead],
                             bass.AP(t.tensor, EPR * (P - 1) - lead, [[EPR, 1], [1, LAST + lead]])).then_inc(edges_in, 16)
            sp.wait_ge(consts, 1)
            sp.dma_start(redirect.rearrange("(p f) o -> p (f o)", p=RP), ramp[:]).then_inc(ramp_out, 16)
            sp.wait_ge(record_ready, 1)
            sp.dma_start(recs.rearrange("(p e) r -> p (e r)", p=P), record[:].rearrange("p e r -> p (e r)")).then_inc(record_out, 16)
            sp.wait_ge(nb_known, 1)
            nb = sp.value_load(v["nb_i"][0:1, 0:1], min_val=1, max_val=MAXB)
            end = sp.value_load(v["nb_i"][0:1, 2:3], min_val=FEWB, max_val=MAXB)
            with sp.If(nb < end):
                with sp.Fori(0, end - nb) as i:
                    at = nc.s_assert_within(HID0 + P + P * CB * (nb + i), 0, HROWS - P * CB,
                                            skip_runtime_bounds_check_because="nb + i is less than MAXB")
                    sp.dma_start(v["h_all"][bass.ds(at, P * CB), :].rearrange("(p r) d -> p (r d)", p=P),
                                 zeros[:]).then_inc(filled, 16)
                    alone_wait(sp, filled, 16 * i + 16, v["mark"])
            sp.wait_ge(record_out, 16)
            sp.wait_ge(ramp_out, 16)

        @block.scalar
        def _(act):
            act.dma_start(bias[0:1, 0:D], v["b1"].rearrange("(o d) -> o d", o=1)).then_inc(weights_in, 16)
            act.dma_start(bias[0:1, D:2 * D], v["b2"].rearrange("(o d) -> o d", o=1)).then_inc(weights_in, 16)
            for n in ("w1l", "w1r", "w2l", "w2r"):
                act.dma_start(W[n + "_sb"][:], v[n].rearrange("(h k) n -> k h n", k=P)).then_inc(weights_in, 16)
            act.wait_ge(bias_ready, 1)
            act.dma_start(bias_parts.rearrange("(o t) n -> o t n", o=1), bpart[:]).then_inc(bias_out, 16)
            act.wait_ge(bias_out, 16)
            for r in range(2):
                act.dma_start(bias3[:, :, r, :], bias_parts.rearrange("t (l n) -> t l n", l=2)).then_inc(bias_in, 16)
            act.wait_ge(bias_in, 32)

        @block.gpsimd
        def _(pool):
            nc.gpsimd.memset(di[:], -1).then_inc(blank, 1)
            nc.gpsimd.memset(si[:], -1).then_inc(blank, 1)
            nc.gpsimd.iota(ramp[:], pattern=[[1, N // RP]], base=0, channel_multiplier=N // RP).then_inc(consts, 1)
            nc.gpsimd.iota(pos1[:], pattern=[[1, EPR]], base=1, channel_multiplier=0,
                           allow_small_or_imprecise_dtypes=True).then_inc(consts, 1)
            nc.gpsimd.iota(v["edge0"][:], pattern=[[1, 1]], base=-1, channel_multiplier=EPR,
                           allow_small_or_imprecise_dtypes=True).then_inc(consts, 1)
            nc.gpsimd.iota(v["slot0"][:], pattern=[[P, CB]], base=HID0 + P, channel_multiplier=1).then_inc(consts, 1)
            nc.gpsimd.iota(f_num[:], pattern=[[1, 1]], base=HID0, channel_multiplier=1).then_inc(consts, 1)
            nc.gpsimd.memset(ident[:], 0.0).then_inc(consts, 1)
            pool.wait_ge(consts, 6)
            nc.gpsimd.affine_select(out=ident[:], in_=ident[:], compare_op=ALU.not_equal, fill=1.0, base=0,
                                    pattern=[[-1, P]], channel_multiplier=1).then_inc(consts, 1)
            nc.gpsimd.memset(onesf[:], 1.0).then_inc(consts, 1)
            nc.gpsimd.memset(ones3[:], 1.0).then_inc(consts, 1)
            pool.wait_ge(consts, 9)
            pool.wait_ge(counted, 1)
            nc.gpsimd.partition_all_reduce(cmax[:], cnt[:], P, bass.bass_isa.ReduceOp.max).then_inc(max_known, 1)
            pool.wait_ge(f_ready, 1)
            pool.wait_ge(ramp_out, 16)
            nc.gpsimd.indirect_dma_start(redirect, bass.IndirectOffsetOnAxis(v["f_put"][:, 0:1], 0), f_num[:], None,
                                         bounds_check=N - 1, oob_is_err=False).then_inc(f_put_out, 16)
            pool.wait_ge(f_put_out, 16)

        @block.tensor
        def _(pe):
            pe.wait_ge(diag_ready, 1)
            nc.tensor.matmul(spread[:], onesf[:], diag[:], start=True, stop=True).then_inc(spread_ready, 1)

        @block.vector
        def _(dve):
            steps = [0]

            def then(ins):
                steps[0] += 1
                ins.then_inc(dve_step, 1)
                dve.wait_ge(dve_step, steps[0])

            ve = nc.vector
            ve.memset(zeros[:], 0.0)
            ve.memset(v["ln_eps"][:], LN_EPS)
            then(ve.memset(v["order"][:], 0.0))
            dve.wait_ge(consts, 9)
            dve.wait_ge(edges_in, 16 * 6)
            ve.tensor_copy(df[:], di[:])
            then(ve.tensor_copy(sf[:], si[:]))
            ve.tensor_tensor(last[:], df[:, 1:EPR + 2], df[:, 2:EPR + 3], ALU.not_equal)
            then(ve.tensor_tensor(lself[:], sf[:], df[:, 1:EPR + 2], ALU.is_equal))
            then(ve.tensor_tensor(lself[:], lself[:], last[:], ALU.mult))
            then(ve.tensor_scalar(tmp[:, 0:EPR], df[:, 1:EPR + 1], 0.0, None, ALU.is_ge))
            then(ve.scalar_tensor_tensor(listed[:], lself[:, 0:EPR], 0.0, tmp[:, 0:EPR], ALU.is_equal, ALU.mult))
            then(ve.tensor_reduce(cnt[:], listed[:], AX.X, ALU.add))
            ve.tensor_tensor(key[:], listed[:], pos1[:], ALU.mult).then_inc(counted, 1)
            ve.tensor_copy(record[:, :, SRC], sf[:, 0:EPR])
            ve.tensor_copy(record[:, :, DST], df[:, 1:EPR + 1])
            then(ve.tensor_tensor(record[:, :, SAME], df[:, 0:EPR], df[:, 1:EPR + 1], ALU.is_equal))
            then(ve.memset(record[:, 0:1, SAME], 0.0))
            then(ve.tensor_scalar(record[:, :, BASE], last[:, 0:EPR], -1.0, 1.0, ALU.mult, ALU.add))
            then(ve.tensor_tensor(tmp[:, 0:EPR], df[:, 1:EPR + 1], df[:, 2:EPR + 2], ALU.is_equal))
            then(ve.tensor_tensor(tmp[:, 0:EPR], tmp[:, 0:EPR], lself[:, 1:EPR + 1], ALU.mult))
            then(ve.tensor_tensor(tmp[:, 0:EPR], tmp[:, 0:EPR], last[:, 0:EPR], ALU.max))
            then(ve.tensor_scalar(over[:], df[:, 1:EPR + 1], df[:, 0:1], None, ALU.is_equal))
            then(ve.tensor_tensor(lself[:, 0:EPR], tmp[:, 0:EPR], listed[:], ALU.mult))
            then(ve.tensor_tensor(record[:, :, ENDF], lself[:, 0:EPR], over[:], ALU.mult))
            then(ve.tensor_tensor(record[:, :, END], lself[:, 0:EPR], record[:, :, ENDF], ALU.subtract))
            then(ve.tensor_reduce(f_has[:], record[:, :, ENDF], AX.X, ALU.add))
            ve.tensor_tensor(over[:], record[:, :, ENDF], record[:, :, BASE], ALU.mult).then_inc(record_ready, 1)
            dve.wait_ge(record_ready, 1)
            then(ve.tensor_reduce(f_tmp[:], over[:], AX.X, ALU.add))
            then(ve.scalar_tensor_tensor(v["f_base"][:], f_tmp[:], 1.0, f_has[:], ALU.add, ALU.subtract))
            then(ve.scalar_tensor_tensor(f_tmp[:], df[:, 0:1], 2.0, f_has[:], ALU.add, ALU.mult))
            then(ve.tensor_scalar(v["f_dst"][:], f_tmp[:], -2.0, None, ALU.add))
            then(ve.tensor_scalar(v["f_get"][:], v["f_dst"][:], 0.0, None, ALU.max))
            then(ve.scalar_tensor_tensor(f_tmp[:], df[:, 0:1], float(-BIG), f_has[:], ALU.add, ALU.mult))
            then(ve.tensor_scalar(v["f_put"][:], f_tmp[:], float(BIG), None, ALU.add))
            ve.tensor_scalar(diag[:], ident[:], v["f_dst"][:, 0:1], None, ALU.mult).then_inc(diag_ready, 1)
            then(ve.scalar_tensor_tensor(l_has[:], tmp[:, EPR - 1:EPR], 0.0, listed[:, EPR - 1:EPR], ALU.is_equal, ALU.mult))
            then(ve.scalar_tensor_tensor(l_dst[:], df[:, EPR:EPR + 1], 3.0, l_has[:], ALU.add, ALU.mult))
            then(ve.tensor_scalar(l_dst[:], l_dst[:], -3.0, None, ALU.add))
            dve.wait_ge(spread_ready, 1)
            ve.tensor_scalar(v["carry"][:], spread[:], l_dst[:, 0:1], None, ALU.is_equal).then_inc(f_ready, 1)
            dve.wait_ge(max_known, 1)
            then(ve.tensor_scalar(nbi[:], cmax[0:1, :], float(CB - 1), None, ALU.add))
            then(ve.tensor_scalar(nbi[:], nbi[:], CB.bit_length() - 1, None, ALU.logical_shift_right))
            then(ve.tensor_scalar(v["nb_i"][:, 0:1], nbi[:], 1.0, None, ALU.max))
            then(ve.tensor_scalar(v["nb_i"][:, 1:2], v["nb_i"][:, 0:1], float(TRI - 1), None, ALU.min))
            then(ve.tensor_scalar(nbi[:], v["nb_i"][:, 0:1], float(FEWB), float(MAXB - FEWB), ALU.is_gt, ALU.mult))
            ve.tensor_scalar(v["nb_i"][:, 2:3], nbi[:], float(FEWB), None, ALU.add).then_inc(nb_known, 1)
            dve.wait_ge(nb_known, 1)
            dve.wait_ge(weights_in, 16 * 6)
            for n in "12":
                ve.tensor_tensor(W[f"w{n}s_sb"][:], W[f"w{n}l_sb"][:], W[f"w{n}r_sb"][:], ALU.add)
            for t in range(2):
                then(ve.tensor_copy(bpart[:, t, :], bias[:]))
                then(ve.tensor_tensor(bias[:], bias[:], bpart[:, t, :], ALU.subtract))
            ve.tensor_copy(bpart[:, 2, :], bias[:]).then_inc(bias_ready, 1)
            nb = dve.value_load(v["nb_i"][0:1, 0:1], min_val=1, max_val=MAXB)
            base = steps[0]
            with dve.Fori(0, nb) as i:
                ve.max(best[:], key[:]).then_inc(dve_step, 1)
                dve.wait_ge(dve_step, 3 * i + base + 1)
                ve.tensor_copy(v["order"][:, bass.ds(CB * i + 2 * CB, CB)], best[:]).then_inc(dve_step, 1)
                ve.match_replace(key[:], best[:], key[:], 0.0).then_inc(dve_step, 1)
                dve.wait_ge(dve_step, 3 * i + base + 3)


def alone_wait(eng, sem, value, mark):
    eng.wait_ge(sem, value)
    eng.sem_inc(mark)


def column_buffers(nc, stack, v):

    def sb(name, shape, dt=F32):
        return stack.enter_context(nc.sbuf_tensor(name, shape, dt))

    c = {
        "gathered": sb("gathered", [P, CB, D + 1]),
        "own": sb("own", [P, CB, D + 1]),
        "acc": [sb(f"acc{i}", [P, D + 1]) for i in range(2)],
        "over_sum": sb("over_sum", [P, D + 1]),
        "sum": [sb(f"sum{i}", [P, D + 1]) for i in range(2)],
        "inv": sb("inv", [P, 2]),
        "mean": [sb(f"mean{i}", [P, D]) for i in range(2)],
        "colT": [sb(f"colT{i}", [P, 2 * H, P]) for i in range(2)],
        "col_ss": sb("col_ss", [P, 2]),
        "col_rt": sb("col_rt", [P, 2]),
        "col_q": sb("col_q", [P, 2]),
        "col_rn": sb("col_rn", [P, 2]),
        "col_junk": [sb(f"col_junk{i}", [P, D], BF16) for i in range(2)],
        "col_out": sb("col_out", [P, CB, D]),
        "ps_colT": [stack.enter_context(nc.psum_tensor(f"ps_colT{i}", [P, 2 * H, P], F32)) for i in range(2)],
    }
    pair = stack.enter_context(nc.psum_tensor("ps_col", [P, 2, D], F32))
    c["ps_col"] = [pair[:, n, :] for n in range(2)]
    return c


def inverse_norm(nc, dve, root, t, result, stepped, n, made):
    nc.vector.reciprocal(t[:], root[:]).then_inc(stepped, 1)
    dve.wait_ge(stepped, n)
    nc.vector.tensor_scalar(result[:], t[:], 1.0 / NORM_EPS, None, ALU.min).then_inc(made, 1)


def column_steps(nc, v, b, s, wl, wr, layer, one_bank):
    ve, se, te = nc.vector, nc.scalar, nc.tensor
    cur, ident, bias3 = v["cur"], v["ident"], v["bias3"]

    def prep(dve, i, q):
        c, par = CB * i + CB - 1 - q, (CB - 1 - q) % 2
        dve.wait_ge(s["gathered"][q], 16 * i + 16)
        dve.wait_ge(s["own"][q], 16 * i + 16)
        ve.scalar_tensor_tensor(b["acc"][par][:], b["acc"][1 - par][:], cur[:, 2, q:q + 1], b["gathered"][:, q, :],
                                ALU.mult, ALU.add).then_inc(s["acc_made"], 1)
        dve.wait_ge(s["acc_made"], c + 1)
        ve.scalar_tensor_tensor(b["over_sum"][:], b["acc"][par][:], cur[:, 4, q:q + 1], b["over_sum"][:],
                                ALU.mult, ALU.add)
        total(dve, c, q, par, cur[:, 3, q:q + 1])

    def total(dve, c, q, par, base):
        dve.wait_ge(s["mean_made"], c + 1)
        ve.scalar_tensor_tensor(b["sum"][par][:], b["own"][:, q, :], base, b["acc"][par][:],
                                ALU.mult, ALU.add).then_inc(s["sum_made"], 1)
        dve.wait_ge(s["sum_made"], c + 1)
        ve.reciprocal(b["inv"][:, par:par + 1], b["sum"][par][:, D:D + 1]).then_inc(s["inv_made"], 1)

    def mean(act, c, par):
        act.wait_ge(s["inv_made"], c + 1)
        act.wait_ge(s["transposed"], c + CB - 1)
        se.activation(b["mean"][par][:], b["sum"][par][:, 0:D], ACT.Copy,
                      scale=b["inv"][:, par:par + 1]).then_inc(s["mean_made"], 1)

    def transposes(pe, c, q, par):
        pe.wait_ge(s["mean_made"], c + 3)
        for h in range(H):
            te.transpose(b["ps_colT"][par][:, h, :], b["mean"][par][:, h * P:(h + 1) * P], ident[:])
        for h in range(H):
            last = te.transpose(b["ps_colT"][par][:, H + h, :], b["own"][:, q, h * P:(h + 1) * P], ident[:])
        last.then_inc(s["transposed"], 1)

    def copy_transposed(act, c, par):
        act.wait_ge(s["transposed"], c + CB + 1)
        act.wait_ge(s["multiplied"], c + 1)
        se.copy(b["colT"][par][:], b["ps_colT"][par][:]).then_inc(s["copied"], 1)

    def products(pe, c, par):
        pe.wait_ge(s["copied"], c + 1)
        pe.wait_ge(s["drained"], c + 1 + (one_bank and par == 0))
        z = b["ps_col"][par]
        te.matmul(z, v["ones3"][:], bias3[:, layer, 0, :], start=True, stop=False)
        for h in range(2 * H):
            last = te.matmul(z, b["colT"][par][:, h, :], (wl if h < H else wr)[:, h % H, :],
                             start=False, stop=(h == 2 * H - 1))
        last.then_inc(s["multiplied"], 1)

    def squares(act, c, par, columns=2):
        act.wait_ge(s["multiplied"], c + 3 + (one_bank and par == 0 and columns == 2))
        se.activation(b["col_junk"][par][:], b["ps_col"][par], ACT.Square,
                      accum_out=b["col_ss"][:, par:par + 1]).then_inc(s["squared"], 1)

    def root(act, n, columns=2):
        act.wait_ge(s["squared"], 2 * n + columns)
        se.activation(b["col_rt"][:], b["col_ss"][:], ACT.Sqrt).then_inc(s["rooted"], 1)

    def norm(dve, n):
        dve.wait_ge(s["rooted"], n + 1)
        inverse_norm(nc, dve, b["col_rt"], b["col_q"], b["col_rn"], s["inverted"], n + 1, s["normed"])

    return prep, total, mean, transposes, copy_transposed, products, squares, root, norm


def clear_semaphores(nc, s):
    with nc.Block() as block:
        @block.gpsimd
        def _(pool):
            for entry in [s[n] for n in s if n not in ("gathered", "own")]:
                for one in entry if isinstance(entry, list) else [entry]:
                    pool.sem_clear(one)


def column_sems(sem, sems):
    s = {n: sem(f"col_{n}") for n in ("acc_made", "sum_made", "inv_made", "mean_made", "transposed", "copied",
                                        "multiplied", "drained", "squared", "rooted", "inverted", "normed",
                                        "over_added", "carried")}
    for n in ("gathered", "own", "stored", "own_stored"):
        s[n] = sems(f"col_{n}", CB)
    return s


def dense_and_first(nc, stack, v, b):
    sem, sems, x, out, h_all = v["sem"], v["sems"], v["x"], v["out"], v["h_all"]
    W, ident, bias3, ones3 = v["W"], v["ident"], v["bias3"], v["ones3"]
    cur, kept, got, valid = v["cur"], v["kept"], v["got"], v["valid"]
    ve, se, te = nc.vector, nc.scalar, nc.tensor

    def sb(name, shape, dt=F32):
        return stack.enter_context(nc.sbuf_tensor(name, shape, dt))

    def pb(name):
        return stack.enter_context(nc.psum_tensor(name, [P, 2, D], F32))

    xt = [sb(f"x_tile{s}", [P, JT, D]) for s in range(SLOTS)]
    ht = [sb(f"h_tile{s}", [P, JT, D]) for s in range(SLOTS)]
    ot = [sb(f"o_tile{s}", [P, JT, D]) for s in range(SLOTS)]
    xT = sb("xT", [P, 2, H, P])
    hT = sb("hT", [P, 2, H, P])
    ss1, rt1, q1, rn1 = (sb(f"{n}1", [P, 2]) for n in ("ss", "rt", "q", "rn"))
    ss2, q2, rn2 = (sb(f"{n}2", [P, 2]) for n in ("ss", "q", "rn"))
    rt2 = [sb(f"rt2_{n}", [P, 2]) for n in range(2)]
    rt3 = sb("rt3", [P, 2])
    junk1, junk2 = sb("junk1", [P, 2, D], BF16), sb("junk2", [P, 2, 2, D], BF16)
    stats, mv, rstd = sb("stats", [P, 2, 6]), sb("mv", [P, 2, 2, 2]), sb("rstd", [P, 2])
    r_idx, r_got = sb("r_idx", [P, CB], I32), sb("r_got", [P, CB], I32)
    ps_xT, ps_hT, ps_z1 = pb("ps_xT"), pb("ps_hT"), pb("ps_z1")
    ps_z2 = [pb("ps_z2a"), pb("ps_z2b")]

    x_in, h_out, o_out = sems("x_in", SLOTS), sems("h_out", SLOTS), sems("o_out", SLOTS)
    xT_made, xT_copied, z1_made, z1_squared, z1_normed, h_made = map(
        sem, ("xT_made", "xT_copied", "z1_made", "z1_squared", "z1_normed", "h_made"))
    hT_made, hT_copied, z2_made, z2_squared, z2_normed = map(
        sem, ("hT_made", "hT_copied", "z2_made", "z2_squared", "z2_normed"))
    z1_rooted, z1_step, z2_rooted, z2_step = map(sem, ("z1_rooted", "z1_step", "z2_rooted", "z2_step"))
    y_made, y_stats, y_aggr, y_rooted, y_rstd, o_made = map(
        sem, ("y_made", "y_stats", "y_aggr", "y_rooted", "y_rstd", "o_made"))
    ready, e_made, rec_got, cur_made, r_put, own_out = map(
        sem, ("ready", "e_made", "rec_got", "cur_made", "r_put", "own_out_all"))
    own_stored = v["col_sems"]["own_stored"]
    conv_step, key_step = sem("conv_step"), sem("key_step")
    r_asked, r_found, r_kept = sem("r_asked"), sem("r_found"), sem("r_kept")
    s = v["col_sems"]
    prep, total, mean, transposes, copy_transposed, products, squares, root, norm = column_steps(
        nc, v, b, s, W["w1l_sb"], W["w1r_sb"], 0, one_bank=True)

    x_sup = x[0:NSUP * ROWS, :].rearrange("(t p j) d -> t p j d", p=P, j=JT)
    h_sup = h_all[0:NSUP * ROWS, :].rearrange("(t p j) d -> t p j d", p=P, j=JT)
    o_sup = out[0:NSUP * ROWS, :].rearrange("(t p j) d -> t p j d", p=P, j=JT)
    tail = lambda a: a[NSUP * ROWS:N, :].rearrange("(p j) d -> p j d", j=2)
    self_x = v["self_x"]

    def counts(eng):
        nb = eng.value_load(v["nb_i"][0:1, 0:1], min_val=1, max_val=MAXB)
        n1 = eng.value_load(v["nb_i"][0:1, 1:2], min_val=1, max_val=TRI - 1)
        return nb, n1

    def loops(eng, step, block_end=None, alone=None):
        nb, n1 = counts(eng)
        with eng.Fori(0, n1) as i:
            for k in range(PAIRS):
                step(i, k, BESIDE[k])
            if block_end:
                block_end(i, nb)
        with eng.Fori(n1, TRI) as i:
            for k in range(PAIRS):
                step(i, k, ())
        step(TRI, 0, ())
        if alone:
            with eng.If(nb > n1):
                with eng.Fori(n1, nb) as i:
                    alone(i)
                    if block_end:
                        block_end(i, nb)
        return nb

    def delayed(eng, i, k, by, work):
        if k >= by or isinstance(i, int):
            work()
        else:
            with eng.If(i > 0):
                work()

    with nc.Block() as block:
        @block.sync
        def _(sp):
            sp.sem_inc(o_out[SLOTS - 1], 16)
            for t in range(SLOTS):
                sp.dma_start(xt[t][:], x_sup[t]).then_inc(x_in[t], 16)

            def stores(i, t, view_h, view_o, part, refill):
                sp.wait_ge(h_made, PAIRS * i + 2 * t + 2)
                sp.dma_start(view_h, ht[t][part]).then_inc(h_out[t], 16)
                if refill:
                    sp.wait_ge(y_made, PAIRS * i + 2 * t + 4)
                    refill()
                sp.wait_ge(o_made, PAIRS * i + 2 * t + 2)
                sp.dma_start(view_o, ot[t][part]).then_inc(o_out[t], 16)

            whole = (slice(0, P), slice(0, JT), slice(0, D))
            with sp.Fori(0, TRI - 1) as i:
                for t in range(SLOTS):
                    n = SLOTS * i + t
                    stores(i, t, h_sup[n], o_sup[n], whole,
                           lambda: sp.dma_start(xt[t][:], x_sup[n + SLOTS]).then_inc(x_in[t], 16))
            for t in range(SLOTS):
                n = SLOTS * (TRI - 1) + t
                stores(TRI - 1, t, h_sup[n], o_sup[n], whole, None if t else
                       lambda: sp.dma_start(xt[0][0:TP, 0:2, :], tail(x)).then_inc(x_in[0], 16))
            part = (slice(0, TP), slice(0, 2), slice(0, D))
            sp.wait_ge(h_made, LASTU + 1)
            sp.dma_start(tail(h_all), ht[0][part]).then_inc(h_out[0], 16)
            sp.wait_ge(o_made, LASTU + 1)
            sp.dma_start(tail(out), ot[0][part]).then_inc(o_out[0], 16)
            for t in range(SLOTS):
                sp.wait_ge(h_out[t], 16 * (TRI + (t == 0)))
                sp.wait_ge(o_out[t], 16 * (TRI + (t in (0, SLOTS - 1))))

        @block.gpsimd
        def _(pool):
            nb, n1 = counts(pool)

            def gather_records(i):
                alone_wait(pool, e_made, i + 1, v["mark"])
                for q in range(CB):
                    nc.gpsimd.indirect_dma_start(got[:, q, :], None, v["recs"],
                                                 bass.IndirectOffsetOnAxis(v["e_idx"][:, q:q + 1], 0)).then_inc(rec_got, 16)

            gather_records(0)
            with pool.Fori(0, nb) as i:
                pool.wait_ge(cur_made, i + 1)
                for q in reversed(range(CB)):
                    pool.wait_ge(s["transposed"], CB * i + CB - q)
                    alone_wait(pool, own_stored[q], 16 * i, v["mark"])
                    nc.gpsimd.indirect_dma_start(b["gathered"][:, q, 0:D], None, x,
                                                 bass.IndirectOffsetOnAxis(v["src_i"][:, q:q + 1], 0)).then_inc(s["gathered"][q], 16)
                    nc.gpsimd.indirect_dma_start(b["own"][:, q, 0:D], None, x,
                                                 bass.IndirectOffsetOnAxis(v["dst_i"][:, q:q + 1], 0)).then_inc(s["own"][q], 16)
                    nc.gpsimd.indirect_dma_start(v["redirect"], bass.IndirectOffsetOnAxis(v["put_i"][:, q:q + 1], 0),
                                                 v["slot_i"][:, q:q + 1], None,
                                                 bounds_check=N - 1, oob_is_err=False).then_inc(r_put, 16)
                gather_records(i + 1)
            q = CB - 1
            pool.wait_ge(s["transposed"], CB * nb + 1)
            alone_wait(pool, own_stored[q], 16 * nb, v["mark"])
            nc.gpsimd.indirect_dma_start(b["own"][:, q, 0:D], None, x,
                                         bass.IndirectOffsetOnAxis(v["f_get"][:, 0:1], 0)).then_inc(s["own"][q], 16)
            pool.wait_ge(cur_made, nb + 1)
            alone_wait(pool, r_put, 16 * CB * nb, v["mark"])
            with pool.Fori(0, nb) as i:
                nc.gpsimd.tensor_copy(r_idx[:], kept[:, bass.ds(i, 1), 0, :].rearrange("p o c -> p (o c)")).then_inc(r_asked, 1)
                alone_wait(pool, r_asked, i + 1, v["mark"])
                for q in range(CB):
                    nc.gpsimd.indirect_dma_start(r_got[:, q:q + 1], None, v["redirect"],
                                                 bass.IndirectOffsetOnAxis(r_idx[:, q:q + 1], 0)).then_inc(r_found, 16)
                pool.wait_ge(r_found, 16 * CB * i + 16 * CB)
                nc.gpsimd.tensor_copy(v["hrow"][:, bass.ds(i, 1), :].rearrange("p o c -> p (o c)"), r_got[:]).then_inc(r_kept, 1)
                pool.wait_ge(r_kept, i + 1)
            pool.wait_ge(rec_got, 16 * CB * nb + 16 * CB)

        @block.tensor
        def _(pe):
            pe.wait_ge(ready, 1)
            pe.sem_inc(s["transposed"], CB)
            pe.sem_inc(s["multiplied"], 2)

            def transpose_x(i, k):
                t = k // 2
                if k % 2 == 0:
                    pe.wait_ge(x_in[t], 16 * i + 16)
                pe.wait_ge(xT_copied, PAIRS * i + k)
                for r in range(2):
                    for h in range(H):
                        last = te.transpose(ps_xT[:, r, h * P:(h + 1) * P],
                                            xt[t][:, 2 * (k % 2) + r, h * P:(h + 1) * P], ident[:])
                last.then_inc(xT_made, 1)

            def layer(z, aT, w, number, made):
                te.matmul(z[:], ones3[:], bias3[:, number], start=True, stop=False)
                for r in range(2):
                    for h in range(H):
                        last = te.matmul(z[:, r, :], aT[:, r, h, :], w[:, h, :], start=False, stop=(r == 1 and h == H - 1))
                last.then_inc(made, 1)

            def layer_2(i, k, par):
                u = PAIRS * i + k
                pe.wait_ge(hT_copied, u)
                pe.wait_ge(y_made, u)
                layer(ps_z2[par], hT, W["w2s_sb"], 1, z2_made)

            def step(i, k, cols):
                u = PAIRS * i + k
                pe.wait_ge(xT_copied, u + 1)
                layer(ps_z1, xT, W["w1s_sb"], 0, z1_made)
                for q in cols:
                    transposes(pe, CB * i + CB - 1 - q, q, (CB - 1 - q) % 2)
                if k < PAIRS - 1 and not (isinstance(i, int) and i == TRI):
                    transpose_x(i, k + 1)
                elif k == PAIRS - 1:
                    transpose_x(i + 1, 0)
                delayed(pe, i, k, 1, lambda: layer_2(i, k, (k + 1) % 2))
                for q in cols:
                    products(pe, CB * i + CB - 1 - q, (CB - 1 - q) % 2)
                pe.wait_ge(h_made, u + 1)
                for r in range(2):
                    for h in range(H):
                        last = te.transpose(ps_hT[:, r, h * P:(h + 1) * P],
                                            ht[k // 2][:, 2 * (k % 2) + r, h * P:(h + 1) * P], ident[:])
                last.then_inc(hT_made, 1)

            def alone(i):
                for q in reversed(range(CB)):
                    transposes(pe, CB * i + CB - 1 - q, q, (CB - 1 - q) % 2)
                    products(pe, CB * i + CB - 1 - q, (CB - 1 - q) % 2)

            transpose_x(0, 0)
            nb = loops(pe, step, alone=alone)
            layer_2(TRI, 1, 0)
            over_column(pe, nb, s, b, v, nc, transposes, products)

        @block.scalar
        def _(act):
            act.sem_inc(s["mean_made"], 2)
            act.sem_inc(s["drained"], 2)
            act.sem_inc(z2_rooted, 1)
            act.sem_inc(y_rooted, 3)

            def squares_2(i, k, par):
                u = PAIRS * i + k
                act.wait_ge(z2_made, u)
                for r in range(2):
                    last = se.activation(junk2[:, par, r, :], ps_z2[par][:, r, :], ACT.Square,
                                         accum_out=ss2[:, r:r + 1])
                last.then_inc(z2_squared, 1)
                act.wait_ge(z2_squared, u)
                act.wait_ge(z2_normed, u)
                se.activation(rt2[par][:], ss2[:], ACT.Sqrt).then_inc(z2_rooted, 1)

            def deviation(i, k, par):
                act.wait_ge(y_aggr, PAIRS * i + k)
                act.wait_ge(y_rstd, PAIRS * i + k)
                se.activation(rt3[:], mv[:, par, :, 1], ACT.Sqrt, bias=v["ln_eps"][:, 0:1]).then_inc(y_rooted, 1)

            def finish(i, qs, rows):
                c, pair = CB * i + CB - 1 - qs[0], CB // 2 * i + (CB - 1 - qs[0]) // 2
                for n, q in enumerate(qs):
                    squares(act, c + n, n, len(qs))
                root(act, pair, len(qs))
                act.wait_ge(s["normed"], pair + 1)
                for n, q in enumerate(qs):
                    act.wait_ge(s["stored"][q], 16 * i)
                    se.activation(b["col_out"][:, q, :], b["ps_col"][n], ACT.Relu,
                                  scale=b["col_rn"][:, n:n + 1]).then_inc(s["drained"], 1)
                for n, q in enumerate(qs):
                    act.wait_ge(s["drained"], c + n + 3)
                    act.dma_start(h_all[bass.ds(HID0 + rows - P * n, P), :], b["col_out"][:, q, :]).then_inc(s["stored"][q], 16)
                    act.dma_start(self_x[bass.ds(rows - P * n, P), :], b["own"][:, q, 0:D]).then_inc(own_stored[q], 16)

            def step(i, k, cols):
                u = PAIRS * i + k
                for q in cols:
                    mean(act, CB * i + CB - 1 - q, (CB - 1 - q) % 2)
                delayed(act, i, k, 3, lambda: deviation(i, k, (k + 1) % 2))
                act.wait_ge(z1_made, u + 1)
                for r in range(2):
                    last = se.activation(junk1[:, r, :], ps_z1[:, r, :], ACT.Square, accum_out=ss1[:, r:r + 1])
                last.then_inc(z1_squared, 1)
                for q in cols:
                    copy_transposed(act, CB * i + CB - 1 - q, (CB - 1 - q) % 2)
                act.wait_ge(z1_squared, u + 1)
                se.activation(rt1[:], ss1[:], ACT.Sqrt).then_inc(z1_rooted, 1)
                act.wait_ge(z1_normed, u + 1)
                if k % 2 == 0:
                    act.wait_ge(h_out[k // 2], 16 * i)
                for r in range(2):
                    last = se.activation(ht[k // 2][:, 2 * (k % 2) + r, :], ps_z1[:, r, :], ACT.Relu, scale=rn1[:, r:r + 1])
                last.then_inc(h_made, 1)
                delayed(act, i, k, 1, lambda: squares_2(i, k, (k + 1) % 2))
                if cols:
                    finish(i, cols, P * CB * i + P * (1 + cols[0]))
                act.wait_ge(hT_made, u + 1)
                se.copy(hT[:].rearrange("p r h c -> p (r h c)"), ps_hT[:].rearrange("p r c -> p (r c)")).then_inc(hT_copied, 1)

            def alone(i):
                for q in range(CB - 1, 0, -2):
                    for n in range(2):
                        mean(act, CB * i + CB - 1 - q + n, n)
                        copy_transposed(act, CB * i + CB - 1 - q + n, n)
                    finish(i, (q, q - 1), P * CB * i + P * (1 + q))

            nb = loops(act, step, alone=alone)
            deviation(TRI, 1, 0)
            squares_2(TRI, 1, 0)
            deviation(TRI, 2, 1)
            deviation(TRI, 3, 0)
            mean(act, CB * nb, 0)
            copy_transposed(act, CB * nb, 0)
            finish(nb, (CB - 1,), 0)
            for q in range(CB):
                act.wait_ge(s["stored"][q], 16 * nb + 16 * (q == CB - 1))
                alone_wait(act, own_stored[q], 16 * nb + 16 * (q == CB - 1), v["mark"])

        @block.vector
        def _(dve):
            for one in (z2_step, z2_normed, y_made, y_stats, y_aggr):
                dve.sem_inc(one, 2)
            dve.sem_inc(y_rstd, 3)
            ve.memset(b["gathered"][:, :, D:D + 1], 1.0)
            ve.memset(b["own"][:, :, D:D + 1], 1.0)
            ve.memset(b["acc"][1][:], 0.0)
            ve.memset(b["over_sum"][:], 0.0)
            ve.tensor_scalar(v["slot_i"][:], v["slot0"][:], float(-P * CB), None, ALU.add).then_inc(ready, 1)
            dve.wait_ge(ready, 1)
            nb_e = counts(dve)[0]

            def keys(i):
                at = nc.s_assert_within(nb_e - i + 1, 0, MAXB + 1,
                                         skip_runtime_bounds_check_because="i is at most nb + 1")
                key = v["order"][:, bass.ds(CB * at, CB)]
                ve.tensor_scalar(valid[:], key, 0.0, None, ALU.is_gt)
                ve.tensor_scalar(v["e_f"][:], key, v["edge0"][:, 0:1], None, ALU.add).then_inc(key_step, 1)
                dve.wait_ge(key_step, i + 1)
                ve.tensor_scalar(v["e_idx"][:], v["e_f"][:], 0.0, None, ALU.max).then_inc(e_made, 1)

            def records(i):
                dve.wait_ge(rec_got, 16 * CB * i + 16 * CB)
                dve.wait_ge(r_put, 16 * CB * i)
                ve.tensor_copy(cur[:, 0, :], got[:, :, SRC])
                ve.tensor_copy(v["src_i"][:], got[:, :, SRC])
                ve.tensor_copy(v["dst_i"][:], got[:, :, DST])
                ve.tensor_tensor(cur[:, 2, :], got[:, :, SAME], valid[:], ALU.mult)
                ve.tensor_copy(cur[:, 3, :], got[:, :, BASE])
                ve.tensor_tensor(cur[:, 4, :], got[:, :, ENDF], valid[:], ALU.mult)
                ve.tensor_tensor(v["end_f"][:], got[:, :, END], valid[:], ALU.mult).then_inc(conv_step, 1)
                dve.wait_ge(conv_step, 3 * i + 1)
                ve.scalar_tensor_tensor(v["end_f"][:], got[:, :, DST], float(-BIG), v["end_f"][:], ALU.add,
                                        ALU.mult).then_inc(conv_step, 1)
                dve.wait_ge(conv_step, 3 * i + 2)
                ve.tensor_scalar(cur[:, 1, :], v["end_f"][:], float(BIG), None, ALU.add).then_inc(conv_step, 1)
                dve.wait_ge(conv_step, 3 * i + 3)
                ve.tensor_copy(kept[:, bass.ds(i, 1), :, :].rearrange("p o k c -> p (o k) c"), cur[:])
                ve.tensor_scalar(v["slot_i"][:], v["slot_i"][:], float(P * CB), None, ALU.add)
                ve.tensor_copy(v["put_i"][:], cur[:, 1, :]).then_inc(cur_made, 1)
                dve.wait_ge(cur_made, i + 1)

            def slot_of(k, by):
                n = (k - by) % PAIRS
                return n // 2, 2 * (n % 2)

            def residual(i, k, par):
                u = PAIRS * i + k
                t, j = slot_of(k, 2)
                dve.wait_ge(z2_rooted, u)
                inverse_norm(nc, dve, rt2[par], q2, rn2, z2_step, u + 1, z2_normed)
                dve.wait_ge(z2_normed, u + 1)
                if j == 0:
                    dve.wait_ge(o_out[t], 16 * i)
                for r in range(2):
                    last = ve.scalar_tensor_tensor(ot[t][:, j + r, :], ps_z2[par][:, r, :], rn2[:, r:r + 1],
                                                   xt[t][:, j + r, :], ALU.mult, ALU.add)
                last.then_inc(y_made, 1)
                dve.wait_ge(y_made, u + 1)
                for r in range(2):
                    last = ve.bn_stats(stats[:, r, :], ot[t][:, j + r, :])
                last.then_inc(y_stats, 1)
                alone_wait(dve, y_stats, u + 1, v["mark"])
                for r in range(2):
                    last = ve.bn_aggr(mv[:, par, r, :], stats[:, r, :])
                last.then_inc(y_aggr, 1)

            def normalise(i, k, par):
                u = PAIRS * i + k
                t, j = slot_of(k, 3)
                dve.wait_ge(y_rooted, u + 1)
                ve.reciprocal(rstd[:], rt3[:]).then_inc(y_rstd, 1)
                dve.wait_ge(y_rstd, u + 1)
                for r in range(2):
                    last = ve.tensor_scalar(ot[t][:, j + r, :], ot[t][:, j + r, :], mv[:, par, r, 0:1], rstd[:, r:r + 1],
                                            ALU.subtract, ALU.mult)
                last.then_inc(o_made, 1)

            def copy_xT(n):
                dve.wait_ge(xT_made, n + 1)
                ve.tensor_copy(xT[:].rearrange("p r h c -> p (r h c)"), ps_xT[:].rearrange("p r c -> p (r c)")).then_inc(xT_copied, 1)

            def step(i, k, cols):
                u = PAIRS * i + k
                for q in cols:
                    prep(dve, i, q)
                delayed(dve, i, k, 3, lambda: normalise(i, k, (k + 1) % 2))
                if not isinstance(i, int):
                    copy_xT(u + 1)
                dve.wait_ge(z1_rooted, u + 1)
                inverse_norm(nc, dve, rt1, q1, rn1, z1_step, u + 1, z1_normed)
                delayed(dve, i, k, 2, lambda: residual(i, k, k % 2))
                if cols:
                    norm(dve, CB // 2 * i + (CB - 1 - cols[0]) // 2)

            def block_end(i, nb):
                records(i + 1)
                keys(i + 2)

            def alone(i):
                for q in range(CB - 1, 0, -2):
                    prep(dve, i, q)
                    prep(dve, i, q - 1)
                    norm(dve, CB // 2 * i + (CB - 1 - q) // 2)

            keys(0)
            records(0)
            keys(1)
            copy_xT(0)
            nb = loops(dve, step, block_end=block_end, alone=alone)
            normalise(TRI, 1, 0)
            residual(TRI, 1, 1)
            normalise(TRI, 2, 1)
            residual(TRI, 2, 0)
            normalise(TRI, 3, 0)
            over_total(dve, nb, s, b, v, nc, total)
            norm(dve, CB // 2 * nb)


def over_column(pe, nb, s, b, v, nc, transposes, products):
    pe.wait_ge(s["acc_made"], CB * nb)
    pe.wait_ge(s["copied"], CB * nb)
    nc.tensor.matmul(b["ps_colT"][1][:].rearrange("p h c -> p (h c)")[:, 0:D + 1], v["carry"][:], b["acc"][1][:],
                     start=True, stop=True).then_inc(s["carried"], 1)
    transposes(pe, CB * nb, CB - 1, 0)
    products(pe, CB * nb, 0)


def over_total(dve, nb, s, b, v, nc, total):
    dve.wait_ge(s["carried"], 1)
    dve.wait_ge(s["inv_made"], CB * nb)
    nc.vector.tensor_tensor(b["acc"][0][:], b["ps_colT"][1][:].rearrange("p h c -> p (h c)")[:, 0:D + 1],
                            b["over_sum"][:], ALU.add).then_inc(s["over_added"], 1)
    dve.wait_ge(s["over_added"], 1)
    dve.wait_ge(s["own"][CB - 1], 16 * nb + 16)
    total(dve, CB * nb, CB - 1, 0, v["f_base"][:, 0:1])


def second_layer(nc, stack, v, b):
    sem, sems, out, h_all, self_x = v["sem"], v["sems"], v["out"], v["h_all"], v["self_x"]
    cur, kept, hrow, W = v["cur"], v["kept"], v["hrow"], v["W"]
    ve, se = nc.vector, nc.scalar

    def sb(name, shape, dt=F32):
        return stack.enter_context(nc.sbuf_tensor(name, shape, dt))

    b = dict(b)
    b["ps_col"] = [stack.enter_context(nc.psum_tensor(f"ps_col_{n}", [P, 2 * D], F32))[:, 0:D] for n in range(2)]
    HB = CB // 2
    x_own = sb("x_own", [P, CB, D])
    get_idx = [sb(f"get_idx{h}", [P, HB], I32) for h in range(2)]
    put_idx = [sb(f"put_idx{h}", [P, HB], I32) for h in range(2)]
    stats, mv, rstd = sb("stats2", [P, 2, 6]), sb("mv2", [P, 2, 2]), sb("rstd2", [P, 2])
    rt3 = sb("rt4", [P, 2])
    cur_in, y_stats, y_aggr, y_rooted, y_rstd, o_made = map(
        sem, ("cols_cur_in", "cols_stats", "cols_aggr", "cols_rooted", "cols_rstd", "cols_o_made"))
    ready, get_made, put_made = sem("l2_ready"), sem("get_made"), sem("put_made")
    s = dict(v["col_sems"])
    s["gathered"], s["own"], s["stored"] = sems("gathered_h", CB), s["stored"], sems("scattered", CB)
    x_in = s["own_stored"]
    prep, total, mean, transposes, copy_transposed, products, squares, root, norm = column_steps(
        nc, v, b, s, W["w2l_sb"], W["w2r_sb"], 1, one_bank=False)

    def count(eng):
        return eng.value_load(v["nb_i"][0:1, 0:1], min_val=1, max_val=MAXB)

    with nc.Block() as block:
        @block.sync
        def _(sp):
            def load(i, q, rows):
                sp.wait_ge(s["transposed"], CB * i + CB - q)
                sp.dma_start(b["own"][:, q, 0:D], h_all[bass.ds(HID0 + rows, P), :]).then_inc(s["own"][q], 16)
                sp.wait_ge(s["stored"][q], 16 * i)
                sp.dma_start(x_own[:, q, :], self_x[bass.ds(rows, P), :]).then_inc(x_in[q], 16)

            nb = count(sp)
            with sp.Fori(0, nb) as i:
                for q in reversed(range(CB)):
                    load(i, q, P * CB * i + P * (1 + q))
            load(nb, CB - 1, 0)

        @block.gpsimd
        def _(pool):
            nb = count(pool)

            def gather(table, i, q):
                h = 0 if q >= HB else 1
                alone_wait(pool, s["transposed"], CB * i + CB - q, v["mark"])
                nc.gpsimd.indirect_dma_start(b["gathered"][:, q, 0:D], None, table,
                                             bass.IndirectOffsetOnAxis(get_idx[h][:, q % HB:q % HB + 1], 0)).then_inc(s["gathered"][q], 16)

            def scatter(i, q):
                h = 0 if q >= HB else 1
                alone_wait(pool, o_made, CB * i + 2 * CB - q, v["mark"])
                nc.gpsimd.indirect_dma_start(out, bass.IndirectOffsetOnAxis(put_idx[h][:, q % HB:q % HB + 1], 0),
                                             b["col_out"][:, q, :], None,
                                             bounds_check=N - 1, oob_is_err=False).then_inc(s["stored"][q], 16)

            def take(tile, source, field, i, lo, made, n, used):
                for q in range(lo, lo + HB):
                    pool.wait_ge(used[q], 16 * i)
                view = (source[:, bass.ds(i, 1), lo:lo + HB] if field is None
                        else source[:, bass.ds(i, 1), field, lo:lo + HB])
                nc.gpsimd.tensor_copy(tile[:], view.rearrange("p o c -> p (o c)")).then_inc(made, 1)
                alone_wait(pool, made, 2 * i + n, v["mark"])

            def sweep(table):
                with pool.Fori(0, nb) as i:
                    take(get_idx[0], hrow, None, i, HB, get_made, 1, s["gathered"])
                    take(put_idx[0], kept, 1, i, HB, put_made, 1, s["stored"])
                    for q in reversed(range(HB, CB)):
                        gather(table, i, q)
                        with pool.If(i > 0):
                            scatter(i - 1, q - HB)
                    take(get_idx[1], hrow, None, i, 0, get_made, 2, s["gathered"])
                    for q in reversed(range(HB)):
                        gather(table, i, q)
                        scatter(i, q + HB)
                    take(put_idx[1], kept, 1, i, 0, put_made, 2, s["stored"])

            with pool.If(nb <= FEWB):
                sweep(h_all[0:N + P * (1 + CB * FEWB), :])
            with pool.Else():
                sweep(h_all)
            for q in reversed(range(HB)):
                scatter(nb - 1, q)
            q = CB - 1
            alone_wait(pool, o_made, CB * nb + CB + 1, v["mark"])
            nc.gpsimd.indirect_dma_start(out, bass.IndirectOffsetOnAxis(v["f_put"][:, 0:1], 0), b["col_out"][:, q, :], None,
                                         bounds_check=N - 1, oob_is_err=False).then_inc(s["stored"][q], 16)
            for q in range(CB):
                pool.wait_ge(s["stored"][q], 16 * nb + 16 * (q == CB - 1))

        @block.tensor
        def _(pe):
            pe.sem_inc(s["transposed"], CB)
            pe.sem_inc(s["multiplied"], 2)
            nb = count(pe)
            with pe.Fori(0, nb) as i:
                transposes(pe, CB * i, CB - 1, 0)
                for j in range(CB):
                    if j + 1 < CB:
                        transposes(pe, CB * i + j + 1, CB - 2 - j, (j + 1) % 2)
                    products(pe, CB * i + j, j % 2)
            over_column(pe, nb, s, b, v, nc, transposes, products)

        @block.scalar
        def _(act):
            act.sem_inc(s["mean_made"], 2)
            nb = count(act)

            def deviation(n):
                act.wait_ge(y_aggr, n + 1)
                se.activation(rt3[:], mv[:, :, 1], ACT.Sqrt, bias=v["ln_eps"][:, 0:1]).then_inc(y_rooted, 1)

            with act.Fori(0, nb) as i:
                for pair in range(CB // 2 + 1):
                    for n in range(2):
                        if pair < CB // 2:
                            mean(act, CB * i + 2 * pair + n, n)
                            copy_transposed(act, CB * i + 2 * pair + n, n)
                    for n in range(2):
                        if pair:
                            squares(act, CB * i + 2 * pair - 2 + n, n)
                    if pair:
                        root(act, CB // 2 * i + pair - 1)
                        deviation(CB // 2 * i + pair - 1)
            mean(act, CB * nb, 0)
            copy_transposed(act, CB * nb, 0)
            squares(act, CB * nb, 0)
            root(act, CB // 2 * nb, 1)
            deviation(CB // 2 * nb)

        @block.vector
        def _(dve):
            dve.sem_inc(s["drained"], 2)
            dve.sem_inc(o_made, CB)
            ve.memset(b["acc"][1][:], 0.0)
            ve.memset(b["over_sum"][:], 0.0).then_inc(ready, 1)
            dve.wait_ge(ready, 1)
            nb = count(dve)

            def output(i, pair, columns=2):
                number, qs = CB // 2 * i + pair, [CB - 1 - 2 * pair - n for n in range(columns)]
                norm(dve, number)
                dve.wait_ge(s["normed"], number + 1)
                for n, q in enumerate(qs):
                    dve.wait_ge(x_in[q], 16 * i + 16)
                    dve.wait_ge(s["stored"][q], 16 * i)
                    ve.scalar_tensor_tensor(b["col_out"][:, q, :], b["ps_col"][n], b["col_rn"][:, n:n + 1],
                                            x_own[:, q, :], ALU.mult, ALU.add).then_inc(s["drained"], 1)
                for n, q in enumerate(qs):
                    dve.wait_ge(s["drained"], 2 * number + n + 3)
                    ve.bn_stats(stats[:, n, :], b["col_out"][:, q, :]).then_inc(y_stats, 1)
                for n, q in enumerate(qs):
                    alone_wait(dve, y_stats, 2 * number + n + 1, v["mark"])
                    last = ve.bn_aggr(mv[:, n, :], stats[:, n, :])
                last.then_inc(y_aggr, 1)

            def normalise(i, pair, columns=2):
                number, qs = CB // 2 * i + pair, [CB - 1 - 2 * pair - n for n in range(columns)]
                dve.wait_ge(y_rooted, number + 1)
                ve.reciprocal(rstd[:], rt3[:]).then_inc(y_rstd, 1)
                dve.wait_ge(y_rstd, number + 1)
                for n, q in enumerate(qs):
                    ve.tensor_scalar(b["col_out"][:, q, :], b["col_out"][:, q, :], mv[:, n, 0:1], rstd[:, n:n + 1],
                                     ALU.subtract, ALU.mult).then_inc(o_made, 1)

            with dve.Fori(0, nb) as i:
                ve.tensor_copy(cur[:], kept[:, bass.ds(i, 1), :, :].rearrange("p o k c -> p (o k) c")).then_inc(cur_in, 1)
                dve.wait_ge(cur_in, i + 1)
                for pair in range(CB // 2 + 1):
                    if pair < CB // 2:
                        prep(dve, i, CB - 1 - 2 * pair)
                        prep(dve, i, CB - 2 - 2 * pair)
                    if pair:
                        output(i, pair - 1)
                        normalise(i, pair - 1)
            over_total(dve, nb, s, b, v, nc, total)
            output(nb, 0, 1)
            normalise(nb, 0, 1)


def kernel(x, src, dst, L0_gnn_W1l, L0_gnn_b1l, L0_gnn_W1r, L0_gnn_W2l, L0_gnn_b2l, L0_gnn_W2r):
    import concourse.bacc as bacc
    from concourse.bass_utils import run_bass_kernel_spmd

    arrays = {
        "x": x, "src": src, "dst": dst,
        "w1l": np.asarray(L0_gnn_W1l).T, "b1": L0_gnn_b1l, "w1r": np.asarray(L0_gnn_W1r).T,
        "w2l": np.asarray(L0_gnn_W2l).T, "b2": L0_gnn_b2l, "w2r": np.asarray(L0_gnn_W2r).T,
    }
    arrays = {name: np.ascontiguousarray(a) for name, a in arrays.items()}
    nc = bacc.Bacc("TRN2", target_bir_lowering=False, num_devices=1)
    args = [nc.dram_tensor(name, a.shape, mybir.dt.from_np(a.dtype), kind="ExternalInput").ap()
            for name, a in arrays.items()]
    out = nc.dram_tensor("out", [N, D], F32, kind="ExternalOutput").ap()
    build_gnn(nc, *args, out)
    result = run_bass_kernel_spmd(nc, [arrays], core_ids=[0])
    return result.results[0]["out"]
```

```python
import numpy as np
import concourse.bass as bass
from concourse import mybir
from contextlib import ExitStack

F32 = mybir.dt.float32
BF16 = mybir.dt.bfloat16
I32 = mybir.dt.int32
ALU = mybir.AluOpType
ACT = mybir.ActivationFunctionType
AX = mybir.AxisListType

P = 128
N = 100000
E = 125000
D = 256
H = D // P
EPR = -(-E // P)
LAST = E - EPR * (P - 1)
CB = 8
MAXB = -(-EPR // CB)
REC = 6
SRC, DST, SAME, BASE, END, ENDF = range(REC)
KEPT = 5
BIG = 1 << 22

ROWS = 512
JT = ROWS // P
SLOTS = 3
TRI = N // ROWS // SLOTS
NSUP = TRI * SLOTS
PAIRS = 2 * SLOTS
TAIL = N - NSUP * ROWS
TP = TAIL // 2
LASTU = NSUP * 2
HID0 = N
HROWS = N + P * (1 + CB * MAXB)
FEWB = 32
RP = 80
LN_EPS = 1e-5
NORM_EPS = 1e-12
WIDE = 2
STARTS = (0, 2, 5, 7)
SUM_A, SUM_B, TURN, MULTIPLY, FINISH = [
    {first + stage: 2 * n for n, first in enumerate(STARTS)} for stage in range(5)]
RECORDS = STARTS[-1] + 2


def build_gnn(nc, x, src, dst, w1l, b1, w1r, w2l, b2, w2r, out):
    ctx = ExitStack()

    def sb(name, shape, dt=F32):
        return ctx.enter_context(nc.sbuf_tensor(name, shape, dt))

    def pb(name, shape):
        return ctx.enter_context(nc.psum_tensor(name, shape, F32))

    def sem(name):
        return ctx.enter_context(nc.semaphore(name))

    def sems(name, n):
        return [sem(f"{name}{i}") for i in range(n)]

    with ctx:
        recs = nc.dram_tensor("edge_records", [P * EPR, REC], F32).ap()
        redirect = nc.dram_tensor("redirect", [N, 1], I32).ap()
        h_all = nc.dram_tensor("h_all", [HROWS, D], F32).ap()
        self_x = nc.dram_tensor("self_x", [P * (1 + CB * MAXB), D], F32).ap()
        bias_parts = nc.dram_tensor("bias_parts", [3, 2 * D], BF16).ap()

        mark = sem("mark")
        ident = sb("ident", [P, P])
        ones3 = sb("ones3", [3, P], BF16)
        ln_eps = sb("ln_eps", [P, 1])
        bias3 = sb("bias3", [3, 2, 2, D], BF16)
        W = {n: sb(n, [P, H, D]) for n in ("w1l_sb", "w1r_sb", "w1s_sb", "w2l_sb", "w2r_sb", "w2s_sb")}
        nb_i = sb("nb_i", [1, 4], I32)
        order = sb("order", [P, (MAXB + 2) * CB])
        edge0 = sb("edge0", [P, 1])
        slot0 = sb("slot0", [P, CB], I32)
        f_dst = sb("f_dst", [P, 1])
        f_base = sb("f_base", [P, 1])
        f_get = sb("f_get", [P, 1], I32)
        f_put = sb("f_put", [P, 1], I32)
        carry = sb("carry", [P, P])
        kept = sb("kept", [P, MAXB + 2, KEPT, CB])
        hrow = sb("hrow", [P, MAXB + 2, CB], I32)
        e_idx = sb("e_idx", [P, CB], I32)
        got = sb("got", [P, CB, REC])
        valid = sb("valid", [P, CB])
        cur = sb("cur", [P, KEPT, CB])
        src_i = sb("src_i", [P, CB], I32)
        dst_i = sb("dst_i", [P, CB], I32)
        put_i = sb("put_i", [P, CB], I32)
        slot_i = sb("slot_i", [P, CB], I32)
        e_f = sb("e_f", [P, CB])
        end_f = sb("end_f", [P, CB])

        with ExitStack() as first:
            prepare_edges(nc, first, locals())
        with ExitStack() as second:
            columns = column_buffers(nc, second, locals())
            col_sems = column_sems(sem, sems)
            with ExitStack() as sweep:
                dense_and_first(nc, sweep, locals(), columns)
            clear_semaphores(nc, col_sems)
            second_layer(nc, second, locals(), columns)
    return nc


def prepare_edges(nc, first, v):
    src, dst, x = v["src"], v["dst"], v["x"]
    recs, redirect, bias_parts = v["recs"], v["redirect"], v["bias_parts"]
    ident, ones3, bias3, W = v["ident"], v["ones3"], v["bias3"], v["W"]

    def sb(name, shape, dt=F32):
        return first.enter_context(nc.sbuf_tensor(name, shape, dt))

    sem = v["sem"]
    di = sb("dst_ints", [P, EPR + 3], I32)
    si = sb("src_ints", [P, EPR + 1], I32)
    df = sb("dst_f", [P, EPR + 3])
    sf = sb("src_f", [P, EPR + 1])
    last = sb("last", [P, EPR + 1])
    lself = sb("lself", [P, EPR + 1])
    tmp = sb("tmp", [P, EPR + 1])
    listed = sb("listed", [P, EPR])
    over = sb("over", [P, EPR])
    record = sb("record", [P, EPR, REC])
    key = sb("key", [P, EPR])
    pos1 = sb("pos1", [P, EPR])
    best = sb("best", [P, CB])
    cnt = sb("cnt", [P, 1])
    cmax = sb("cmax", [P, 1])
    nbi = sb("nbi", [1, 1], I32)
    f_has = sb("f_has", [P, 1])
    f_tmp = sb("f_tmp", [P, 1])
    l_has = sb("l_has", [P, 1])
    l_dst = sb("l_dst", [P, 1])
    diag = sb("diag", [P, P])
    onesf = sb("onesf", [P, P])
    ramp = sb("ramp", [RP, N // RP], I32)
    bias = sb("bias", [1, 2 * D])
    bpart = sb("bpart", [1, 3, 2 * D], BF16)
    spread = first.enter_context(nc.psum_tensor("spread", [P, P], F32))
    f_num = sb("f_num", [P, 1], I32)
    zeros = sb("zeros", [P, CB * D])

    blank = sem("blank")
    edges_in = sem("edges_in")
    weights_in = sem("weights_in")
    ramp_out = sem("ramp_out")
    consts = sem("consts")
    dve_step = sem("dve_step")
    counted = sem("counted")
    max_known = sem("max_known")
    diag_ready = sem("diag_ready")
    spread_ready = sem("spread_ready")
    record_ready = sem("record_ready")
    record_out = sem("record_out")
    bias_ready = sem("bias_ready")
    bias_out = sem("bias_out")
    bias_in = sem("bias_in")
    f_ready = sem("f_ready")
    f_put_out = sem("f_put_out")
    nb_known = sem("nb_known")
    filled = sem("filled")

    with nc.Block() as block:
        @block.sync
        def _(sp):
            sp.wait_ge(blank, 2)
            for tile, lead, width in ((di, 1, EPR + 3), (si, 0, EPR + 1)):
                t = dst if tile is di else src
                if lead:
                    sp.dma_start(tile[0:1, 1:width], bass.AP(t.tensor, 0, [[EPR, 1], [1, width - 1]])).then_inc(edges_in, 16)
                else:
                    sp.dma_start(tile[0:1, :], bass.AP(t.tensor, 0, [[EPR, 1], [1, width]])).then_inc(edges_in, 16)
                sp.dma_start(tile[1:P - 1, :], bass.AP(t.tensor, EPR - lead, [[EPR, P - 2], [1, width]])).then_inc(edges_in, 16)
                sp.dma_start(tile[P - 1:P, 0:LAST + lead],
                             bass.AP(t.tensor, EPR * (P - 1) - lead, [[EPR, 1], [1, LAST + lead]])).then_inc(edges_in, 16)
            sp.wait_ge(consts, 1)
            sp.dma_start(redirect.rearrange("(p f) o -> p (f o)", p=RP), ramp[:]).then_inc(ramp_out, 16)
            sp.wait_ge(record_ready, 1)
            sp.dma_start(recs.rearrange("(p e) r -> p (e r)", p=P), record[:].rearrange("p e r -> p (e r)")).then_inc(record_out, 16)
            sp.wait_ge(nb_known, 1)
            nb = sp.value_load(v["nb_i"][0:1, 0:1], min_val=1, max_val=MAXB)
            end = sp.value_load(v["nb_i"][0:1, 2:3], min_val=FEWB, max_val=MAXB)
            with sp.If(nb < end):
                with sp.Fori(0, end - nb) as i:
                    at = nc.s_assert_within(HID0 + P + P * CB * (nb + i), 0, HROWS - P * CB,
                                            skip_runtime_bounds_check_because="nb + i is less than MAXB")
                    sp.dma_start(v["h_all"][bass.ds(at, P * CB), :].rearrange("(p r) d -> p (r d)", p=P),
                                 zeros[:]).then_inc(filled, 16)
                    alone_wait(sp, filled, 16 * i + 16, v["mark"])
            sp.wait_ge(record_out, 16)
            sp.wait_ge(ramp_out, 16)

        @block.scalar
        def _(act):
            act.dma_start(bias[0:1, 0:D], v["b1"].rearrange("(o d) -> o d", o=1)).then_inc(weights_in, 16)
            act.dma_start(bias[0:1, D:2 * D], v["b2"].rearrange("(o d) -> o d", o=1)).then_inc(weights_in, 16)
            for n in ("w1l", "w1r", "w2l", "w2r"):
                act.dma_start(W[n + "_sb"][:], v[n].rearrange("(h k) n -> k h n", k=P)).then_inc(weights_in, 16)
            act.wait_ge(bias_ready, 1)
            act.dma_start(bias_parts.rearrange("(o t) n -> o t n", o=1), bpart[:]).then_inc(bias_out, 16)
            act.wait_ge(bias_out, 16)
            for r in range(2):
                act.dma_start(bias3[:, :, r, :], bias_parts.rearrange("t (l n) -> t l n", l=2)).then_inc(bias_in, 16)
            act.wait_ge(bias_in, 32)

        @block.gpsimd
        def _(pool):
            nc.gpsimd.memset(di[:], -1).then_inc(blank, 1)
            nc.gpsimd.memset(si[:], -1).then_inc(blank, 1)
            nc.gpsimd.iota(ramp[:], pattern=[[1, N // RP]], base=0, channel_multiplier=N // RP).then_inc(consts, 1)
            nc.gpsimd.iota(pos1[:], pattern=[[1, EPR]], base=1, channel_multiplier=0,
                           allow_small_or_imprecise_dtypes=True).then_inc(consts, 1)
            nc.gpsimd.iota(v["edge0"][:], pattern=[[1, 1]], base=-1, channel_multiplier=EPR,
                           allow_small_or_imprecise_dtypes=True).then_inc(consts, 1)
            nc.gpsimd.iota(v["slot0"][:], pattern=[[P, CB]], base=HID0 + P, channel_multiplier=1).then_inc(consts, 1)
            nc.gpsimd.iota(f_num[:], pattern=[[1, 1]], base=HID0, channel_multiplier=1).then_inc(consts, 1)
            nc.gpsimd.memset(ident[:], 0.0).then_inc(consts, 1)
            pool.wait_ge(consts, 6)
            nc.gpsimd.affine_select(out=ident[:], in_=ident[:], compare_op=ALU.not_equal, fill=1.0, base=0,
                                    pattern=[[-1, P]], channel_multiplier=1).then_inc(consts, 1)
            nc.gpsimd.memset(onesf[:], 1.0).then_inc(consts, 1)
            nc.gpsimd.memset(ones3[:], 1.0).then_inc(consts, 1)
            pool.wait_ge(consts, 9)
            pool.wait_ge(counted, 1)
            nc.gpsimd.partition_all_reduce(cmax[:], cnt[:], P, bass.bass_isa.ReduceOp.max).then_inc(max_known, 1)
            pool.wait_ge(f_ready, 1)
            pool.wait_ge(ramp_out, 16)
            nc.gpsimd.indirect_dma_start(redirect, bass.IndirectOffsetOnAxis(v["f_put"][:, 0:1], 0), f_num[:], None,
                                         bounds_check=N - 1, oob_is_err=False).then_inc(f_put_out, 16)
            pool.wait_ge(f_put_out, 16)

        @block.tensor
        def _(pe):
            pe.wait_ge(diag_ready, 1)
            nc.tensor.matmul(spread[:], onesf[:], diag[:], start=True, stop=True).then_inc(spread_ready, 1)

        @block.vector
        def _(dve):
            steps = [0]

            def then(ins):
                steps[0] += 1
                ins.then_inc(dve_step, 1)
                dve.wait_ge(dve_step, steps[0])

            ve = nc.vector
            ve.memset(zeros[:], 0.0)
            ve.memset(v["ln_eps"][:], LN_EPS)
            then(ve.memset(v["order"][:], 0.0))
            dve.wait_ge(consts, 9)
            dve.wait_ge(edges_in, 16 * 6)
            ve.tensor_copy(df[:], di[:])
            then(ve.tensor_copy(sf[:], si[:]))
            ve.tensor_tensor(last[:], df[:, 1:EPR + 2], df[:, 2:EPR + 3], ALU.not_equal)
            then(ve.tensor_tensor(lself[:], sf[:], df[:, 1:EPR + 2], ALU.is_equal))
            then(ve.tensor_tensor(lself[:], lself[:], last[:], ALU.mult))
            then(ve.tensor_scalar(tmp[:, 0:EPR], df[:, 1:EPR + 1], 0.0, None, ALU.is_ge))
            then(ve.scalar_tensor_tensor(listed[:], lself[:, 0:EPR], 0.0, tmp[:, 0:EPR], ALU.is_equal, ALU.mult))
            then(ve.tensor_reduce(cnt[:], listed[:], AX.X, ALU.add))
            ve.tensor_tensor(key[:], listed[:], pos1[:], ALU.mult).then_inc(counted, 1)
            ve.tensor_copy(record[:, :, SRC], sf[:, 0:EPR])
            ve.tensor_copy(record[:, :, DST], df[:, 1:EPR + 1])
            then(ve.tensor_tensor(record[:, :, SAME], df[:, 0:EPR], df[:, 1:EPR + 1], ALU.is_equal))
            then(ve.memset(record[:, 0:1, SAME], 0.0))
            then(ve.tensor_scalar(record[:, :, BASE], last[:, 0:EPR], -1.0, 1.0, ALU.mult, ALU.add))
            then(ve.tensor_tensor(tmp[:, 0:EPR], df[:, 1:EPR + 1], df[:, 2:EPR + 2], ALU.is_equal))
            then(ve.tensor_tensor(tmp[:, 0:EPR], tmp[:, 0:EPR], lself[:, 1:EPR + 1], ALU.mult))
            then(ve.tensor_tensor(tmp[:, 0:EPR], tmp[:, 0:EPR], last[:, 0:EPR], ALU.max))
            then(ve.tensor_scalar(over[:], df[:, 1:EPR + 1], df[:, 0:1], None, ALU.is_equal))
            then(ve.tensor_tensor(lself[:, 0:EPR], tmp[:, 0:EPR], listed[:], ALU.mult))
            then(ve.tensor_tensor(record[:, :, ENDF], lself[:, 0:EPR], over[:], ALU.mult))
            then(ve.tensor_tensor(record[:, :, END], lself[:, 0:EPR], record[:, :, ENDF], ALU.subtract))
            then(ve.tensor_reduce(f_has[:], record[:, :, ENDF], AX.X, ALU.add))
            ve.tensor_tensor(over[:], record[:, :, ENDF], record[:, :, BASE], ALU.mult).then_inc(record_ready, 1)
            dve.wait_ge(record_ready, 1)
            then(ve.tensor_reduce(f_tmp[:], over[:], AX.X, ALU.add))
            then(ve.scalar_tensor_tensor(v["f_base"][:], f_tmp[:], 1.0, f_has[:], ALU.add, ALU.subtract))
            then(ve.scalar_tensor_tensor(f_tmp[:], df[:, 0:1], 2.0, f_has[:], ALU.add, ALU.mult))
            then(ve.tensor_scalar(v["f_dst"][:], f_tmp[:], -2.0, None, ALU.add))
            then(ve.tensor_scalar(v["f_get"][:], v["f_dst"][:], 0.0, None, ALU.max))
            then(ve.scalar_tensor_tensor(f_tmp[:], df[:, 0:1], float(-BIG), f_has[:], ALU.add, ALU.mult))
            then(ve.tensor_scalar(v["f_put"][:], f_tmp[:], float(BIG), None, ALU.add))
            ve.tensor_scalar(diag[:], ident[:], v["f_dst"][:, 0:1], None, ALU.mult).then_inc(diag_ready, 1)
            then(ve.scalar_tensor_tensor(l_has[:], tmp[:, EPR - 1:EPR], 0.0, listed[:, EPR - 1:EPR], ALU.is_equal, ALU.mult))
            then(ve.scalar_tensor_tensor(l_dst[:], df[:, EPR:EPR + 1], 3.0, l_has[:], ALU.add, ALU.mult))
            then(ve.tensor_scalar(l_dst[:], l_dst[:], -3.0, None, ALU.add))
            dve.wait_ge(spread_ready, 1)
            ve.tensor_scalar(v["carry"][:], spread[:], l_dst[:, 0:1], None, ALU.is_equal).then_inc(f_ready, 1)
            dve.wait_ge(max_known, 1)
            then(ve.tensor_scalar(nbi[:], cmax[0:1, :], float(CB - 1), None, ALU.add))
            then(ve.tensor_scalar(nbi[:], nbi[:], CB.bit_length() - 1, None, ALU.logical_shift_right))
            then(ve.tensor_scalar(v["nb_i"][:, 0:1], nbi[:], 1.0, None, ALU.max))
            then(ve.tensor_scalar(v["nb_i"][:, 1:2], v["nb_i"][:, 0:1], float((TRI - 2) // WIDE), None, ALU.min))
            then(ve.tensor_scalar(nbi[:], v["nb_i"][:, 0:1], float(FEWB), float(MAXB - FEWB), ALU.is_gt, ALU.mult))
            then(ve.tensor_scalar(v["nb_i"][:, 3:4], v["nb_i"][:, 0:1], -1.0, None, ALU.add))
            ve.tensor_scalar(v["nb_i"][:, 2:3], nbi[:], float(FEWB), None, ALU.add).then_inc(nb_known, 1)
            dve.wait_ge(nb_known, 1)
            dve.wait_ge(weights_in, 16 * 6)
            for n in "12":
                ve.tensor_tensor(W[f"w{n}s_sb"][:], W[f"w{n}l_sb"][:], W[f"w{n}r_sb"][:], ALU.add)
            for t in range(2):
                then(ve.tensor_copy(bpart[:, t, :], bias[:]))
                then(ve.tensor_tensor(bias[:], bias[:], bpart[:, t, :], ALU.subtract))
            ve.tensor_copy(bpart[:, 2, :], bias[:]).then_inc(bias_ready, 1)
            nb = dve.value_load(v["nb_i"][0:1, 0:1], min_val=1, max_val=MAXB)
            base = steps[0]
            with dve.Fori(0, nb) as i:
                ve.max(best[:], key[:]).then_inc(dve_step, 1)
                dve.wait_ge(dve_step, 3 * i + base + 1)
                ve.tensor_copy(v["order"][:, bass.ds(CB * i + 2 * CB, CB)], best[:]).then_inc(dve_step, 1)
                ve.match_replace(key[:], best[:], key[:], 0.0).then_inc(dve_step, 1)
                dve.wait_ge(dve_step, 3 * i + base + 3)


def alone_wait(eng, sem, value, mark):
    eng.wait_ge(sem, value)
    eng.sem_inc(mark)


def column_buffers(nc, stack, v):

    def sb(name, shape, dt=F32):
        return stack.enter_context(nc.sbuf_tensor(name, shape, dt))

    c = {
        "gathered": sb("gathered", [P, CB, D + 1]),
        "own": sb("own", [P, CB, D + 1]),
        "acc": [sb(f"acc{i}", [P, D + 1]) for i in range(2)],
        "over_sum": sb("over_sum", [P, D + 1]),
        "sum": [sb(f"sum{i}", [P, D + 1]) for i in range(2)],
        "inv": sb("inv", [P, 4]),
        "mean": [sb(f"mean{i}", [P, D]) for i in range(2)],
        "colT": [sb(f"colT{i}", [P, 2 * H, P]) for i in range(2)],
        "col_ss": sb("col_ss", [P, 2]),
        "col_rt": sb("col_rt", [P, 2]),
        "col_q": sb("col_q", [P, 2]),
        "col_rn": sb("col_rn", [P, 2]),
        "col_junk": [sb(f"col_junk{i}", [P, D], BF16) for i in range(2)],
        "col_out": sb("col_out", [P, CB, D]),
        "ps_colT": [stack.enter_context(nc.psum_tensor(f"ps_colT{i}", [P, 2 * H, P], F32)) for i in range(2)],
    }
    pair = stack.enter_context(nc.psum_tensor("ps_col", [P, 2, D], F32))
    c["ps_col"] = [pair[:, n, :] for n in range(2)]
    return c


def inverse_norm(nc, dve, root, t, result, stepped, n, made):
    nc.vector.reciprocal(t[:], root[:]).then_inc(stepped, 1)
    dve.wait_ge(stepped, n)
    nc.vector.tensor_scalar(result[:], t[:], 1.0 / NORM_EPS, None, ALU.min).then_inc(made, 1)


def column_steps(nc, v, b, s, wl, wr, layer, one_bank):
    ve, se, te = nc.vector, nc.scalar, nc.tensor
    cur, ident, bias3 = v["cur"], v["ident"], v["bias3"]
    deep = len(b["sum"])

    def run(dve, i, j):
        q, par = CB - 1 - j, j % 2
        dve.wait_ge(s["gathered"][q], 16 * i + 16)
        ve.scalar_tensor_tensor(b["acc"][par][:], b["acc"][1 - par][:], cur[:, 2, q:q + 1], b["gathered"][:, q, :],
                                ALU.mult, ALU.add).then_inc(s["acc_made"], 1)

    def over(j):
        q = CB - 1 - j
        ve.scalar_tensor_tensor(b["over_sum"][:], b["acc"][j % 2][:], cur[:, 4, q:q + 1], b["over_sum"][:],
                                ALU.mult, ALU.add)

    def add_own(dve, i, j, base=None):
        q, buf = CB - 1 - j, j % deep
        dve.wait_ge(s["own"][q], 16 * i + 16)
        dve.wait_ge(s["mean_made"], CB * i + j + 1)
        ve.scalar_tensor_tensor(b["sum"][buf][:], b["own"][:, q, :], cur[:, 3, q:q + 1] if base is None else base,
                                b["acc"][j % 2][:], ALU.mult, ALU.add).then_inc(s["sum_made"], 1)

    def invert(dve, i, j):
        buf = j % deep
        dve.wait_ge(s["sum_made"], CB * i + j + 1)
        ve.reciprocal(b["inv"][:, buf:buf + 1], b["sum"][buf][:, D:D + 1]).then_inc(s["inv_made"], 1)

    def column_sum(dve, i, j):
        run(dve, i, j)
        dve.wait_ge(s["acc_made"], CB * i + j + 1)
        add_own(dve, i, j)
        over(j)
        invert(dve, i, j)

    def pair_sums(dve, i, j):
        run(dve, i, j)
        dve.wait_ge(s["acc_made"], CB * i + j + 1)
        over(j)
        run(dve, i, j + 1)
        add_own(dve, i, j)
        dve.wait_ge(s["acc_made"], CB * i + j + 2)
        over(j + 1)
        add_own(dve, i, j + 1)
        invert(dve, i, j)
        invert(dve, i, j + 1)

    def mean(act, i, j):
        buf = j % deep
        act.wait_ge(s["inv_made"], CB * i + j + 1)
        act.wait_ge(s["transposed"], CB * i + j + CB - deep + 1)
        se.activation(b["mean"][buf][:], b["sum"][buf][:, 0:D], ACT.Copy,
                      scale=b["inv"][:, buf:buf + 1]).then_inc(s["mean_made"], 1)

    def transposes(pe, i, j):
        q, buf = CB - 1 - j, j % deep
        pe.wait_ge(s["mean_made"], CB * i + j + deep + 1)
        for h in range(H):
            te.transpose(b["ps_colT"][buf][:, h, :], b["mean"][buf][:, h * P:(h + 1) * P], ident[:])
        for h in range(H):
            last = te.transpose(b["ps_colT"][buf][:, H + h, :], b["own"][:, q, h * P:(h + 1) * P], ident[:])
        last.then_inc(s["transposed"], 1)

    def copy_transposed(act, i, j):
        buf = j % deep
        act.wait_ge(s["transposed"], CB * i + j + CB + 1)
        act.wait_ge(s["multiplied"], CB * i + j + 1)
        se.copy(b["colT"][buf][:], b["ps_colT"][buf][:]).then_inc(s["copied"], 1)

    def products(pe, i, j):
        buf = j % deep
        pe.wait_ge(s["copied"], CB * i + j + 1)
        pe.wait_ge(s["drained"], CB * i + j + 1 + (one_bank and j % 2 == 0))
        z = b["ps_col"][buf]
        te.matmul(z, v["ones3"][:], bias3[:, layer, 0, :], start=True, stop=False)
        for h in range(2 * H):
            last = te.matmul(z, b["colT"][buf][:, h, :], (wl if h < H else wr)[:, h % H, :],
                             start=False, stop=(h == 2 * H - 1))
        last.then_inc(s["multiplied"], 1)

    def norms(act, i, j, columns=2):
        for n in range(columns):
            buf = (j + n) % deep
            act.wait_ge(s["multiplied"], CB * i + j + n + deep + 1 + (one_bank and n == 0 and columns == 2))
            se.activation(b["col_junk"][buf][:], b["ps_col"][buf], ACT.Square,
                          accum_out=b["col_ss"][:, n:n + 1]).then_inc(s["squared"], 1)
        act.wait_ge(s["squared"], CB * i + j + columns)
        act.wait_ge(s["normed"], CB // 2 * i + j // 2)
        se.activation(b["col_rt"][:], b["col_ss"][:], ACT.Sqrt).then_inc(s["rooted"], 1)

    def inverse_norms(dve, i, j):
        n = CB // 2 * i + j // 2 + 1
        dve.wait_ge(s["rooted"], n)
        inverse_norm(nc, dve, b["col_rt"], b["col_q"], b["col_rn"], s["inverted"], n, s["normed"])

    return dict(column_sum=column_sum, pair_sums=pair_sums, add_own=add_own, invert=invert, mean=mean,
                transposes=transposes, copy_transposed=copy_transposed, products=products, norms=norms,
                inverse_norms=inverse_norms)


def clear_semaphores(nc, s):
    with nc.Block() as block:
        @block.gpsimd
        def _(pool):
            for entry in [s[n] for n in s if n not in ("gathered", "own")]:
                for one in entry if isinstance(entry, list) else [entry]:
                    pool.sem_clear(one)


def column_sems(sem, sems):
    s = {n: sem(f"col_{n}") for n in ("acc_made", "sum_made", "inv_made", "mean_made", "transposed", "copied",
                                        "multiplied", "drained", "squared", "rooted", "inverted", "normed",
                                        "over_added", "carried")}
    for n in ("gathered", "own", "stored", "own_stored"):
        s[n] = sems(f"col_{n}", CB)
    return s


def dense_and_first(nc, stack, v, b):
    sem, sems, x, out, h_all = v["sem"], v["sems"], v["x"], v["out"], v["h_all"]
    W, ident, bias3, ones3 = v["W"], v["ident"], v["bias3"], v["ones3"]
    cur, kept, got, valid = v["cur"], v["kept"], v["got"], v["valid"]
    ve, se, te = nc.vector, nc.scalar, nc.tensor

    def sb(name, shape, dt=F32):
        return stack.enter_context(nc.sbuf_tensor(name, shape, dt))

    def pb(name):
        return stack.enter_context(nc.psum_tensor(name, [P, 2, D], F32))

    xt = [sb(f"x_tile{s}", [P, JT, D]) for s in range(SLOTS)]
    ht = [sb(f"h_tile{s}", [P, JT, D]) for s in range(SLOTS)]
    ot = [sb(f"o_tile{s}", [P, JT, D]) for s in range(SLOTS)]
    xT = sb("xT", [P, 2, H, P])
    hT = sb("hT", [P, 2, H, P])
    ss1, rt1, q1, rn1 = (sb(f"{n}1", [P, 2]) for n in ("ss", "rt", "q", "rn"))
    ss2, q2, rn2 = (sb(f"{n}2", [P, 2]) for n in ("ss", "q", "rn"))
    rt2 = [sb(f"rt2_{n}", [P, 2]) for n in range(2)]
    rt3 = sb("rt3", [P, 2])
    junk1, junk2 = sb("junk1", [P, 2, D], BF16), sb("junk2", [P, 2, 2, D], BF16)
    stats, mv, rstd = sb("stats", [P, 2, 6]), sb("mv", [P, 2, 2, 2]), sb("rstd", [P, 2])
    r_idx, r_got = sb("r_idx", [P, CB], I32), sb("r_got", [P, CB], I32)
    ps_xT, ps_hT, ps_z1 = pb("ps_xT"), pb("ps_hT"), pb("ps_z1")
    ps_z2 = [pb("ps_z2a"), pb("ps_z2b")]

    x_in, h_out, o_out = sems("x_in", SLOTS), sems("h_out", SLOTS), sems("o_out", SLOTS)
    xT_made, xT_copied, z1_made, z1_squared, z1_normed, h_made = map(
        sem, ("xT_made", "xT_copied", "z1_made", "z1_squared", "z1_normed", "h_made"))
    hT_made, hT_copied, z2_made, z2_squared, z2_normed = map(
        sem, ("hT_made", "hT_copied", "z2_made", "z2_squared", "z2_normed"))
    z1_rooted, z1_step, z2_rooted, z2_step = map(sem, ("z1_rooted", "z1_step", "z2_rooted", "z2_step"))
    y_made, y_stats, y_aggr, y_rooted, y_rstd, o_made = map(
        sem, ("y_made", "y_stats", "y_aggr", "y_rooted", "y_rstd", "o_made"))
    ready, e_made, rec_got, cur_made, r_put, own_out = map(
        sem, ("ready", "e_made", "rec_got", "cur_made", "r_put", "own_out_all"))
    own_stored = v["col_sems"]["own_stored"]
    conv_step, key_step = sem("conv_step"), sem("key_step")
    r_asked, r_found, r_kept = sem("r_asked"), sem("r_found"), sem("r_kept")
    s = v["col_sems"]
    col = column_steps(
        nc, v, b, s, W["w1l_sb"], W["w1r_sb"], 0, one_bank=True)

    x_sup = x[0:NSUP * ROWS, :].rearrange("(t p j) d -> t p j d", p=P, j=JT)
    h_sup = h_all[0:NSUP * ROWS, :].rearrange("(t p j) d -> t p j d", p=P, j=JT)
    o_sup = out[0:NSUP * ROWS, :].rearrange("(t p j) d -> t p j d", p=P, j=JT)
    tail = lambda a: a[NSUP * ROWS:N, :].rearrange("(p j) d -> p j d", j=2)
    self_x = v["self_x"]

    def counts(eng):
        nb = eng.value_load(v["nb_i"][0:1, 0:1], min_val=1, max_val=MAXB)
        n1 = eng.value_load(v["nb_i"][0:1, 1:2], min_val=1, max_val=(TRI - 2) // WIDE)
        return nb, n1

    def loops(eng, step, finale=None, block_end=None, alone=None):
        nb, n1 = counts(eng)
        with eng.Fori(0, n1) as i:
            for m in range(WIDE * PAIRS):
                step(WIDE * i + m // PAIRS, m % PAIRS, m, i, m < PAIRS)
                if block_end and m == RECORDS:
                    block_end(i, nb)
        with eng.Fori(WIDE * n1, TRI) as i:
            for k in range(PAIRS):
                step(i, k)
        step(TRI, 0)
        if finale:
            finale()
        if alone:
            with eng.If(nb > n1):
                with eng.Fori(n1, nb) as i:
                    alone(i)
                    if block_end:
                        block_end(i, nb)
        return nb

    def delayed(eng, i, k, by, early, work):
        if k >= by or not early:
            work()
        else:
            with eng.If(i > 0):
                work()

    with nc.Block() as block:
        @block.sync
        def _(sp):
            sp.sem_inc(o_out[SLOTS - 1], 16)
            for t in range(SLOTS):
                sp.dma_start(xt[t][:], x_sup[t]).then_inc(x_in[t], 16)

            def stores(i, t, view_h, view_o, part, refill):
                sp.wait_ge(h_made, PAIRS * i + 2 * t + 2)
                sp.dma_start(view_h, ht[t][part]).then_inc(h_out[t], 16)
                if refill:
                    sp.wait_ge(y_made, PAIRS * i + 2 * t + 4)
                    refill()
                sp.wait_ge(o_made, PAIRS * i + 2 * t + 2)
                sp.dma_start(view_o, ot[t][part]).then_inc(o_out[t], 16)

            whole = (slice(0, P), slice(0, JT), slice(0, D))
            def store_columns(i, j, columns=2):
                for n in range(columns):
                    q = CB - 1 - j - n
                    rows = P * CB * i + P * (1 + q) if columns == 2 else 0
                    sp.wait_ge(s["drained"], CB * i + CB - 1 - q + 3)
                    sp.dma_start(h_all[bass.ds(HID0 + rows, P), :], b["col_out"][:, q, :]).then_inc(s["stored"][q], 16)
                    sp.dma_start(self_x[bass.ds(rows, P), :], b["own"][:, q, 0:D]).then_inc(own_stored[q], 16)

            def whole_slot(i, t):
                n = SLOTS * i + t
                stores(i, t, h_sup[n], o_sup[n], whole,
                       lambda: sp.dma_start(xt[t][:], x_sup[n + SLOTS]).then_inc(x_in[t], 16))

            nb, n1 = counts(sp)
            with sp.Fori(0, n1) as i:
                for m in range(WIDE * SLOTS):
                    whole_slot(WIDE * i + m // SLOTS, m % SLOTS)
                    for step in (2 * m, 2 * m + 1):
                        if step in FINISH:
                            store_columns(i, FINISH[step])
            with sp.Fori(WIDE * n1, TRI - 1) as i:
                for t in range(SLOTS):
                    whole_slot(i, t)
            for t in range(SLOTS):
                n = SLOTS * (TRI - 1) + t
                stores(TRI - 1, t, h_sup[n], o_sup[n], whole, None if t else
                       lambda: sp.dma_start(xt[0][0:TP, 0:2, :], tail(x)).then_inc(x_in[0], 16))
            part = (slice(0, TP), slice(0, 2), slice(0, D))
            sp.wait_ge(h_made, LASTU + 1)
            sp.dma_start(tail(h_all), ht[0][part]).then_inc(h_out[0], 16)
            sp.wait_ge(o_made, LASTU + 1)
            sp.dma_start(tail(out), ot[0][part]).then_inc(o_out[0], 16)
            with sp.If(nb > n1):
                with sp.Fori(n1, nb) as i:
                    for j in range(0, CB, 2):
                        store_columns(i, j)
            store_columns(nb, 0, 1)
            for q in range(CB):
                sp.wait_ge(s["stored"][q], 16 * nb + 16 * (q == CB - 1))
                alone_wait(sp, own_stored[q], 16 * nb + 16 * (q == CB - 1), v["mark"])
            for t in range(SLOTS):
                sp.wait_ge(h_out[t], 16 * (TRI + (t == 0)))
                sp.wait_ge(o_out[t], 16 * (TRI + (t in (0, SLOTS - 1))))

        @block.gpsimd
        def _(pool):
            nb, n1 = counts(pool)

            def gather_records(i):
                alone_wait(pool, e_made, i + 1, v["mark"])
                for q in range(CB):
                    nc.gpsimd.indirect_dma_start(got[:, q, :], None, v["recs"],
                                                 bass.IndirectOffsetOnAxis(v["e_idx"][:, q:q + 1], 0)).then_inc(rec_got, 16)

            gather_records(0)
            with pool.Fori(0, nb) as i:
                pool.wait_ge(cur_made, i + 1)
                for q in reversed(range(CB)):
                    pool.wait_ge(s["transposed"], CB * i + CB - q)
                    alone_wait(pool, own_stored[q], 16 * i, v["mark"])
                    nc.gpsimd.indirect_dma_start(b["gathered"][:, q, 0:D], None, x,
                                                 bass.IndirectOffsetOnAxis(v["src_i"][:, q:q + 1], 0)).then_inc(s["gathered"][q], 16)
                    nc.gpsimd.indirect_dma_start(b["own"][:, q, 0:D], None, x,
                                                 bass.IndirectOffsetOnAxis(v["dst_i"][:, q:q + 1], 0)).then_inc(s["own"][q], 16)
                    nc.gpsimd.indirect_dma_start(v["redirect"], bass.IndirectOffsetOnAxis(v["put_i"][:, q:q + 1], 0),
                                                 v["slot_i"][:, q:q + 1], None,
                                                 bounds_check=N - 1, oob_is_err=False).then_inc(r_put, 16)
                gather_records(i + 1)
            q = CB - 1
            pool.wait_ge(s["transposed"], CB * nb + 1)
            alone_wait(pool, own_stored[q], 16 * nb, v["mark"])
            nc.gpsimd.indirect_dma_start(b["own"][:, q, 0:D], None, x,
                                         bass.IndirectOffsetOnAxis(v["f_get"][:, 0:1], 0)).then_inc(s["own"][q], 16)
            pool.wait_ge(cur_made, nb + 1)
            alone_wait(pool, r_put, 16 * CB * nb, v["mark"])
            with pool.Fori(0, nb) as i:
                nc.gpsimd.tensor_copy(r_idx[:], kept[:, bass.ds(i, 1), 0, :].rearrange("p o c -> p (o c)")).then_inc(r_asked, 1)
                alone_wait(pool, r_asked, i + 1, v["mark"])
                for q in range(CB):
                    nc.gpsimd.indirect_dma_start(r_got[:, q:q + 1], None, v["redirect"],
                                                 bass.IndirectOffsetOnAxis(r_idx[:, q:q + 1], 0)).then_inc(r_found, 16)
                pool.wait_ge(r_found, 16 * CB * i + 16 * CB)
                nc.gpsimd.tensor_copy(v["hrow"][:, bass.ds(i, 1), :].rearrange("p o c -> p (o c)"), r_got[:]).then_inc(r_kept, 1)
                pool.wait_ge(r_kept, i + 1)
            pool.wait_ge(rec_got, 16 * CB * nb + 16 * CB)

        @block.tensor
        def _(pe):
            pe.wait_ge(ready, 1)
            pe.sem_inc(s["transposed"], CB)
            pe.sem_inc(s["multiplied"], 2)

            def transpose_x(i, k):
                t = k // 2
                if k % 2 == 0:
                    pe.wait_ge(x_in[t], 16 * i + 16)
                pe.wait_ge(xT_copied, PAIRS * i + k)
                for r in range(2):
                    for h in range(H):
                        last = te.transpose(ps_xT[:, r, h * P:(h + 1) * P],
                                            xt[t][:, 2 * (k % 2) + r, h * P:(h + 1) * P], ident[:])
                last.then_inc(xT_made, 1)

            def layer(z, aT, w, number, made):
                te.matmul(z[:], ones3[:], bias3[:, number], start=True, stop=False)
                for r in range(2):
                    for h in range(H):
                        last = te.matmul(z[:, r, :], aT[:, r, h, :], w[:, h, :], start=False, stop=(r == 1 and h == H - 1))
                last.then_inc(made, 1)

            def layer_2(i, k, par):
                u = PAIRS * i + k
                pe.wait_ge(hT_copied, u)
                pe.wait_ge(y_made, u)
                layer(ps_z2[par], hT, W["w2s_sb"], 1, z2_made)

            def step(i, k, m=None, block=None, early=False):
                u = PAIRS * i + k
                pe.wait_ge(xT_copied, u + 1)
                layer(ps_z1, xT, W["w1s_sb"], 0, z1_made)
                if k < PAIRS - 1 and not (isinstance(i, int) and i == TRI):
                    transpose_x(i, k + 1)
                elif k == PAIRS - 1:
                    transpose_x(i + 1, 0)
                delayed(pe, i, k, 1, early, lambda: layer_2(i, k, (k + 1) % 2))
                if m in MULTIPLY:
                    for j in (MULTIPLY[m], MULTIPLY[m] + 1):
                        col["products"](pe, block, j)
                if m in TURN:
                    for j in (TURN[m], TURN[m] + 1):
                        col["transposes"](pe, block, j)
                pe.wait_ge(h_made, u + 1)
                for r in range(2):
                    for h in range(H):
                        last = te.transpose(ps_hT[:, r, h * P:(h + 1) * P],
                                            ht[k // 2][:, 2 * (k % 2) + r, h * P:(h + 1) * P], ident[:])
                last.then_inc(hT_made, 1)

            def alone(i):
                for j in range(CB):
                    col["transposes"](pe, i, j)
                    col["products"](pe, i, j)

            transpose_x(0, 0)
            nb = loops(pe, step, lambda: layer_2(TRI, 1, 0), alone=alone)
            over_column(pe, nb, s, b, v, nc, col)

        @block.scalar
        def _(act):
            act.sem_inc(s["mean_made"], 2)
            act.sem_inc(s["drained"], 2)
            act.sem_inc(z2_rooted, 1)
            act.sem_inc(y_rooted, 3)

            def squares_2(i, k, par):
                u = PAIRS * i + k
                act.wait_ge(z2_made, u)
                for r in range(2):
                    last = se.activation(junk2[:, par, r, :], ps_z2[par][:, r, :], ACT.Square,
                                         accum_out=ss2[:, r:r + 1])
                last.then_inc(z2_squared, 1)
                act.wait_ge(z2_squared, u)
                act.wait_ge(z2_normed, u)
                se.activation(rt2[par][:], ss2[:], ACT.Sqrt).then_inc(z2_rooted, 1)

            def deviation(i, k, par):
                act.wait_ge(y_aggr, PAIRS * i + k)
                act.wait_ge(y_rstd, PAIRS * i + k)
                se.activation(rt3[:], mv[:, par, :, 1], ACT.Sqrt, bias=v["ln_eps"][:, 0:1]).then_inc(y_rooted, 1)

            def finish(i, j, columns=2):
                act.wait_ge(s["normed"], CB // 2 * i + j // 2 + 1)
                for n in range(columns):
                    q = CB - 1 - j - n
                    act.wait_ge(s["stored"][q], 16 * i)
                    se.activation(b["col_out"][:, q, :], b["ps_col"][n], ACT.Relu,
                                  scale=b["col_rn"][:, n:n + 1]).then_inc(s["drained"], 1)

            def step(i, k, m=None, block=None, early=False):
                u = PAIRS * i + k
                if m in TURN:
                    for j in (TURN[m], TURN[m] + 1):
                        col["mean"](act, block, j)
                if m in MULTIPLY:
                    for j in (MULTIPLY[m], MULTIPLY[m] + 1):
                        col["copy_transposed"](act, block, j)
                act.wait_ge(z1_made, u + 1)
                for r in range(2):
                    last = se.activation(junk1[:, r, :], ps_z1[:, r, :], ACT.Square, accum_out=ss1[:, r:r + 1])
                last.then_inc(z1_squared, 1)
                act.wait_ge(z1_squared, u + 1)
                se.activation(rt1[:], ss1[:], ACT.Sqrt).then_inc(z1_rooted, 1)
                act.wait_ge(z1_normed, u + 1)
                if k % 2 == 0:
                    act.wait_ge(h_out[k // 2], 16 * i)
                for r in range(2):
                    last = se.activation(ht[k // 2][:, 2 * (k % 2) + r, :], ps_z1[:, r, :], ACT.Relu, scale=rn1[:, r:r + 1])
                last.then_inc(h_made, 1)
                delayed(act, i, k, 1, early, lambda: squares_2(i, k, (k + 1) % 2))
                if m in FINISH:
                    finish(block, FINISH[m])
                act.wait_ge(hT_made, u + 1)
                se.copy(hT[:].rearrange("p r h c -> p (r h c)"), ps_hT[:].rearrange("p r c -> p (r c)")).then_inc(hT_copied, 1)
                delayed(act, i, k, 3, early, lambda: deviation(i, k, (k + 1) % 2))
                if m in MULTIPLY:
                    col["norms"](act, block, MULTIPLY[m])

            def alone(i):
                for pair in range(0, CB, 2):
                    for j in (pair, pair + 1):
                        col["mean"](act, i, j)
                        col["copy_transposed"](act, i, j)
                    col["norms"](act, i, pair)
                    finish(i, pair)

            def finale():
                deviation(TRI, 1, 0)
                squares_2(TRI, 1, 0)
                deviation(TRI, 2, 1)
                deviation(TRI, 3, 0)

            nb = loops(act, step, finale, alone=alone)
            col["mean"](act, nb, 0)
            col["copy_transposed"](act, nb, 0)
            col["norms"](act, nb, 0, 1)
            finish(nb, 0, 1)

        @block.vector
        def _(dve):
            for one in (z2_step, z2_normed, y_made, y_stats, y_aggr):
                dve.sem_inc(one, 2)
            dve.sem_inc(y_rstd, 3)
            ve.memset(b["gathered"][:, :, D:D + 1], 1.0)
            ve.memset(b["own"][:, :, D:D + 1], 1.0)
            ve.memset(b["acc"][1][:], 0.0)
            ve.memset(b["over_sum"][:], 0.0)
            ve.tensor_scalar(v["slot_i"][:], v["slot0"][:], float(-P * CB), None, ALU.add).then_inc(ready, 1)
            dve.wait_ge(ready, 1)
            nb_e = counts(dve)[0]

            def keys(i):
                at = nc.s_assert_within(nb_e - i + 1, 0, MAXB + 1,
                                         skip_runtime_bounds_check_because="i is at most nb + 1")
                key = v["order"][:, bass.ds(CB * at, CB)]
                ve.tensor_scalar(valid[:], key, 0.0, None, ALU.is_gt)
                ve.tensor_scalar(v["e_f"][:], key, v["edge0"][:, 0:1], None, ALU.add).then_inc(key_step, 1)
                dve.wait_ge(key_step, i + 1)
                ve.tensor_scalar(v["e_idx"][:], v["e_f"][:], 0.0, None, ALU.max).then_inc(e_made, 1)

            def records(i):
                dve.wait_ge(rec_got, 16 * CB * i + 16 * CB)
                dve.wait_ge(r_put, 16 * CB * i)
                ve.tensor_copy(cur[:, 0, :], got[:, :, SRC])
                ve.tensor_copy(v["src_i"][:], got[:, :, SRC])
                ve.tensor_copy(v["dst_i"][:], got[:, :, DST])
                ve.tensor_tensor(cur[:, 2, :], got[:, :, SAME], valid[:], ALU.mult)
                ve.tensor_copy(cur[:, 3, :], got[:, :, BASE])
                ve.tensor_tensor(cur[:, 4, :], got[:, :, ENDF], valid[:], ALU.mult)
                ve.tensor_tensor(v["end_f"][:], got[:, :, END], valid[:], ALU.mult).then_inc(conv_step, 1)
                dve.wait_ge(conv_step, 3 * i + 1)
                ve.scalar_tensor_tensor(v["end_f"][:], got[:, :, DST], float(-BIG), v["end_f"][:], ALU.add,
                                        ALU.mult).then_inc(conv_step, 1)
                dve.wait_ge(conv_step, 3 * i + 2)
                ve.tensor_scalar(cur[:, 1, :], v["end_f"][:], float(BIG), None, ALU.add).then_inc(conv_step, 1)
                dve.wait_ge(conv_step, 3 * i + 3)
                ve.tensor_copy(kept[:, bass.ds(i, 1), :, :].rearrange("p o k c -> p (o k) c"), cur[:])
                ve.tensor_scalar(v["slot_i"][:], v["slot_i"][:], float(P * CB), None, ALU.add)
                ve.tensor_copy(v["put_i"][:], cur[:, 1, :]).then_inc(cur_made, 1)
                dve.wait_ge(cur_made, i + 1)

            def slot_of(k, by):
                n = (k - by) % PAIRS
                return n // 2, 2 * (n % 2)

            def residual(i, k, par):
                u = PAIRS * i + k
                t, j = slot_of(k, 2)
                dve.wait_ge(z2_rooted, u)
                inverse_norm(nc, dve, rt2[par], q2, rn2, z2_step, u + 1, z2_normed)
                dve.wait_ge(z2_normed, u + 1)
                if j == 0:
                    dve.wait_ge(o_out[t], 16 * i)
                for r in range(2):
                    last = ve.scalar_tensor_tensor(ot[t][:, j + r, :], ps_z2[par][:, r, :], rn2[:, r:r + 1],
                                                   xt[t][:, j + r, :], ALU.mult, ALU.add)
                last.then_inc(y_made, 1)
                dve.wait_ge(y_made, u + 1)
                for r in range(2):
                    last = ve.bn_stats(stats[:, r, :], ot[t][:, j + r, :])
                last.then_inc(y_stats, 1)
                alone_wait(dve, y_stats, u + 1, v["mark"])
                for r in range(2):
                    last = ve.bn_aggr(mv[:, par, r, :], stats[:, r, :])
                last.then_inc(y_aggr, 1)

            def normalise(i, k, par):
                u = PAIRS * i + k
                t, j = slot_of(k, 3)
                dve.wait_ge(y_rooted, u + 1)
                ve.reciprocal(rstd[:], rt3[:]).then_inc(y_rstd, 1)
                dve.wait_ge(y_rstd, u + 1)
                for r in range(2):
                    last = ve.tensor_scalar(ot[t][:, j + r, :], ot[t][:, j + r, :], mv[:, par, r, 0:1], rstd[:, r:r + 1],
                                            ALU.subtract, ALU.mult)
                last.then_inc(o_made, 1)

            def copy_xT(n):
                dve.wait_ge(xT_made, n + 1)
                ve.tensor_copy(xT[:].rearrange("p r h c -> p (r h c)"), ps_xT[:].rearrange("p r c -> p (r c)")).then_inc(xT_copied, 1)

            def step(i, k, m=None, block=None, early=False):
                u = PAIRS * i + k
                if not isinstance(i, int):
                    copy_xT(u + 1)
                dve.wait_ge(z1_rooted, u + 1)
                inverse_norm(nc, dve, rt1, q1, rn1, z1_step, u + 1, z1_normed)
                if m in FINISH:
                    col["inverse_norms"](dve, block, FINISH[m])
                delayed(dve, i, k, 2, early, lambda: residual(i, k, k % 2))
                if m in SUM_A:
                    col["column_sum"](dve, block, SUM_A[m])
                if m in SUM_B:
                    col["column_sum"](dve, block, SUM_B[m] + 1)
                delayed(dve, i, k, 3, early, lambda: normalise(i, k, (k + 1) % 2))

            def block_end(i, nb):
                records(i + 1)
                keys(i + 2)

            def alone(i):
                for j in range(0, CB, 2):
                    col["pair_sums"](dve, i, j)
                    col["inverse_norms"](dve, i, j)

            keys(0)
            records(0)
            keys(1)
            copy_xT(0)
            def finale():
                residual(TRI, 1, 1)
                normalise(TRI, 1, 0)
                residual(TRI, 2, 0)
                normalise(TRI, 2, 1)
                dve.wait_ge(o_made, LASTU)
                normalise(TRI, 3, 0)

            nb = loops(dve, step, finale, block_end, alone)
            over_total(dve, nb, s, b, v, nc, col)
            col["inverse_norms"](dve, nb, 0)


def over_column(pe, nb, s, b, v, nc, col):
    pe.wait_ge(s["acc_made"], CB * nb)
    pe.wait_ge(s["copied"], CB * nb)
    nc.tensor.matmul(b["ps_colT"][1][:].rearrange("p h c -> p (h c)")[:, 0:D + 1], v["carry"][:], b["acc"][1][:],
                     start=True, stop=True).then_inc(s["carried"], 1)
    col["transposes"](pe, nb, 0)
    col["products"](pe, nb, 0)


def over_total(dve, nb, s, b, v, nc, col):
    dve.wait_ge(s["carried"], 1)
    dve.wait_ge(s["inv_made"], CB * nb)
    nc.vector.tensor_tensor(b["acc"][0][:], b["ps_colT"][1][:].rearrange("p h c -> p (h c)")[:, 0:D + 1],
                            b["over_sum"][:], ALU.add).then_inc(s["over_added"], 1)
    dve.wait_ge(s["over_added"], 1)
    col["add_own"](dve, nb, 0, v["f_base"][:, 0:1])
    col["invert"](dve, nb, 0)


def second_layer(nc, stack, v, b):
    sem, sems, out, h_all, self_x = v["sem"], v["sems"], v["out"], v["h_all"], v["self_x"]
    cur, kept, hrow, W = v["cur"], v["kept"], v["hrow"], v["W"]
    ve, se = nc.vector, nc.scalar

    def sb(name, shape, dt=F32):
        return stack.enter_context(nc.sbuf_tensor(name, shape, dt))

    b = dict(b)
    deep = 4
    for name, shape in (("sum", [P, D + 1]), ("mean", [P, D]), ("colT", [P, 2 * H, P])):
        b[name] = b[name] + [sb(f"{name}_{n}", shape) for n in range(2, deep)]
    b["col_junk"] = b["col_junk"] + [sb(f"col_junk_{n}", [P, D], BF16) for n in range(2, deep)]
    b["ps_colT"] = b["ps_colT"] + [stack.enter_context(nc.psum_tensor(f"ps_colT_{n}", [P, 2 * H, P], F32))
                                   for n in range(2, deep)]
    b["ps_col"] = [b["ps_col"][0]] + [stack.enter_context(nc.psum_tensor(f"ps_col_{n}", [P, 2 * D], F32))[:, 0:D]
                                      for n in range(1, deep)]
    HB = CB // 2
    x_own = sb("x_own", [P, CB, D])
    get_idx = [sb(f"get_idx{h}", [P, HB], I32) for h in range(2)]
    put_idx = [sb(f"put_idx{h}", [P, HB], I32) for h in range(2)]
    stats, mv = sb("stats2", [P, 2, 6]), sb("mv2", [P, 2, 2, 2])
    rt3, rstd, shift = sb("rt4", [P, 2, 2]), sb("rstd2", [P, 2, 2]), sb("shift", [P, 2, 2])
    cur_in, y_stats, y_aggr, y_rooted, y_rstd, y_shift, o_made = map(
        sem, ("cols_cur_in", "cols_stats", "cols_aggr", "cols_rooted", "cols_rstd", "cols_shift", "cols_o_made"))
    ready, get_made, put_made = sem("l2_ready"), sem("get_made"), sem("put_made")
    s = dict(v["col_sems"])
    s["gathered"], s["own"], s["stored"] = sems("gathered_h", CB), s["stored"], sems("scattered", CB)
    x_in = s["own_stored"]
    col = column_steps(nc, v, b, s, W["w2l_sb"], W["w2r_sb"], 1, one_bank=False)

    def count(eng):
        return eng.value_load(v["nb_i"][0:1, 3:4], min_val=0, max_val=MAXB - 1)

    def stage(i, pair, by, work):
        if pair >= by:
            work(i, 2 * (pair - by))
        elif not isinstance(i, int):
            work(i - 1, 2 * (pair - by) + CB)

    def blocks(eng, body, last):
        for pair in range(CB // 2):
            body(0, pair)
        with eng.If(last > 0):
            with eng.Fori(0, last) as i:
                for pair in range(CB // 2):
                    body(i + 1, pair)

    with nc.Block() as block:
        @block.sync
        def _(sp):
            last = count(sp)

            def load_own(i, j, columns=2):
                for q in range(CB - 1 - j, CB - 1 - j - columns, -1):
                    rows = P * CB * i + P * (1 + q) if columns == 2 else 0
                    if not isinstance(i, int):
                        sp.wait_ge(s["transposed"], CB * i + CB - q)
                    sp.dma_start(b["own"][:, q, 0:D], h_all[bass.ds(HID0 + rows, P), :]).then_inc(s["own"][q], 16)

            def load_x(i, j, columns=2):
                for q in range(CB - 1 - j, CB - 1 - j - columns, -1):
                    rows = P * CB * i + P * (1 + q) if columns == 2 else 0
                    if not isinstance(i, int):
                        sp.wait_ge(s["drained"], CB * (i - 1) + CB - q + deep)
                    sp.dma_start(x_own[:, q, :], self_x[bass.ds(rows, P), :]).then_inc(x_in[q], 16)

            def body(i, pair):
                load_own(i, 2 * pair)
                if pair >= 2:
                    load_x(i, 2 * pair - 4)
                elif not isinstance(i, int):
                    load_x(i - 1, 2 * pair + 4)

            blocks(sp, body, last)
            load_x(last, 4)
            load_x(last, 6)
            load_own(last + 1, 0, 1)
            load_x(last + 1, 0, 1)

        @block.gpsimd
        def _(pool):
            last = count(pool)

            def gather(table, i, j):
                if not isinstance(i, int):
                    alone_wait(pool, s["acc_made"], CB * i - CB + j + 2, v["mark"])
                for q in (CB - 1 - j, CB - 2 - j):
                    nc.gpsimd.indirect_dma_start(b["gathered"][:, q, 0:D], None, table,
                                                 bass.IndirectOffsetOnAxis(get_idx[j // HB][:, q % HB:q % HB + 1], 0)).then_inc(s["gathered"][q], 16)

            def scatter(i, j):
                alone_wait(pool, o_made, CB * i + j + 2 + 4, v["mark"])
                for q in (CB - 1 - j, CB - 2 - j):
                    nc.gpsimd.indirect_dma_start(out, bass.IndirectOffsetOnAxis(put_idx[j // HB][:, q % HB:q % HB + 1], 0),
                                                 b["col_out"][:, q, :], None,
                                                 bounds_check=N - 1, oob_is_err=False).then_inc(s["stored"][q], 16)

            def take(tile, source, field, i, lo, made, n, used):
                if not isinstance(i, int):
                    for q in range(lo, lo + HB):
                        pool.wait_ge(used[q], 16 * i)
                view = (source[:, bass.ds(i, 1), lo:lo + HB] if field is None
                        else source[:, bass.ds(i, 1), field, lo:lo + HB])
                nc.gpsimd.tensor_copy(tile[:], view.rearrange("p o c -> p (o c)")).then_inc(made, 1)
                alone_wait(pool, made, 2 * i + n, v["mark"])

            def body(table, i, pair):
                j = 2 * pair
                later = not isinstance(i, int)
                if pair == 0:
                    take(get_idx[0], hrow, None, i, HB, get_made, 1, s["gathered"])
                if pair == 2:
                    take(get_idx[1], hrow, None, i, 0, get_made, 2, s["gathered"])
                    if later:
                        take(put_idx[0], kept, 1, i - 1, HB, put_made, 1, s["stored"])
                gather(table, i, j)
                if later and pair < 2:
                    with pool.If(i > 1):
                        scatter(i - 2, HB + j)
                elif later:
                    scatter(i - 1, j - HB)
                if later and pair == 3:
                    take(put_idx[1], kept, 1, i - 1, 0, put_made, 2, s["stored"])

            with pool.If(last < FEWB):
                blocks(pool, lambda i, pair: body(h_all[0:N + P * (1 + CB * FEWB), :], i, pair), last)
            with pool.Else():
                blocks(pool, lambda i, pair: body(h_all, i, pair), last)
            with pool.If(last > 0):
                scatter(last - 1, HB)
                scatter(last - 1, HB + 2)
            take(put_idx[0], kept, 1, last, HB, put_made, 1, s["stored"])
            scatter(last, 0)
            scatter(last, 2)
            take(put_idx[1], kept, 1, last, 0, put_made, 2, s["stored"])
            scatter(last, HB)
            scatter(last, HB + 2)
            q = CB - 1
            alone_wait(pool, o_made, CB * (last + 1) + 1 + 4, v["mark"])
            nc.gpsimd.indirect_dma_start(out, bass.IndirectOffsetOnAxis(v["f_put"][:, 0:1], 0), b["col_out"][:, q, :], None,
                                         bounds_check=N - 1, oob_is_err=False).then_inc(s["stored"][q], 16)
            for q in range(CB):
                pool.wait_ge(s["stored"][q], 16 * (last + 1) + 16 * (q == CB - 1))

        @block.tensor
        def _(pe):
            pe.sem_inc(s["transposed"], CB)
            pe.sem_inc(s["multiplied"], deep)
            last = count(pe)

            def pair_of(name):
                def work(i, j):
                    col[name](pe, i, j)
                    col[name](pe, i, j + 1)
                return work

            def body(i, pair):
                stage(i, pair, 1, pair_of("transposes"))
                stage(i, pair, 2, pair_of("products"))

            blocks(pe, body, last)
            stage(last + 1, 0, 1, pair_of("transposes"))
            stage(last + 1, 0, 2, pair_of("products"))
            stage(last + 1, 1, 2, pair_of("products"))
            over_column(pe, last + 1, s, b, v, nc, col)

        @block.scalar
        def _(act):
            act.sem_inc(s["mean_made"], deep)
            act.sem_inc(o_made, 4)
            last = count(act)

            def pair_of(name):
                def work(i, j):
                    col[name](act, i, j)
                    col[name](act, i, j + 1)
                return work

            def deviation(i, j):
                n, par = CB // 2 * i + j // 2, j // 2 % 2
                act.wait_ge(y_aggr, n + 1)
                se.activation(rt3[:, par, :], mv[:, par, :, 1], ACT.Sqrt, bias=v["ln_eps"][:, 0:1]).then_inc(y_rooted, 1)

            def normalise(i, j, columns=2):
                n, par = CB // 2 * i + j // 2, j // 2 % 2
                act.wait_ge(y_shift, n + 1)
                for n in range(columns):
                    q = CB - 1 - j - n
                    se.activation(b["col_out"][:, q, :], b["col_out"][:, q, :], ACT.Identity,
                                  scale=rstd[:, par, n:n + 1], bias=shift[:, par, n:n + 1]).then_inc(o_made, 1)

            def norms(i, j):
                col["norms"](act, i, j)

            def body(i, pair):
                stage(i, pair, 4, deviation)
                stage(i, pair, 1, pair_of("mean"))
                stage(i, pair, 2, pair_of("copy_transposed"))
                stage(i, pair, 3, norms)
                stage(i, pair, 4, normalise)

            blocks(act, body, last)
            deviation(last, 0)
            stage(last + 1, 0, 1, pair_of("mean"))
            for pair in range(4):
                if pair:
                    deviation(last, 2 * pair)
                if pair < 2:
                    stage(last + 1, pair, 2, pair_of("copy_transposed"))
                if pair < 3:
                    stage(last + 1, pair, 3, norms)
                normalise(last, 2 * pair)
            col["mean"](act, last + 1, 0)
            col["copy_transposed"](act, last + 1, 0)
            col["norms"](act, last + 1, 0, 1)
            deviation(last + 1, 0)
            normalise(last + 1, 0, 1)

        @block.vector
        def _(dve):
            dve.sem_inc(s["drained"], deep)
            ve.memset(b["acc"][1][:], 0.0)
            ve.memset(b["over_sum"][:], 0.0).then_inc(ready, 1)
            dve.wait_ge(ready, 1)
            last = count(dve)

            def output(i, j, columns=2):
                number, par = CB // 2 * i + j // 2, j // 2 % 2
                col["inverse_norms"](dve, i, j)
                dve.wait_ge(s["normed"], number + 1)
                for n in range(columns):
                    q = CB - 1 - j - n
                    dve.wait_ge(x_in[q], 16 * i + 16)
                    dve.wait_ge(s["stored"][q], 16 * i)
                    ve.scalar_tensor_tensor(b["col_out"][:, q, :], b["ps_col"][(j + n) % deep], b["col_rn"][:, n:n + 1],
                                            x_own[:, q, :], ALU.mult, ALU.add).then_inc(s["drained"], 1)
                for n in range(columns):
                    dve.wait_ge(s["drained"], 2 * number + n + deep + 1)
                    ve.bn_stats(stats[:, n, :], b["col_out"][:, CB - 1 - j - n, :]).then_inc(y_stats, 1)
                for n in range(columns):
                    alone_wait(dve, y_stats, 2 * number + n + 1, v["mark"])
                    last = ve.bn_aggr(mv[:, par, n, :], stats[:, n, :])
                last.then_inc(y_aggr, 1)

            def factors(i, j):
                n, par = CB // 2 * i + j // 2, j // 2 % 2
                dve.wait_ge(y_rooted, n + 1)
                dve.wait_ge(o_made, 2 * n + 2)
                ve.reciprocal(rstd[:, par, :], rt3[:, par, :]).then_inc(y_rstd, 1)
                dve.wait_ge(y_rstd, n + 1)
                ve.scalar_tensor_tensor(shift[:, par, :], mv[:, par, :, 0], -1.0, rstd[:, par, :],
                                        ALU.mult, ALU.mult).then_inc(y_shift, 1)

            def sums(i, j):
                col["pair_sums"](dve, i, j)

            def body(i, pair):
                if pair == 0:
                    ve.tensor_copy(cur[:], kept[:, bass.ds(i, 1), :, :].rearrange("p o k c -> p (o k) c")).then_inc(cur_in, 1)
                    dve.wait_ge(cur_in, i + 1)
                stage(i, pair, 0, sums)
                stage(i, pair, 4, factors)
                stage(i, pair, 3, output)

            blocks(dve, body, last)
            for pair in range(4):
                factors(last, 2 * pair)
                if pair < 3:
                    stage(last + 1, pair, 3, output)
            over_total(dve, last + 1, s, b, v, nc, col)
            output(last + 1, 0, 1)
            factors(last + 1, 0)


def kernel(x, src, dst, L0_gnn_W1l, L0_gnn_b1l, L0_gnn_W1r, L0_gnn_W2l, L0_gnn_b2l, L0_gnn_W2r):
    import concourse.bacc as bacc
    from concourse.bass_utils import run_bass_kernel_spmd

    arrays = {
        "x": x, "src": src, "dst": dst,
        "w1l": np.asarray(L0_gnn_W1l).T, "b1": L0_gnn_b1l, "w1r": np.asarray(L0_gnn_W1r).T,
        "w2l": np.asarray(L0_gnn_W2l).T, "b2": L0_gnn_b2l, "w2r": np.asarray(L0_gnn_W2r).T,
    }
    arrays = {name: np.ascontiguousarray(a) for name, a in arrays.items()}
    nc = bacc.Bacc("TRN2", target_bir_lowering=False, num_devices=1)
    args = [nc.dram_tensor(name, a.shape, mybir.dt.from_np(a.dtype), kind="ExternalInput").ap()
            for name, a in arrays.items()]
    out = nc.dram_tensor("out", [N, D], F32, kind="ExternalOutput").ap()
    build_gnn(nc, *args, out)
    result = run_bass_kernel_spmd(nc, [arrays], core_ids=[0])
    return result.results[0]["out"]
```

```python
import numpy as np
import concourse.bass as bass
from concourse import mybir
from contextlib import ExitStack

F32 = mybir.dt.float32
BF16 = mybir.dt.bfloat16
I32 = mybir.dt.int32
ALU = mybir.AluOpType
ACT = mybir.ActivationFunctionType
AX = mybir.AxisListType

P = 128
N = 100000
E = 125000
D = 256
H = D // P
EPR = -(-E // P)
LAST = E - EPR * (P - 1)
CB = 8
MAXB = -(-EPR // CB)
REC = 6
SRC, DST, SAME, BASE, END, ENDF = range(REC)
KEPT = 5
BIG = 1 << 22

ROWS = 512
JT = ROWS // P
SLOTS = 3
TRI = N // ROWS // SLOTS
NSUP = TRI * SLOTS
PAIRS = 2 * SLOTS
TAIL = N - NSUP * ROWS
TP = TAIL // 2
LASTU = NSUP * 2
HID0 = N
HROWS = N + P * (1 + CB * MAXB)
FEWB = 32
RP = 80
LN_EPS = 1e-5
NORM_EPS = 1e-12
PASSES = PAIRS // 2
SUM = {0: (0, 1), 1: (2,), 2: (3,), 3: (4, 5), 4: (6,), 5: (7,)}
TURN = {1: 0, 3: 2, 4: 4, 6: 6}
MULTIPLY = {2: 0, 4: 2, 5: 4, 7: 6}
FINISH = {3: 0, 5: 2, 6: 4, 8: 6}
RECORDS = 2


def build_gnn(nc, x, src, dst, w1l, b1, w1r, w2l, b2, w2r, out):
    ctx = ExitStack()

    def sb(name, shape, dt=F32):
        return ctx.enter_context(nc.sbuf_tensor(name, shape, dt))

    def pb(name, shape):
        return ctx.enter_context(nc.psum_tensor(name, shape, F32))

    def sem(name):
        return ctx.enter_context(nc.semaphore(name))

    def sems(name, n):
        return [sem(f"{name}{i}") for i in range(n)]

    with ctx:
        recs = nc.dram_tensor("edge_records", [P * EPR, REC], F32).ap()
        redirect = nc.dram_tensor("redirect", [N, 1], I32).ap()
        h_all = nc.dram_tensor("h_all", [HROWS, D], F32).ap()
        self_x = nc.dram_tensor("self_x", [P * (1 + CB * MAXB), D], F32).ap()
        bias_parts = nc.dram_tensor("bias_parts", [3, 2 * D], BF16).ap()

        mark = sem("mark")
        ident = sb("ident", [P, P])
        ones3 = sb("ones3", [3, P], BF16)
        ln_eps = sb("ln_eps", [P, 1])
        bias3 = sb("bias3", [3, 2, 2, D], BF16)
        W = {n: sb(n, [P, H, D]) for n in ("w1l_sb", "w1r_sb", "w1s_sb", "w2l_sb", "w2r_sb", "w2s_sb")}
        nb_i = sb("nb_i", [1, 7], I32)
        order = sb("order", [P, (MAXB + 2 + PASSES) * CB])
        key = sb("key", [P, EPR])
        best = sb("best", [P, CB])
        edge0 = sb("edge0", [P, 1])
        slot0 = sb("slot0", [P, CB], I32)
        f_dst = sb("f_dst", [P, 1])
        f_base = sb("f_base", [P, 1])
        f_get = sb("f_get", [P, 1], I32)
        f_put = sb("f_put", [P, 1], I32)
        carry = sb("carry", [P, P])
        kept = sb("kept", [P, MAXB + 2, KEPT, CB])
        hrow = sb("hrow", [P, MAXB + 2, CB], I32)
        e_idx = sb("e_idx", [P, CB], I32)
        got = sb("got", [P, CB, REC])
        valid = sb("valid", [P, CB])
        cur = sb("cur", [P, KEPT, CB])
        src_i = sb("src_i", [P, CB], I32)
        dst_i = sb("dst_i", [P, CB], I32)
        put_i = sb("put_i", [P, CB], I32)
        slot_i = sb("slot_i", [P, CB], I32)
        e_f = sb("e_f", [P, CB])
        end_f = sb("end_f", [P, CB])

        with ExitStack() as first:
            prepare_edges(nc, first, locals())
        with ExitStack() as second:
            columns = column_buffers(nc, second, locals())
            col_sems = column_sems(sem, sems)
            with ExitStack() as sweep:
                dense_and_first(nc, sweep, locals(), columns)
            clear_semaphores(nc, col_sems)
            second_layer(nc, second, locals(), columns)
    return nc


def prepare_edges(nc, first, v):
    src, dst = v["src"], v["dst"]
    recs, redirect, bias_parts = v["recs"], v["redirect"], v["bias_parts"]
    ident, ones3, bias3, W = v["ident"], v["ones3"], v["bias3"], v["W"]

    def sb(name, shape, dt=F32):
        return first.enter_context(nc.sbuf_tensor(name, shape, dt))

    sem = v["sem"]
    di = sb("dst_ints", [P, EPR + 3], I32)
    si = sb("src_ints", [P, EPR + 1], I32)
    df = sb("dst_f", [P, EPR + 3])
    sf = sb("src_f", [P, EPR + 1])
    last = sb("last", [P, EPR + 1])
    lself = sb("lself", [P, EPR + 1])
    tmp = sb("tmp", [P, EPR + 1])
    listed = sb("listed", [P, EPR])
    over = sb("over", [P, EPR])
    record = sb("record", [P, EPR, REC])
    pos1 = sb("pos1", [P, EPR])
    key = v["key"]
    cnt = sb("cnt", [P, 1])
    cmax = sb("cmax", [P, 1])
    nbi = sb("nbi", [1, 1], I32)
    f_has = sb("f_has", [P, 1])
    f_tmp = sb("f_tmp", [P, 1])
    l_has = sb("l_has", [P, 1])
    l_dst = sb("l_dst", [P, 1])
    diag = sb("diag", [P, P])
    onesf = sb("onesf", [P, P])
    ramp = sb("ramp", [RP, N // RP], I32)
    bias = sb("bias", [1, 2 * D])
    bpart = sb("bpart", [1, 3, 2 * D], BF16)
    spread = first.enter_context(nc.psum_tensor("spread", [P, P], F32))
    f_num = sb("f_num", [P, 1], I32)
    zeros = sb("zeros", [P, CB * D])

    blank = sem("blank")
    edges_in = sem("edges_in")
    weights_in = sem("weights_in")
    ramp_out = sem("ramp_out")
    consts = sem("consts")
    dve_step = sem("dve_step")
    counted = sem("counted")
    max_known = sem("max_known")
    diag_ready = sem("diag_ready")
    spread_ready = sem("spread_ready")
    record_ready = sem("record_ready")
    record_out = sem("record_out")
    bias_ready = sem("bias_ready")
    bias_out = sem("bias_out")
    bias_in = sem("bias_in")
    f_ready = sem("f_ready")
    f_put_out = sem("f_put_out")
    nb_known = sem("nb_known")
    filled = sem("filled")

    with nc.Block() as block:
        @block.sync
        def _(sp):
            sp.wait_ge(blank, 2)
            for tile, lead, width in ((di, 1, EPR + 3), (si, 0, EPR + 1)):
                t = dst if tile is di else src
                if lead:
                    sp.dma_start(tile[0:1, 1:width], bass.AP(t.tensor, 0, [[EPR, 1], [1, width - 1]])).then_inc(edges_in, 16)
                else:
                    sp.dma_start(tile[0:1, :], bass.AP(t.tensor, 0, [[EPR, 1], [1, width]])).then_inc(edges_in, 16)
                sp.dma_start(tile[1:P - 1, :], bass.AP(t.tensor, EPR - lead, [[EPR, P - 2], [1, width]])).then_inc(edges_in, 16)
                sp.dma_start(tile[P - 1:P, 0:LAST + lead],
                             bass.AP(t.tensor, EPR * (P - 1) - lead, [[EPR, 1], [1, LAST + lead]])).then_inc(edges_in, 16)
            sp.wait_ge(consts, 1)
            sp.dma_start(redirect.rearrange("(p f) o -> p (f o)", p=RP), ramp[:]).then_inc(ramp_out, 16)
            sp.wait_ge(record_ready, 1)
            sp.dma_start(recs.rearrange("(p e) r -> p (e r)", p=P), record[:].rearrange("p e r -> p (e r)")).then_inc(record_out, 16)
            sp.wait_ge(nb_known, 1)
            nb = sp.value_load(v["nb_i"][0:1, 0:1], min_val=1, max_val=MAXB)
            end = sp.value_load(v["nb_i"][0:1, 2:3], min_val=FEWB, max_val=MAXB)
            with sp.If(nb < end):
                with sp.Fori(0, end - nb) as i:
                    at = nc.s_assert_within(HID0 + P + P * CB * (nb + i), 0, HROWS - P * CB,
                                            skip_runtime_bounds_check_because="nb + i is less than MAXB")
                    sp.dma_start(v["h_all"][bass.ds(at, P * CB), :].rearrange("(p r) d -> p (r d)", p=P),
                                 zeros[:]).then_inc(filled, 16)
                    alone_wait(sp, filled, 16 * i + 16, v["mark"])
            sp.wait_ge(record_out, 16)
            sp.wait_ge(ramp_out, 16)

        @block.scalar
        def _(act):
            act.dma_start(bias[0:1, 0:D], v["b1"].rearrange("(o d) -> o d", o=1)).then_inc(weights_in, 16)
            act.dma_start(bias[0:1, D:2 * D], v["b2"].rearrange("(o d) -> o d", o=1)).then_inc(weights_in, 16)
            for n in ("w1l", "w1r", "w2l", "w2r"):
                act.dma_start(W[n + "_sb"][:], v[n].rearrange("(h k) n -> k h n", k=P)).then_inc(weights_in, 16)
            act.wait_ge(bias_ready, 1)
            act.dma_start(bias_parts.rearrange("(o t) n -> o t n", o=1), bpart[:]).then_inc(bias_out, 16)
            act.wait_ge(bias_out, 16)
            for r in range(2):
                act.dma_start(bias3[:, :, r, :], bias_parts.rearrange("t (l n) -> t l n", l=2)).then_inc(bias_in, 16)
            act.wait_ge(bias_in, 32)

        @block.gpsimd
        def _(pool):
            nc.gpsimd.memset(di[:], -1).then_inc(blank, 1)
            nc.gpsimd.memset(si[:], -1).then_inc(blank, 1)
            nc.gpsimd.iota(ramp[:], pattern=[[1, N // RP]], base=0, channel_multiplier=N // RP).then_inc(consts, 1)
            nc.gpsimd.iota(pos1[:], pattern=[[1, EPR]], base=1, channel_multiplier=0,
                           allow_small_or_imprecise_dtypes=True).then_inc(consts, 1)
            nc.gpsimd.iota(v["edge0"][:], pattern=[[1, 1]], base=-1, channel_multiplier=EPR,
                           allow_small_or_imprecise_dtypes=True).then_inc(consts, 1)
            nc.gpsimd.iota(v["slot0"][:], pattern=[[P, CB]], base=HID0 + P, channel_multiplier=1).then_inc(consts, 1)
            nc.gpsimd.iota(f_num[:], pattern=[[1, 1]], base=HID0, channel_multiplier=1).then_inc(consts, 1)
            nc.gpsimd.memset(ident[:], 0.0).then_inc(consts, 1)
            pool.wait_ge(consts, 6)
            nc.gpsimd.affine_select(out=ident[:], in_=ident[:], compare_op=ALU.not_equal, fill=1.0, base=0,
                                    pattern=[[-1, P]], channel_multiplier=1).then_inc(consts, 1)
            nc.gpsimd.memset(onesf[:], 1.0).then_inc(consts, 1)
            nc.gpsimd.memset(ones3[:], 1.0).then_inc(consts, 1)
            pool.wait_ge(consts, 9)
            pool.wait_ge(counted, 1)
            nc.gpsimd.partition_all_reduce(cmax[:], cnt[:], P, bass.bass_isa.ReduceOp.max).then_inc(max_known, 1)
            pool.wait_ge(f_ready, 1)
            pool.wait_ge(ramp_out, 16)
            nc.gpsimd.indirect_dma_start(redirect, bass.IndirectOffsetOnAxis(v["f_put"][:, 0:1], 0), f_num[:], None,
                                         bounds_check=N - 1, oob_is_err=False).then_inc(f_put_out, 16)
            pool.wait_ge(f_put_out, 16)

        @block.tensor
        def _(pe):
            pe.wait_ge(diag_ready, 1)
            nc.tensor.matmul(spread[:], onesf[:], diag[:], start=True, stop=True).then_inc(spread_ready, 1)

        @block.vector
        def _(dve):
            steps = [0]

            def then(ins):
                steps[0] += 1
                ins.then_inc(dve_step, 1)
                dve.wait_ge(dve_step, steps[0])

            ve = nc.vector
            ve.memset(zeros[:], 0.0)
            ve.memset(v["ln_eps"][:], LN_EPS)
            then(ve.memset(v["order"][:], 0.0))
            dve.wait_ge(consts, 9)
            dve.wait_ge(edges_in, 16 * 6)
            ve.tensor_copy(df[:], di[:])
            then(ve.tensor_copy(sf[:], si[:]))
            ve.tensor_tensor(last[:], df[:, 1:EPR + 2], df[:, 2:EPR + 3], ALU.not_equal)
            then(ve.tensor_tensor(lself[:], sf[:], df[:, 1:EPR + 2], ALU.is_equal))
            then(ve.tensor_tensor(lself[:], lself[:], last[:], ALU.mult))
            then(ve.tensor_scalar(tmp[:, 0:EPR], df[:, 1:EPR + 1], 0.0, None, ALU.is_ge))
            then(ve.scalar_tensor_tensor(listed[:], lself[:, 0:EPR], 0.0, tmp[:, 0:EPR], ALU.is_equal, ALU.mult))
            then(ve.tensor_reduce(cnt[:], listed[:], AX.X, ALU.add))
            ve.tensor_tensor(key[:], listed[:], pos1[:], ALU.mult).then_inc(counted, 1)
            ve.tensor_copy(record[:, :, SRC], sf[:, 0:EPR])
            ve.tensor_copy(record[:, :, DST], df[:, 1:EPR + 1])
            then(ve.tensor_tensor(record[:, :, SAME], df[:, 0:EPR], df[:, 1:EPR + 1], ALU.is_equal))
            then(ve.memset(record[:, 0:1, SAME], 0.0))
            then(ve.tensor_scalar(record[:, :, BASE], last[:, 0:EPR], -1.0, 1.0, ALU.mult, ALU.add))
            then(ve.tensor_tensor(tmp[:, 0:EPR], df[:, 1:EPR + 1], df[:, 2:EPR + 2], ALU.is_equal))
            then(ve.tensor_tensor(tmp[:, 0:EPR], tmp[:, 0:EPR], lself[:, 1:EPR + 1], ALU.mult))
            then(ve.tensor_tensor(tmp[:, 0:EPR], tmp[:, 0:EPR], last[:, 0:EPR], ALU.max))
            then(ve.tensor_scalar(over[:], df[:, 1:EPR + 1], df[:, 0:1], None, ALU.is_equal))
            then(ve.tensor_tensor(lself[:, 0:EPR], tmp[:, 0:EPR], listed[:], ALU.mult))
            then(ve.tensor_tensor(record[:, :, ENDF], lself[:, 0:EPR], over[:], ALU.mult))
            then(ve.tensor_tensor(record[:, :, END], lself[:, 0:EPR], record[:, :, ENDF], ALU.subtract))
            then(ve.tensor_reduce(f_has[:], record[:, :, ENDF], AX.X, ALU.add))
            ve.tensor_tensor(over[:], record[:, :, ENDF], record[:, :, BASE], ALU.mult).then_inc(record_ready, 1)
            dve.wait_ge(record_ready, 1)
            then(ve.tensor_reduce(f_tmp[:], over[:], AX.X, ALU.add))
            then(ve.scalar_tensor_tensor(v["f_base"][:], f_tmp[:], 1.0, f_has[:], ALU.add, ALU.subtract))
            then(ve.scalar_tensor_tensor(f_tmp[:], df[:, 0:1], 2.0, f_has[:], ALU.add, ALU.mult))
            then(ve.tensor_scalar(v["f_dst"][:], f_tmp[:], -2.0, None, ALU.add))
            then(ve.tensor_scalar(v["f_get"][:], v["f_dst"][:], 0.0, None, ALU.max))
            then(ve.scalar_tensor_tensor(f_tmp[:], df[:, 0:1], float(-BIG), f_has[:], ALU.add, ALU.mult))
            then(ve.tensor_scalar(v["f_put"][:], f_tmp[:], float(BIG), None, ALU.add))
            ve.tensor_scalar(diag[:], ident[:], v["f_dst"][:, 0:1], None, ALU.mult).then_inc(diag_ready, 1)
            then(ve.scalar_tensor_tensor(l_has[:], tmp[:, EPR - 1:EPR], 0.0, listed[:, EPR - 1:EPR], ALU.is_equal, ALU.mult))
            then(ve.scalar_tensor_tensor(l_dst[:], df[:, EPR:EPR + 1], 3.0, l_has[:], ALU.add, ALU.mult))
            then(ve.tensor_scalar(l_dst[:], l_dst[:], -3.0, None, ALU.add))
            dve.wait_ge(spread_ready, 1)
            ve.tensor_scalar(v["carry"][:], spread[:], l_dst[:, 0:1], None, ALU.is_equal).then_inc(f_ready, 1)
            dve.wait_ge(max_known, 1)
            then(ve.tensor_scalar(nbi[:], cmax[0:1, :], float(CB - 1), None, ALU.add))
            then(ve.tensor_scalar(nbi[:], nbi[:], CB.bit_length() - 1, None, ALU.logical_shift_right))
            then(ve.tensor_scalar(v["nb_i"][:, 0:1], nbi[:], 1.0, None, ALU.max))
            then(ve.tensor_scalar(nbi[:], v["nb_i"][:, 0:1], float(PASSES - 1), float(-(-(1 << 16) // PASSES)), ALU.add, ALU.mult))
            then(ve.tensor_scalar(v["nb_i"][:, 4:5], nbi[:], 16, None, ALU.logical_shift_right))
            then(ve.tensor_scalar(v["nb_i"][:, 6:7], v["nb_i"][:, 4:5], -1.0, None, ALU.add))
            then(ve.tensor_scalar(nbi[:], v["nb_i"][:, 4:5], -1.0, float(TRI - 3), ALU.mult, ALU.add))
            then(ve.tensor_tensor(v["nb_i"][:, 1:2], nbi[:], v["nb_i"][:, 0:1], ALU.min))
            then(ve.tensor_scalar(v["nb_i"][:, 5:6], v["nb_i"][:, 1:2], -1.0, None, ALU.add))
            then(ve.tensor_scalar(nbi[:], v["nb_i"][:, 0:1], float(FEWB), float(MAXB - FEWB), ALU.is_gt, ALU.mult))
            then(ve.tensor_scalar(v["nb_i"][:, 3:4], v["nb_i"][:, 0:1], -1.0, None, ALU.add))
            ve.tensor_scalar(v["nb_i"][:, 2:3], nbi[:], float(FEWB), None, ALU.add).then_inc(nb_known, 1)
            dve.wait_ge(nb_known, 1)
            dve.wait_ge(weights_in, 16 * 6)
            for n in "12":
                ve.tensor_tensor(W[f"w{n}s_sb"][:], W[f"w{n}l_sb"][:], W[f"w{n}r_sb"][:], ALU.add)
            for t in range(2):
                then(ve.tensor_copy(bpart[:, t, :], bias[:]))
                then(ve.tensor_tensor(bias[:], bias[:], bpart[:, t, :], ALU.subtract))
            ve.tensor_copy(bpart[:, 2, :], bias[:]).then_inc(bias_ready, 1)


def alone_wait(eng, sem, value, mark):
    eng.wait_ge(sem, value)
    eng.sem_inc(mark)


def column_buffers(nc, stack, v):

    def sb(name, shape, dt=F32):
        return stack.enter_context(nc.sbuf_tensor(name, shape, dt))

    c = {
        "gathered": sb("gathered", [P, CB, D + 1]),
        "own": sb("own", [P, CB, D + 1]),
        "acc": [sb(f"acc{i}", [P, D + 1]) for i in range(2)],
        "over_sum": sb("over_sum", [P, D + 1]),
        "sum": [sb(f"sum{i}", [P, D + 1]) for i in range(2)],
        "inv": sb("inv", [P, 4]),
        "mean": [sb(f"mean{i}", [P, D]) for i in range(2)],
        "colT": [sb(f"colT{i}", [P, 2 * H, P]) for i in range(2)],
        "col_ss": sb("col_ss", [P, 2]),
        "col_rt": sb("col_rt", [P, 2]),
        "col_q": sb("col_q", [P, 2]),
        "col_rn": sb("col_rn", [P, 2]),
        "col_junk": [sb(f"col_junk{i}", [P, D], BF16) for i in range(2)],
        "col_out": sb("col_out", [P, CB, D]),
        "ps_colT": [stack.enter_context(nc.psum_tensor(f"ps_colT{i}", [P, 2 * H, P], F32)) for i in range(2)],
    }
    pair = stack.enter_context(nc.psum_tensor("ps_col", [P, 2, D], F32))
    c["ps_col"] = [pair[:, n, :] for n in range(2)]
    return c


def inverse_norm(nc, dve, root, t, result, stepped, n, made, parts=(0, 1)):
    if 0 in parts:
        nc.vector.reciprocal(t[:], root[:]).then_inc(stepped, 1)
    if 1 in parts:
        dve.wait_ge(stepped, n)
        nc.vector.tensor_scalar(result[:], t[:], 1.0 / NORM_EPS, None, ALU.min).then_inc(made, 1)


def column_steps(nc, v, b, s, wl, wr, layer, one_bank):
    ve, se, te = nc.vector, nc.scalar, nc.tensor
    cur, ident, bias3 = v["cur"], v["ident"], v["bias3"]
    deep = len(b["sum"])

    def run(dve, i, j):
        q, par = CB - 1 - j, j % 2
        dve.wait_ge(s["gathered"][q], 16 * i + 16)
        ve.scalar_tensor_tensor(b["acc"][par][:], b["acc"][1 - par][:], cur[:, 2, q:q + 1], b["gathered"][:, q, :],
                                ALU.mult, ALU.add).then_inc(s["acc_made"], 1)

    def over(j):
        q = CB - 1 - j
        ve.scalar_tensor_tensor(b["over_sum"][:], b["acc"][j % 2][:], cur[:, 4, q:q + 1], b["over_sum"][:],
                                ALU.mult, ALU.add)

    def add_own(dve, i, j, base=None):
        q, buf = CB - 1 - j, j % deep
        dve.wait_ge(s["own"][q], 16 * i + 16)
        dve.wait_ge(s["mean_made"], CB * i + j + 1)
        ve.scalar_tensor_tensor(b["sum"][buf][:], b["own"][:, q, :], cur[:, 3, q:q + 1] if base is None else base,
                                b["acc"][j % 2][:], ALU.mult, ALU.add).then_inc(s["sum_made"], 1)

    def invert(dve, i, j):
        buf = j % deep
        dve.wait_ge(s["sum_made"], CB * i + j + 1)
        ve.reciprocal(b["inv"][:, buf:buf + 1], b["sum"][buf][:, D:D + 1]).then_inc(s["inv_made"], 1)

    def column_sum(dve, i, j):
        run(dve, i, j)
        dve.wait_ge(s["acc_made"], CB * i + j + 1)
        add_own(dve, i, j)
        over(j)
        invert(dve, i, j)

    def pair_sums(dve, i, j):
        run(dve, i, j)
        dve.wait_ge(s["acc_made"], CB * i + j + 1)
        over(j)
        run(dve, i, j + 1)
        add_own(dve, i, j)
        dve.wait_ge(s["acc_made"], CB * i + j + 2)
        over(j + 1)
        add_own(dve, i, j + 1)

    def pair_inverts(dve, i, j):
        invert(dve, i, j)
        invert(dve, i, j + 1)

    def mean(act, i, j):
        buf = j % deep
        act.wait_ge(s["inv_made"], CB * i + j + 1)
        act.wait_ge(s["transposed"], CB * i + j + CB - deep + 1)
        se.activation(b["mean"][buf][:], b["sum"][buf][:, 0:D], ACT.Copy,
                      scale=b["inv"][:, buf:buf + 1]).then_inc(s["mean_made"], 1)

    def transposes(pe, i, j):
        q, buf = CB - 1 - j, j % deep
        pe.wait_ge(s["mean_made"], CB * i + j + deep + 1)
        for h in range(H):
            te.transpose(b["ps_colT"][buf][:, h, :], b["mean"][buf][:, h * P:(h + 1) * P], ident[:])
        for h in range(H):
            last = te.transpose(b["ps_colT"][buf][:, H + h, :], b["own"][:, q, h * P:(h + 1) * P], ident[:])
        last.then_inc(s["transposed"], 1)

    def copy_transposed(act, i, j):
        buf = j % deep
        act.wait_ge(s["transposed"], CB * i + j + CB + 1)
        act.wait_ge(s["multiplied"], CB * i + j + 1)
        se.copy(b["colT"][buf][:], b["ps_colT"][buf][:]).then_inc(s["copied"], 1)

    def products(pe, i, j):
        buf = j % deep
        pe.wait_ge(s["copied"], CB * i + j + 1)
        pe.wait_ge(s["drained"], CB * i + j + 1 + (one_bank and j % 2 == 0))
        z = b["ps_col"][buf]
        te.matmul(z, v["ones3"][:], bias3[:, layer, 0, :], start=True, stop=False)
        for h in range(2 * H):
            last = te.matmul(z, b["colT"][buf][:, h, :], (wl if h < H else wr)[:, h % H, :],
                             start=False, stop=(h == 2 * H - 1))
        last.then_inc(s["multiplied"], 1)

    def norms(act, i, j, columns=2):
        for n in range(columns):
            buf = (j + n) % deep
            act.wait_ge(s["multiplied"], CB * i + j + n + deep + 1 + (one_bank and n == 0 and columns == 2))
            se.activation(b["col_junk"][buf][:], b["ps_col"][buf], ACT.Square,
                          accum_out=b["col_ss"][:, n:n + 1]).then_inc(s["squared"], 1)
        act.wait_ge(s["squared"], CB * i + j + columns)
        act.wait_ge(s["normed"], CB // 2 * i + j // 2)
        se.activation(b["col_rt"][:], b["col_ss"][:], ACT.Sqrt).then_inc(s["rooted"], 1)

    def inverse_norms(dve, i, j, parts=(0, 1)):
        n = CB // 2 * i + j // 2 + 1
        if 0 in parts:
            dve.wait_ge(s["rooted"], n)
        inverse_norm(nc, dve, b["col_rt"], b["col_q"], b["col_rn"], s["inverted"], n, s["normed"], parts)

    return dict(column_sum=column_sum, pair_sums=pair_sums, pair_inverts=pair_inverts, add_own=add_own, invert=invert,
                mean=mean,
                transposes=transposes, copy_transposed=copy_transposed, products=products, norms=norms,
                inverse_norms=inverse_norms)


def clear_semaphores(nc, s):
    with nc.Block() as block:
        @block.gpsimd
        def _(pool):
            for entry in [s[n] for n in s if n not in ("gathered", "own")]:
                for one in entry if isinstance(entry, list) else [entry]:
                    pool.sem_clear(one)


def column_sems(sem, sems):
    s = {n: sem(f"col_{n}") for n in ("acc_made", "sum_made", "inv_made", "mean_made", "transposed", "copied",
                                        "multiplied", "drained", "squared", "rooted", "inverted", "normed",
                                        "over_added", "carried")}
    for n in ("gathered", "own", "stored", "own_stored"):
        s[n] = sems(f"col_{n}", CB)
    return s


def dense_and_first(nc, stack, v, b):
    sem, sems, x, out, h_all = v["sem"], v["sems"], v["x"], v["out"], v["h_all"]
    W, ident, bias3, ones3 = v["W"], v["ident"], v["bias3"], v["ones3"]
    cur, kept, got, valid = v["cur"], v["kept"], v["got"], v["valid"]
    ve, se, te = nc.vector, nc.scalar, nc.tensor

    def sb(name, shape, dt=F32):
        return stack.enter_context(nc.sbuf_tensor(name, shape, dt))

    def pb(name):
        return stack.enter_context(nc.psum_tensor(name, [P, 2, D], F32))

    xt = [sb(f"x_tile{s}", [P, JT, D]) for s in range(SLOTS)]
    ht = [sb(f"h_tile{s}", [P, JT, D]) for s in range(SLOTS)]
    ot = [sb(f"o_tile{s}", [P, JT, D]) for s in range(SLOTS)]
    xT = sb("xT", [P, 2, H, P])
    hT = sb("hT", [P, 2, H, P])
    ss1, rt1, q1, rn1 = (sb(f"{n}1", [P, 2]) for n in ("ss", "rt", "q", "rn"))
    ss2, q2, rn2 = (sb(f"{n}2", [P, 2]) for n in ("ss", "q", "rn"))
    rt2 = [sb(f"rt2_{n}", [P, 2]) for n in range(2)]
    rt3 = sb("rt3", [P, 2])
    junk1, junk2 = sb("junk1", [P, 2, D], BF16), sb("junk2", [P, 2, 2, D], BF16)
    stats, mv, rstd = sb("stats", [P, 2, 6]), sb("mv", [P, 2, 2, 2]), sb("rstd", [P, 2])
    r_idx, r_got = sb("r_idx", [P, CB], I32), sb("r_got", [P, CB], I32)
    ps_xT, ps_hT, ps_z1 = pb("ps_xT"), pb("ps_hT"), pb("ps_z1")
    ps_z2 = [pb("ps_z2a"), pb("ps_z2b")]

    x_in, h_out, o_out = sems("x_in", SLOTS), sems("h_out", SLOTS), sems("o_out", SLOTS)
    xT_made, xT_copied, z1_made, z1_squared, z1_normed, h_made = map(
        sem, ("xT_made", "xT_copied", "z1_made", "z1_squared", "z1_normed", "h_made"))
    hT_made, hT_copied, z2_made, z2_squared, z2_normed = map(
        sem, ("hT_made", "hT_copied", "z2_made", "z2_squared", "z2_normed"))
    z1_rooted, z1_step, z2_rooted, z2_step = map(sem, ("z1_rooted", "z1_step", "z2_rooted", "z2_step"))
    y_made, y_stats, y_aggr, y_rooted, y_rstd, o_made = map(
        sem, ("y_made", "y_stats", "y_aggr", "y_rooted", "y_rstd", "o_made"))
    ready, e_made, rec_got, cur_made, r_put = map(
        sem, ("ready", "e_made", "rec_got", "cur_made", "r_put"))
    own_stored = v["col_sems"]["own_stored"]
    conv_step, key_step, pass_step = sem("conv_step"), sem("key_step"), sem("pass_step")
    indices = sem("indices")
    coming = sb("coming", [P, KEPT, CB])
    r_asked, r_found, r_kept = sem("r_asked"), sem("r_found"), sem("r_kept")
    s = v["col_sems"]
    col = column_steps(
        nc, v, b, s, W["w1l_sb"], W["w1r_sb"], 0, one_bank=True)

    x_sup = x[0:NSUP * ROWS, :].rearrange("(t p j) d -> t p j d", p=P, j=JT)
    h_sup = h_all[0:NSUP * ROWS, :].rearrange("(t p j) d -> t p j d", p=P, j=JT)
    o_sup = out[0:NSUP * ROWS, :].rearrange("(t p j) d -> t p j d", p=P, j=JT)
    tail = lambda a: a[NSUP * ROWS:N, :].rearrange("(p j) d -> p j d", j=2)
    self_x = v["self_x"]

    def counts(eng):
        nb = eng.value_load(v["nb_i"][0:1, 0:1], min_val=1, max_val=MAXB)
        n1 = eng.value_load(v["nb_i"][0:1, 5:6], min_val=0, max_val=TRI - 5) + 1
        np = eng.value_load(v["nb_i"][0:1, 6:7], min_val=0, max_val=-(-MAXB // PASSES) - 1) + 1
        return nb, n1, np

    def loops(eng, step, finale=None, passes=None, between=None, block_end=None, alone=None):
        nb, n1, np = counts(eng)

        def with_passes(i, early):
            for k in range(PAIRS):
                step(i, k, early=early)
                if passes:
                    passes(i, k)

        with_passes(0, True)
        with eng.If(np > 1):
            with eng.Fori(0, np - 1) as i:
                with_passes(i + 1, False)
        for k in range(PAIRS):
            step(np, k)
            if between:
                between(k)
        def with_columns(i, now, before):
            for k in range(PAIRS):
                step(i, k, now, before)
                if block_end and now is not None:
                    block_end(k, now, nb)

        with_columns(np + 1, 0, None)
        with eng.If(n1 > 1):
            with eng.Fori(0, n1 - 1) as i:
                with_columns(np + 2 + i, i + 1, i)
        with_columns(np + 1 + n1, None, n1 - 1)
        with eng.Fori(np + 2 + n1, TRI) as i:
            for k in range(PAIRS):
                step(i, k)
        step(TRI, 0)
        if finale:
            finale()
        if alone:
            with eng.If(nb > n1):
                with eng.Fori(n1, nb) as i:
                    alone(i)
                    if block_end:
                        for k in range(PAIRS):
                            block_end(k, i, nb)
        return nb

    def beside(stage, k, now, before):
        found = []
        if now is not None and k in stage:
            found.append((now, stage[k]))
        if before is not None and k + PAIRS in stage:
            found.append((before, stage[k + PAIRS]))
        return found

    def delayed(eng, i, k, by, early, work):
        if k >= by or not early:
            work()

    def is_tail(i):
        return isinstance(i, int) and i == TRI

    with nc.Block() as block:
        @block.sync
        def _(sp):
            sp.sem_inc(o_out[SLOTS - 1], 16)
            for t in range(SLOTS):
                sp.dma_start(xt[t][:], x_sup[t]).then_inc(x_in[t], 16)

            def stores(i, t, view_h, view_o, part, refill):
                sp.wait_ge(h_made, PAIRS * i + 2 * t + 2)
                sp.dma_start(view_h, ht[t][part]).then_inc(h_out[t], 16)
                if refill:
                    sp.wait_ge(y_made, PAIRS * i + 2 * t + 4)
                    refill()
                sp.wait_ge(o_made, PAIRS * i + 2 * t + 2)
                sp.dma_start(view_o, ot[t][part]).then_inc(o_out[t], 16)

            whole = (slice(0, P), slice(0, JT), slice(0, D))
            def store_columns(i, j, columns=2):
                for n in range(columns):
                    q = CB - 1 - j - n
                    rows = P * CB * i + P * (1 + q) if columns == 2 else 0
                    sp.wait_ge(s["drained"], CB * i + CB - 1 - q + 3)
                    sp.dma_start(h_all[bass.ds(HID0 + rows, P), :], b["col_out"][:, q, :]).then_inc(s["stored"][q], 16)

            def whole_slot(i, t):
                n = nc.s_assert_within(SLOTS * i + t, 0, NSUP - SLOTS - 1,
                                       skip_runtime_bounds_check_because="i is less than TRI - 1")
                stores(i, t, h_sup[n], o_sup[n], whole,
                       lambda: sp.dma_start(xt[t][:], x_sup[n + SLOTS]).then_inc(x_in[t], 16))

            nb, n1, np = counts(sp)
            def with_columns(i, now, before):
                for t in range(SLOTS):
                    whole_slot(i, t)
                    for k in (2 * t, 2 * t + 1):
                        for block, j in beside(FINISH, k, now, before):
                            store_columns(block, j)

            with sp.Fori(0, np + 1) as i:
                with_columns(i, None, None)
            with_columns(np + 1, 0, None)
            with sp.If(n1 > 1):
                with sp.Fori(0, n1 - 1) as i:
                    with_columns(np + 2 + i, i + 1, i)
            with_columns(np + 1 + n1, None, n1 - 1)
            with sp.If(np + 2 + n1 < TRI - 1):
                with sp.Fori(np + 2 + n1, TRI - 1) as i:
                    with_columns(i, None, None)
            for t in range(SLOTS):
                n = SLOTS * (TRI - 1) + t
                stores(TRI - 1, t, h_sup[n], o_sup[n], whole, None if t else
                       lambda: sp.dma_start(xt[0][0:TP, 0:2, :], tail(x)).then_inc(x_in[0], 16))
            part = (slice(0, TP), slice(0, 2), slice(0, D))
            sp.wait_ge(h_made, LASTU + 1)
            sp.dma_start(tail(h_all), ht[0][part]).then_inc(h_out[0], 16)
            sp.wait_ge(o_made, LASTU + 1)
            sp.dma_start(tail(out), ot[0][part]).then_inc(o_out[0], 16)
            with sp.If(nb > n1):
                with sp.Fori(n1, nb) as i:
                    for j in range(0, CB, 2):
                        store_columns(i, j)
            store_columns(nb, 0, 1)
            for q in range(CB):
                alone_wait(sp, s["stored"][q], 16 * nb + 16 * (q == CB - 1), v["mark"])
            for t in range(SLOTS):
                sp.wait_ge(h_out[t], 16 * (TRI + (t == 0)))
                sp.wait_ge(o_out[t], 16 * (TRI + (t in (0, SLOTS - 1))))

        @block.gpsimd
        def _(pool):
            nb = counts(pool)[0]

            def gather_records(i):
                alone_wait(pool, e_made, i + 1, v["mark"])
                for q in range(CB):
                    nc.gpsimd.indirect_dma_start(got[:, q, :], None, v["recs"],
                                                 bass.IndirectOffsetOnAxis(v["e_idx"][:, q:q + 1], 0)).then_inc(rec_got, 16)

            gather_records(0)
            with pool.Fori(0, nb) as i:
                pool.wait_ge(indices, i + 1)
                gather_records(i + 1)
                for q in reversed(range(CB)):
                    pool.wait_ge(s["transposed"], CB * i + CB - q)
                    alone_wait(pool, own_stored[q], 16 * i, v["mark"])
                    nc.gpsimd.indirect_dma_start(b["gathered"][:, q, 0:D], None, x,
                                                 bass.IndirectOffsetOnAxis(v["src_i"][:, q:q + 1], 0)).then_inc(s["gathered"][q], 16)
                    nc.gpsimd.indirect_dma_start(b["own"][:, q, 0:D], None, x,
                                                 bass.IndirectOffsetOnAxis(v["dst_i"][:, q:q + 1], 0)).then_inc(s["own"][q], 16)
                    nc.gpsimd.indirect_dma_start(v["redirect"], bass.IndirectOffsetOnAxis(v["put_i"][:, q:q + 1], 0),
                                                 v["slot_i"][:, q:q + 1], None,
                                                 bounds_check=N - 1, oob_is_err=False).then_inc(r_put, 16)
            q = CB - 1
            pool.wait_ge(s["transposed"], CB * nb + 1)
            alone_wait(pool, own_stored[q], 16 * nb, v["mark"])
            nc.gpsimd.indirect_dma_start(b["own"][:, q, 0:D], None, x,
                                         bass.IndirectOffsetOnAxis(v["f_get"][:, 0:1], 0)).then_inc(s["own"][q], 16)
            pool.wait_ge(indices, nb + 1)
            alone_wait(pool, r_put, 16 * CB * nb, v["mark"])
            with pool.Fori(0, nb) as i:
                nc.gpsimd.tensor_copy(r_idx[:], kept[:, bass.ds(i, 1), 0, :].rearrange("p o c -> p (o c)")).then_inc(r_asked, 1)
                alone_wait(pool, r_asked, i + 1, v["mark"])
                for q in range(CB):
                    nc.gpsimd.indirect_dma_start(r_got[:, q:q + 1], None, v["redirect"],
                                                 bass.IndirectOffsetOnAxis(r_idx[:, q:q + 1], 0)).then_inc(r_found, 16)
                pool.wait_ge(r_found, 16 * CB * i + 16 * CB)
                nc.gpsimd.tensor_copy(v["hrow"][:, bass.ds(i, 1), :].rearrange("p o c -> p (o c)"), r_got[:]).then_inc(r_kept, 1)
                pool.wait_ge(r_kept, i + 1)
            pool.wait_ge(rec_got, 16 * CB * nb + 16 * CB)

        @block.tensor
        def _(pe):
            pe.wait_ge(ready, 1)
            pe.sem_inc(s["transposed"], CB)
            pe.sem_inc(s["multiplied"], 2)

            def transpose_x(i, k):
                t = k // 2
                if k % 2 == 0:
                    pe.wait_ge(x_in[t], 16 * i + 16)
                pe.wait_ge(xT_copied, PAIRS * i + k)
                for r in range(2):
                    for h in range(H):
                        last = te.transpose(ps_xT[:, r, h * P:(h + 1) * P],
                                            xt[t][:, 2 * (k % 2) + r, h * P:(h + 1) * P], ident[:])
                last.then_inc(xT_made, 1)

            def layer(z, aT, w, number, made):
                te.matmul(z[:], ones3[:], bias3[:, number], start=True, stop=False)
                for r in range(2):
                    for h in range(H):
                        last = te.matmul(z[:, r, :], aT[:, r, h, :], w[:, h, :], start=False, stop=(r == 1 and h == H - 1))
                last.then_inc(made, 1)

            def layer_2(i, k, par):
                u = PAIRS * i + k
                pe.wait_ge(hT_copied, u)
                pe.wait_ge(y_made, u)
                layer(ps_z2[par], hT, W["w2s_sb"], 1, z2_made)

            def step(i, k, now=None, before=None, early=False):
                u = PAIRS * i + k
                pe.wait_ge(xT_copied, u + 1)
                layer(ps_z1, xT, W["w1s_sb"], 0, z1_made)
                if k < PAIRS - 1 and not is_tail(i):
                    transpose_x(i, k + 1)
                elif k == PAIRS - 1:
                    transpose_x(i + 1, 0)
                delayed(pe, i, k, 1, early, lambda: layer_2(i, k, (k + 1) % 2))
                for block, j in beside(MULTIPLY, k, now, before):
                    col["products"](pe, block, j)
                    col["products"](pe, block, j + 1)
                for block, j in beside(TURN, k, now, before):
                    col["transposes"](pe, block, j)
                    col["transposes"](pe, block, j + 1)
                pe.wait_ge(h_made, u + 1)
                for r in range(2):
                    for h in range(H):
                        last = te.transpose(ps_hT[:, r, h * P:(h + 1) * P],
                                            ht[k // 2][:, 2 * (k % 2) + r, h * P:(h + 1) * P], ident[:])
                last.then_inc(hT_made, 1)

            def alone(i):
                for j in range(CB):
                    col["transposes"](pe, i, j)
                    col["products"](pe, i, j)

            transpose_x(0, 0)
            nb = loops(pe, step, lambda: layer_2(TRI, 1, 0), alone=alone)
            over_column(pe, nb, s, b, v, nc, col)

        @block.scalar
        def _(act):
            act.sem_inc(s["mean_made"], 2)
            act.sem_inc(s["drained"], 2)
            act.sem_inc(z2_rooted, 1)
            act.sem_inc(y_rooted, 3)

            def squares_2(i, k, par):
                u = PAIRS * i + k
                act.wait_ge(z2_made, u)
                for r in range(2):
                    last = se.activation(junk2[:, par, r, :], ps_z2[par][:, r, :], ACT.Square,
                                         accum_out=ss2[:, r:r + 1])
                last.then_inc(z2_squared, 1)
                act.wait_ge(z2_squared, u)
                act.wait_ge(z2_normed, u)
                se.activation(rt2[par][:], ss2[:], ACT.Sqrt).then_inc(z2_rooted, 1)

            def deviation(i, k, par):
                act.wait_ge(y_aggr, PAIRS * i + k)
                act.wait_ge(y_rstd, PAIRS * i + k)
                se.activation(rt3[:], mv[:, par, :, 1], ACT.Sqrt, bias=v["ln_eps"][:, 0:1]).then_inc(y_rooted, 1)

            def store_own(i, j, columns=2):
                for q in range(CB - 1 - j, CB - 1 - j - columns, -1):
                    rows = P * CB * i + P * (1 + q) if columns == 2 else 0
                    act.wait_ge(s["own"][q], 16 * i + 16)
                    act.dma_start(self_x[bass.ds(rows, P), :], b["own"][:, q, 0:D]).then_inc(own_stored[q], 16)

            def finish(i, j, columns=2):
                act.wait_ge(s["normed"], CB // 2 * i + j // 2 + 1)
                for n in range(columns):
                    q = CB - 1 - j - n
                    act.wait_ge(s["stored"][q], 16 * i)
                    se.activation(b["col_out"][:, q, :], b["ps_col"][n], ACT.Relu,
                                  scale=b["col_rn"][:, n:n + 1]).then_inc(s["drained"], 1)

            def step(i, k, now=None, before=None, early=False):
                u = PAIRS * i + k
                for block, j in beside(MULTIPLY, k, now, before):
                    col["copy_transposed"](act, block, j)
                    col["copy_transposed"](act, block, j + 1)
                for block, j in beside(TURN, k, now, before):
                    col["mean"](act, block, j)
                    col["mean"](act, block, j + 1)
                    store_own(block, j)
                act.wait_ge(z1_made, u + 1)
                for r in range(2):
                    last = se.activation(junk1[:, r, :], ps_z1[:, r, :], ACT.Square, accum_out=ss1[:, r:r + 1])
                last.then_inc(z1_squared, 1)
                act.wait_ge(z1_squared, u + 1)
                se.activation(rt1[:], ss1[:], ACT.Sqrt).then_inc(z1_rooted, 1)
                for block, j in beside(FINISH, k, now, before):
                    finish(block, j)
                act.wait_ge(z1_normed, u + 1)
                if k % 2 == 0:
                    act.wait_ge(h_out[k // 2], 16 * i)
                for r in range(2):
                    last = se.activation(ht[k // 2][:, 2 * (k % 2) + r, :], ps_z1[:, r, :], ACT.Relu, scale=rn1[:, r:r + 1])
                last.then_inc(h_made, 1)
                delayed(act, i, k, 1, early, lambda: squares_2(i, k, (k + 1) % 2))
                act.wait_ge(hT_made, u + 1)
                se.copy(hT[:].rearrange("p r h c -> p (r h c)"), ps_hT[:].rearrange("p r c -> p (r c)")).then_inc(hT_copied, 1)
                delayed(act, i, k, 3, early, lambda: deviation(i, k, (k + 1) % 2))
                for block, j in beside(MULTIPLY, k, now, before):
                    col["norms"](act, block, j)

            def alone(i):
                for pair in range(0, CB, 2):
                    for j in (pair, pair + 1):
                        col["mean"](act, i, j)
                        col["copy_transposed"](act, i, j)
                    store_own(i, pair)
                    col["norms"](act, i, pair)
                    finish(i, pair)

            def finale():
                deviation(TRI, 1, 0)
                squares_2(TRI, 1, 0)
                deviation(TRI, 2, 1)
                deviation(TRI, 3, 0)

            nb = loops(act, step, finale, alone=alone)
            col["mean"](act, nb, 0)
            col["copy_transposed"](act, nb, 0)
            store_own(nb, 0, 1)
            col["norms"](act, nb, 0, 1)
            finish(nb, 0, 1)
            for q in range(CB):
                alone_wait(act, own_stored[q], 16 * nb + 16 * (q == CB - 1), v["mark"])

        @block.vector
        def _(dve):
            for one in (z2_step, z2_normed, y_made, y_stats, y_aggr):
                dve.sem_inc(one, 2)
            dve.sem_inc(y_rstd, 3)
            ve.memset(b["gathered"][:, :, D:D + 1], 1.0)
            ve.memset(b["own"][:, :, D:D + 1], 1.0)
            ve.memset(b["acc"][1][:], 0.0)
            ve.memset(b["over_sum"][:], 0.0)
            ve.tensor_scalar(v["slot_i"][:], v["slot0"][:], float(-P * CB), None, ALU.add).then_inc(ready, 1)
            dve.wait_ge(ready, 1)
            nb_e = counts(dve)[0]

            def keys(i):
                at = nc.s_assert_within(nb_e - i + 1, 0, MAXB + 1,
                                         skip_runtime_bounds_check_because="i is at most nb + 1")
                key = v["order"][:, bass.ds(CB * at, CB)]
                ve.tensor_scalar(valid[:], key, 0.0, None, ALU.is_gt)
                ve.tensor_scalar(v["e_f"][:], key, v["edge0"][:, 0:1], None, ALU.add).then_inc(key_step, 1)
                dve.wait_ge(key_step, i + 1)
                ve.tensor_scalar(v["e_idx"][:], v["e_f"][:], 0.0, None, ALU.max).then_inc(e_made, 1)

            def records(i):
                dve.wait_ge(rec_got, 16 * CB * i + 16 * CB)
                dve.wait_ge(r_put, 16 * CB * i)
                dve.wait_ge(s["gathered"][0], 16 * i)
                dve.wait_ge(s["own"][0], 16 * i)
                ve.tensor_copy(coming[:, 0, :], got[:, :, SRC])
                ve.tensor_copy(v["src_i"][:], got[:, :, SRC])
                ve.tensor_copy(v["dst_i"][:], got[:, :, DST])
                ve.tensor_tensor(coming[:, 2, :], got[:, :, SAME], valid[:], ALU.mult)
                ve.tensor_copy(coming[:, 3, :], got[:, :, BASE])
                ve.tensor_tensor(coming[:, 4, :], got[:, :, ENDF], valid[:], ALU.mult)
                ve.tensor_tensor(v["end_f"][:], got[:, :, END], valid[:], ALU.mult).then_inc(conv_step, 1)
                dve.wait_ge(conv_step, 3 * i + 1)
                ve.scalar_tensor_tensor(v["end_f"][:], got[:, :, DST], float(-BIG), v["end_f"][:], ALU.add,
                                        ALU.mult).then_inc(conv_step, 1)
                dve.wait_ge(conv_step, 3 * i + 2)
                ve.tensor_scalar(coming[:, 1, :], v["end_f"][:], float(BIG), None, ALU.add).then_inc(conv_step, 1)
                dve.wait_ge(conv_step, 3 * i + 3)
                ve.tensor_copy(kept[:, bass.ds(i, 1), :, :].rearrange("p o k c -> p (o k) c"), coming[:])
                ve.tensor_scalar(v["slot_i"][:], v["slot_i"][:], float(P * CB), None, ALU.add)
                ve.tensor_copy(v["put_i"][:], coming[:, 1, :]).then_inc(indices, 1)
                dve.wait_ge(indices, i + 1)

            def next_block(i):
                ve.tensor_copy(cur[:], coming[:]).then_inc(cur_made, 1)
                dve.wait_ge(cur_made, i + 1)

            def slot_of(k, by):
                n = (k - by) % PAIRS
                return n // 2, 2 * (n % 2)

            def residual(i, k, par):
                u = PAIRS * i + k
                t, j = slot_of(k, 2)
                dve.wait_ge(z2_rooted, u)
                inverse_norm(nc, dve, rt2[par], q2, rn2, z2_step, u + 1, z2_normed)
                dve.wait_ge(z2_normed, u + 1)
                if j == 0:
                    dve.wait_ge(o_out[t], 16 * i)
                for r in range(2):
                    last = ve.scalar_tensor_tensor(ot[t][:, j + r, :], ps_z2[par][:, r, :], rn2[:, r:r + 1],
                                                   xt[t][:, j + r, :], ALU.mult, ALU.add)
                last.then_inc(y_made, 1)
                dve.wait_ge(y_made, u + 1)
                for r in range(2):
                    last = ve.bn_stats(stats[:, r, :], ot[t][:, j + r, :])
                last.then_inc(y_stats, 1)
                alone_wait(dve, y_stats, u + 1, v["mark"])
                for r in range(2):
                    last = ve.bn_aggr(mv[:, par, r, :], stats[:, r, :])
                last.then_inc(y_aggr, 1)

            def normalise(i, k, par):
                u = PAIRS * i + k
                t, j = slot_of(k, 3)
                dve.wait_ge(y_rooted, u + 1)
                ve.reciprocal(rstd[:], rt3[:]).then_inc(y_rstd, 1)
                dve.wait_ge(y_rstd, u + 1)
                for r in range(2):
                    last = ve.tensor_scalar(ot[t][:, j + r, :], ot[t][:, j + r, :], mv[:, par, r, 0:1], rstd[:, r:r + 1],
                                            ALU.subtract, ALU.mult)
                last.then_inc(o_made, 1)

            def copy_xT(n):
                dve.wait_ge(xT_made, n + 1)
                ve.tensor_copy(xT[:].rearrange("p r h c -> p (r h c)"), ps_xT[:].rearrange("p r c -> p (r c)")).then_inc(xT_copied, 1)

            def step(i, k, now=None, before=None, early=False):
                u = PAIRS * i + k
                for block, j in beside(FINISH, k, now, before):
                    col["inverse_norms"](dve, block, j)
                if not is_tail(i):
                    copy_xT(u + 1)
                dve.wait_ge(z1_rooted, u + 1)
                inverse_norm(nc, dve, rt1, q1, rn1, z1_step, u + 1, z1_normed)
                delayed(dve, i, k, 2, early, lambda: residual(i, k, k % 2))
                for block, columns in beside(SUM, k, now, None):
                    for j in columns:
                        col["column_sum"](dve, block, j)
                delayed(dve, i, k, 3, early, lambda: normalise(i, k, (k + 1) % 2))

            def block_end(k, i, nb):
                if k == RECORDS:
                    records(i + 1)
                    keys(i + 2)
                if k == PAIRS - 1:
                    next_block(i + 1)

            def alone(i):
                for j in range(0, CB, 2):
                    col["pair_sums"](dve, i, j)
                    col["pair_inverts"](dve, i, j)
                    col["inverse_norms"](dve, i, j)

            def passes(i, k):
                n = PASSES * i + k // 2
                if k % 2 == 0:
                    alone_wait(dve, pass_step, 2 * n, v["mark"])
                    ve.max(v["best"][:], v["key"][:]).then_inc(pass_step, 1)
                else:
                    dve.wait_ge(pass_step, 2 * n + 1)
                    ve.tensor_copy(v["order"][:, bass.ds(CB * n + 2 * CB, CB)], v["best"][:])
                    ve.match_replace(v["key"][:], v["best"][:], v["key"][:], 0.0).then_inc(pass_step, 1)

            def between(k):
                if k == 0:
                    keys(0)
                if k == PAIRS - 2:
                    records(0)
                    next_block(0)
                    keys(1)

            copy_xT(0)
            def finale():
                residual(TRI, 1, 1)
                normalise(TRI, 1, 0)
                residual(TRI, 2, 0)
                normalise(TRI, 2, 1)
                dve.wait_ge(o_made, LASTU)
                normalise(TRI, 3, 0)

            nb = loops(dve, step, finale, passes, between, block_end, alone)
            over_total(dve, nb, s, b, v, nc, col)
            col["inverse_norms"](dve, nb, 0)


def over_column(pe, nb, s, b, v, nc, col):
    pe.wait_ge(s["acc_made"], CB * nb)
    pe.wait_ge(s["copied"], CB * nb)
    nc.tensor.matmul(b["ps_colT"][1][:].rearrange("p h c -> p (h c)")[:, 0:D + 1], v["carry"][:], b["acc"][1][:],
                     start=True, stop=True).then_inc(s["carried"], 1)
    col["transposes"](pe, nb, 0)
    col["products"](pe, nb, 0)


def over_total(dve, nb, s, b, v, nc, col):
    dve.wait_ge(s["carried"], 1)
    dve.wait_ge(s["inv_made"], CB * nb)
    nc.vector.tensor_tensor(b["acc"][0][:], b["ps_colT"][1][:].rearrange("p h c -> p (h c)")[:, 0:D + 1],
                            b["over_sum"][:], ALU.add).then_inc(s["over_added"], 1)
    dve.wait_ge(s["over_added"], 1)
    col["add_own"](dve, nb, 0, v["f_base"][:, 0:1])
    col["invert"](dve, nb, 0)


def second_layer(nc, stack, v, b):
    sem, sems, out, h_all, self_x = v["sem"], v["sems"], v["out"], v["h_all"], v["self_x"]
    cur, kept, hrow, W = v["cur"], v["kept"], v["hrow"], v["W"]
    ve, se = nc.vector, nc.scalar

    def sb(name, shape, dt=F32):
        return stack.enter_context(nc.sbuf_tensor(name, shape, dt))

    b = dict(b)
    deep = 4
    for name, shape in (("sum", [P, D + 1]), ("mean", [P, D]), ("colT", [P, 2 * H, P])):
        b[name] = b[name] + [sb(f"{name}_{n}", shape) for n in range(2, deep)]
    b["col_junk"] = b["col_junk"] + [sb(f"col_junk_{n}", [P, D], BF16) for n in range(2, deep)]
    b["ps_colT"] = b["ps_colT"] + [stack.enter_context(nc.psum_tensor(f"ps_colT_{n}", [P, 2 * H, P], F32))
                                   for n in range(2, deep)]
    b["ps_col"] = [b["ps_col"][0]] + [stack.enter_context(nc.psum_tensor(f"ps_col_{n}", [P, 2 * D], F32))[:, 0:D]
                                      for n in range(1, deep)]
    HB = CB // 2
    x_own = sb("x_own", [P, CB, D])
    get_idx = [sb(f"get_idx{h}", [P, HB], I32) for h in range(2)]
    put_idx = [sb(f"put_idx{h}", [P, HB], I32) for h in range(2)]
    stats, mv = sb("stats2", [P, 2, 6]), sb("mv2", [P, 2, 2, 2])
    rt3, rstd, shift = sb("rt4", [P, 2, 2]), sb("rstd2", [P, 2, 2]), sb("shift", [P, 2, 2])
    cur_in, y_stats, y_aggr, y_rooted, y_rstd, y_shift, o_made = map(
        sem, ("cols_cur_in", "cols_stats", "cols_aggr", "cols_rooted", "cols_rstd", "cols_shift", "cols_o_made"))
    ready, get_made, put_made = sem("l2_ready"), sem("get_made"), sem("put_made")
    s = dict(v["col_sems"])
    s["gathered"], s["own"], s["stored"] = sems("gathered_h", CB), s["stored"], sems("scattered", CB)
    x_in = s["own_stored"]
    col = column_steps(nc, v, b, s, W["w2l_sb"], W["w2r_sb"], 1, one_bank=False)

    def count(eng):
        return eng.value_load(v["nb_i"][0:1, 3:4], min_val=0, max_val=MAXB - 1)

    def stage(i, pair, by, work):
        if pair >= by:
            work(i, 2 * (pair - by))
        elif not isinstance(i, int):
            work(i - 1, 2 * (pair - by) + CB)

    def blocks(eng, body, last):
        for pair in range(CB // 2):
            body(0, pair)
        with eng.If(last > 0):
            with eng.Fori(0, last) as i:
                for pair in range(CB // 2):
                    body(i + 1, pair)

    with nc.Block() as block:
        @block.sync
        def _(sp):
            last = count(sp)

            def load_own(i, j, columns=2):
                for q in range(CB - 1 - j, CB - 1 - j - columns, -1):
                    rows = P * CB * i + P * (1 + q) if columns == 2 else 0
                    if not isinstance(i, int):
                        sp.wait_ge(s["transposed"], CB * i + CB - q)
                    sp.dma_start(b["own"][:, q, 0:D], h_all[bass.ds(HID0 + rows, P), :]).then_inc(s["own"][q], 16)

            def load_x(i, j, columns=2):
                for q in range(CB - 1 - j, CB - 1 - j - columns, -1):
                    rows = P * CB * i + P * (1 + q) if columns == 2 else 0
                    if not isinstance(i, int):
                        sp.wait_ge(s["drained"], CB * (i - 1) + CB - q + deep)
                    sp.dma_start(x_own[:, q, :], self_x[bass.ds(rows, P), :]).then_inc(x_in[q], 16)

            def body(i, pair):
                load_own(i, 2 * pair)
                if pair >= 2:
                    load_x(i, 2 * pair - 4)
                elif not isinstance(i, int):
                    load_x(i - 1, 2 * pair + 4)

            blocks(sp, body, last)
            load_x(last, 4)
            load_x(last, 6)
            load_own(last + 1, 0, 1)
            load_x(last + 1, 0, 1)

        @block.gpsimd
        def _(pool):
            last = count(pool)

            def gather(table, i, j):
                if not isinstance(i, int):
                    alone_wait(pool, s["acc_made"], CB * i - CB + j + 2, v["mark"])
                for q in (CB - 1 - j, CB - 2 - j):
                    nc.gpsimd.indirect_dma_start(b["gathered"][:, q, 0:D], None, table,
                                                 bass.IndirectOffsetOnAxis(get_idx[j // HB][:, q % HB:q % HB + 1], 0)).then_inc(s["gathered"][q], 16)

            def scatter(i, j):
                alone_wait(pool, o_made, CB * i + j + 2 + 4, v["mark"])
                for q in (CB - 1 - j, CB - 2 - j):
                    nc.gpsimd.indirect_dma_start(out, bass.IndirectOffsetOnAxis(put_idx[j // HB][:, q % HB:q % HB + 1], 0),
                                                 b["col_out"][:, q, :], None,
                                                 bounds_check=N - 1, oob_is_err=False).then_inc(s["stored"][q], 16)

            def take(tile, source, field, i, lo, made, n, used):
                if not isinstance(i, int):
                    for q in range(lo, lo + HB):
                        pool.wait_ge(used[q], 16 * i)
                view = (source[:, bass.ds(i, 1), lo:lo + HB] if field is None
                        else source[:, bass.ds(i, 1), field, lo:lo + HB])
                nc.gpsimd.tensor_copy(tile[:], view.rearrange("p o c -> p (o c)")).then_inc(made, 1)
                alone_wait(pool, made, 2 * i + n, v["mark"])

            def body(table, i, pair):
                j = 2 * pair
                later = not isinstance(i, int)
                if pair == 0:
                    take(get_idx[0], hrow, None, i, HB, get_made, 1, s["gathered"])
                if pair == 2:
                    take(get_idx[1], hrow, None, i, 0, get_made, 2, s["gathered"])
                    if later:
                        take(put_idx[0], kept, 1, i - 1, HB, put_made, 1, s["stored"])
                gather(table, i, j)
                if later and pair < 2:
                    with pool.If(i > 1):
                        scatter(i - 2, HB + j)
                elif later:
                    scatter(i - 1, j - HB)
                if later and pair == 3:
                    take(put_idx[1], kept, 1, i - 1, 0, put_made, 2, s["stored"])

            with pool.If(last < FEWB):
                blocks(pool, lambda i, pair: body(h_all[0:N + P * (1 + CB * FEWB), :], i, pair), last)
            with pool.Else():
                blocks(pool, lambda i, pair: body(h_all, i, pair), last)
            with pool.If(last > 0):
                scatter(last - 1, HB)
                scatter(last - 1, HB + 2)
            take(put_idx[0], kept, 1, last, HB, put_made, 1, s["stored"])
            scatter(last, 0)
            scatter(last, 2)
            take(put_idx[1], kept, 1, last, 0, put_made, 2, s["stored"])
            scatter(last, HB)
            scatter(last, HB + 2)
            q = CB - 1
            alone_wait(pool, o_made, CB * (last + 1) + 1 + 4, v["mark"])
            nc.gpsimd.indirect_dma_start(out, bass.IndirectOffsetOnAxis(v["f_put"][:, 0:1], 0), b["col_out"][:, q, :], None,
                                         bounds_check=N - 1, oob_is_err=False).then_inc(s["stored"][q], 16)
            for q in range(CB):
                pool.wait_ge(s["stored"][q], 16 * (last + 1) + 16 * (q == CB - 1))

        @block.tensor
        def _(pe):
            pe.sem_inc(s["transposed"], CB)
            pe.sem_inc(s["multiplied"], deep)
            last = count(pe)

            def pair_of(name):
                def work(i, j):
                    col[name](pe, i, j)
                    col[name](pe, i, j + 1)
                return work

            def body(i, pair):
                stage(i, pair, 1, pair_of("transposes"))
                stage(i, pair, 2, pair_of("products"))

            blocks(pe, body, last)
            stage(last + 1, 0, 1, pair_of("transposes"))
            stage(last + 1, 0, 2, pair_of("products"))
            stage(last + 1, 1, 2, pair_of("products"))
            over_column(pe, last + 1, s, b, v, nc, col)

        @block.scalar
        def _(act):
            act.sem_inc(s["mean_made"], deep)
            act.sem_inc(o_made, 4)
            last = count(act)

            def pair_of(name):
                def work(i, j):
                    col[name](act, i, j)
                    col[name](act, i, j + 1)
                return work

            def deviation(i, j):
                n, par = CB // 2 * i + j // 2, j // 2 % 2
                act.wait_ge(y_aggr, n + 1)
                se.activation(rt3[:, par, :], mv[:, par, :, 1], ACT.Sqrt, bias=v["ln_eps"][:, 0:1]).then_inc(y_rooted, 1)

            def normalise(i, j, columns=2):
                n, par = CB // 2 * i + j // 2, j // 2 % 2
                act.wait_ge(y_shift, n + 1)
                for n in range(columns):
                    q = CB - 1 - j - n
                    se.activation(b["col_out"][:, q, :], b["col_out"][:, q, :], ACT.Identity,
                                  scale=rstd[:, par, n:n + 1], bias=shift[:, par, n:n + 1]).then_inc(o_made, 1)

            def norms(i, j):
                col["norms"](act, i, j)

            def body(i, pair):
                stage(i, pair, 1, pair_of("mean"))
                stage(i, pair, 2, pair_of("copy_transposed"))
                stage(i, pair, 3, norms)
                stage(i, pair, 4, deviation)
                stage(i, pair, 4, normalise)

            blocks(act, body, last)
            stage(last + 1, 0, 1, pair_of("mean"))
            for pair in range(4):
                if pair < 2:
                    stage(last + 1, pair, 2, pair_of("copy_transposed"))
                if pair < 3:
                    stage(last + 1, pair, 3, norms)
                deviation(last, 2 * pair)
                normalise(last, 2 * pair)
            col["mean"](act, last + 1, 0)
            col["copy_transposed"](act, last + 1, 0)
            col["norms"](act, last + 1, 0, 1)
            deviation(last + 1, 0)
            normalise(last + 1, 0, 1)

        @block.vector
        def _(dve):
            dve.sem_inc(s["drained"], deep)
            ve.memset(b["acc"][1][:], 0.0)
            ve.memset(b["over_sum"][:], 0.0).then_inc(ready, 1)
            dve.wait_ge(ready, 1)
            last = count(dve)

            def output(i, j, columns=2):
                number, par = CB // 2 * i + j // 2, j // 2 % 2
                dve.wait_ge(s["normed"], number + 1)
                for n in range(columns):
                    q = CB - 1 - j - n
                    dve.wait_ge(x_in[q], 16 * i + 16)
                    dve.wait_ge(s["stored"][q], 16 * i)
                    ve.scalar_tensor_tensor(b["col_out"][:, q, :], b["ps_col"][(j + n) % deep], b["col_rn"][:, n:n + 1],
                                            x_own[:, q, :], ALU.mult, ALU.add).then_inc(s["drained"], 1)
                for n in range(columns):
                    dve.wait_ge(s["drained"], 2 * number + n + deep + 1)
                    ve.bn_stats(stats[:, n, :], b["col_out"][:, CB - 1 - j - n, :]).then_inc(y_stats, 1)
                alone_wait(dve, y_stats, 2 * number + columns, v["mark"])
                for n in range(columns):
                    last = ve.bn_aggr(mv[:, par, n, :], stats[:, n, :])
                last.then_inc(y_aggr, 1)

            def factor(i, j):
                n, par = CB // 2 * i + j // 2, j // 2 % 2
                dve.wait_ge(y_rooted, n + 1)
                dve.wait_ge(o_made, 2 * n + 2)
                ve.reciprocal(rstd[:, par, :], rt3[:, par, :]).then_inc(y_rstd, 1)

            def shifts(i, j):
                n, par = CB // 2 * i + j // 2, j // 2 % 2
                dve.wait_ge(y_rstd, n + 1)
                ve.scalar_tensor_tensor(shift[:, par, :], mv[:, par, :, 0], -1.0, rstd[:, par, :],
                                        ALU.mult, ALU.mult).then_inc(y_shift, 1)

            def norms(part):
                return lambda i, j: col["inverse_norms"](dve, i, j, (part,))

            def body(i, pair):
                if pair == 0:
                    ve.tensor_copy(cur[:], kept[:, bass.ds(i, 1), :, :].rearrange("p o k c -> p (o k) c")).then_inc(cur_in, 1)
                    dve.wait_ge(cur_in, i + 1)
                stage(i, pair, 0, lambda i, j: col["pair_sums"](dve, i, j))
                stage(i, pair, 3, norms(0))
                stage(i, pair, 4, factor)
                stage(i, pair, 0, lambda i, j: col["pair_inverts"](dve, i, j))
                stage(i, pair, 3, norms(1))
                stage(i, pair, 4, shifts)
                stage(i, pair, 3, output)

            blocks(dve, body, last)
            for pair in range(4):
                if pair < 3:
                    stage(last + 1, pair, 3, norms(0))
                    stage(last + 1, pair, 3, norms(1))
                factor(last, 2 * pair)
                shifts(last, 2 * pair)
                if pair < 3:
                    stage(last + 1, pair, 3, output)
            over_total(dve, last + 1, s, b, v, nc, col)
            norms(0)(last + 1, 0)
            norms(1)(last + 1, 0)
            output(last + 1, 0, 1)
            factor(last + 1, 0)
            shifts(last + 1, 0)


def kernel(x, src, dst, L0_gnn_W1l, L0_gnn_b1l, L0_gnn_W1r, L0_gnn_W2l, L0_gnn_b2l, L0_gnn_W2r):
    import concourse.bacc as bacc
    from concourse.bass_utils import run_bass_kernel_spmd

    arrays = {
        "x": x, "src": src, "dst": dst,
        "w1l": np.asarray(L0_gnn_W1l).T, "b1": L0_gnn_b1l, "w1r": np.asarray(L0_gnn_W1r).T,
        "w2l": np.asarray(L0_gnn_W2l).T, "b2": L0_gnn_b2l, "w2r": np.asarray(L0_gnn_W2r).T,
    }
    arrays = {name: np.ascontiguousarray(a) for name, a in arrays.items()}
    nc = bacc.Bacc("TRN2", target_bir_lowering=False, num_devices=1)
    args = [nc.dram_tensor(name, a.shape, mybir.dt.from_np(a.dtype), kind="ExternalInput").ap()
            for name, a in arrays.items()]
    out = nc.dram_tensor("out", [N, D], F32, kind="ExternalOutput").ap()
    build_gnn(nc, *args, out)
    result = run_bass_kernel_spmd(nc, [arrays], core_ids=[0])
    return result.results[0]["out"]
```
